# Optimizing a Trainium2 kernel written in Bass

```python
import numpy as np
import jax
import jax.numpy as jnp

def _softmax(x, axis=-1):
    return jax.nn.softmax(x, axis=axis)

def _gelu(x):
    return jax.nn.gelu(x, approximate=True)

def _silu(x):
    return jax.nn.silu(x)

def _sigmoid(x):
    return jax.nn.sigmoid(x)

def _layernorm(x, axis=-1, eps=1e-05):
    m = jnp.mean(x, axis=axis, keepdims=True)
    v = jnp.var(x, axis=axis, keepdims=True)
    return (x - m) / jnp.sqrt(v + eps)

def _scatter_add(tgt, idx, src, axis=0):
    return tgt.at[idx].add(src)

def _segment_sum(src, seg, n):
    return jax.ops.segment_sum(src, seg, n)
kernel_name = 'mk_xattn_ffn_d2_seqx_r8_ff52cc'

def setup_inputs(seed: int=0):
    np.random.seed(seed)
    _w = jnp.asarray

    def _rec_inputs():
        import jax
        import jax.numpy as jnp
        _rk = jax.random.key(seed)
        x = 7.22e-05 + 1 * jax.random.normal(jax.random.fold_in(_rk, 1), (8, 128, 512), jnp.float32)
        _lenS = 128 - jax.random.randint(jax.random.fold_in(_rk, 7), (8,), 0, max(1, 128 // 4) + 1, jnp.int32)
        _lenS2 = 128 - jax.random.randint(jax.random.fold_in(_rk, 8), (8,), 0, max(1, 128 // 4) + 1, jnp.int32)
        _ctx_4096P = jax.random.normal(jax.random.fold_in(_rk, 11), (8, 16, 512), jnp.float32)
        _ctx_4096c = jax.random.dirichlet(jax.random.fold_in(_rk, 511), 0.3 * jnp.ones((16,), jnp.float32), (8, 128))
        _ctx_4096t = jnp.einsum('bsk,bkd->bsd', _ctx_4096c, _ctx_4096P)
        _ctx_4096t = _ctx_4096t * jax.lax.rsqrt(jnp.mean(jnp.square(_ctx_4096t)) + 1e-12) * 0.953939
        ctx_4096 = 4.13588e-05 + 0.999923 * (_ctx_4096t + 0.3 * jax.random.normal(jax.random.fold_in(_rk, 611), (8, 128, 512), jnp.float32))
        _validS = jnp.arange(128)[None, :] < _lenS[:, None]
        _validS2 = jnp.arange(128)[None, :] < _lenS2[:, None]
        _causal = jnp.tril(jnp.ones((128, 128), dtype=bool))
        mask_1x1xSxS2_bk0 = jnp.logical_not(jnp.broadcast_to(_validS2[0:1, None, None, :], (1, 1, 128, 128)))
        mask_Bx1x4096_ff1 = jnp.where(jnp.ones((8, 1, 512), dtype=bool), 1.0, 0.0).astype(jnp.float32)
        return (x, ctx_4096, mask_1x1xSxS2_bk0, mask_Bx1x4096_ff1)
    x, ctx_4096, mask_1x1xSxS2_bk0, mask_Bx1x4096_ff1 = _rec_inputs()

    def _L0_xattn_setup():
        import jax, jax.numpy as jnp
        import numpy as np
        B, T, D_MODEL = (1, 256, 512)
        NUM_Q_HEADS, NUM_KV_HEADS, KEY_SIZE = (32, 8, 128)
        ATTN_MULT = 0.08838834764831845
        MAX_ATTN_VAL = 30.0

        def rotate_half(x):
            x1, x2 = jnp.split(x, 2, axis=-1)
            return jnp.concatenate((-x2, x1), axis=-1)

        def apply_rope(x):
            b, t, h, d = x.shape
            exponents = jnp.arange(0, d, 2, dtype=jnp.float32)
            inv_freq = 1.0 / 10000.0 ** (exponents / d)
            pos = jnp.arange(t, dtype=jnp.float32)
            phase = pos[:, None] * inv_freq[None, :]
            phase = jnp.tile(phase, (1, 2))[None, :, None, :]
            return (x * jnp.cos(phase) + rotate_half(x) * jnp.sin(phase)).astype(x.dtype)
        key = jax.random.key(seed)
        ks = jax.random.split(key, 8)
        query = jax.random.normal(ks[0], (B, T, D_MODEL), dtype=jnp.float32)
        kk = jax.random.normal(ks[1], (B, T, D_MODEL), dtype=jnp.float32)
        vv = jax.random.normal(ks[2], (B, T, D_MODEL), dtype=jnp.float32)
        mask = jnp.tril(jnp.ones((T, T), dtype=bool))[None, None, :, :]
        s = 0.02
        Wq = jax.random.normal(ks[3], (D_MODEL, NUM_Q_HEADS * KEY_SIZE), dtype=jnp.float32) * s
        Wk = jax.random.normal(ks[4], (D_MODEL, NUM_KV_HEADS * KEY_SIZE), dtype=jnp.float32) * s
        Wv = jax.random.normal(ks[5], (D_MODEL, NUM_KV_HEADS * KEY_SIZE), dtype=jnp.float32) * s
        Wo = jax.random.normal(ks[6], (NUM_Q_HEADS * KEY_SIZE, D_MODEL), dtype=jnp.float32) * s
        return {'query': query, 'key': kk, 'value': vv, 'mask': mask, 'Wq': Wq, 'Wk': Wk, 'Wv': Wv, 'Wo': Wo}
    _L0_xattn_all = _L0_xattn_setup()
    _L0_xattn_in = {k: v for k, v in _L0_xattn_all.items() if k in ('Wq', 'Wk', 'Wv', 'Wo')}
    del _L0_xattn_all

    def _L0_ffn_setup():
        import jax, jax.numpy as jnp
        import numpy as np
        H, FF = (512, 1792)
        B, S = (4, 256)
        key = jax.random.key(seed)
        ks = jax.random.split(key, 7)
        x = jax.random.normal(ks[0], (B, S, H), dtype=jnp.float32)
        gate_t = jax.random.randint(ks[1], (FF, H), -1, 2, dtype=jnp.int32)
        up_t = jax.random.randint(ks[2], (FF, H), -1, 2, dtype=jnp.int32)
        down_t = jax.random.randint(ks[3], (H, FF), -1, 2, dtype=jnp.int32)
        gate_s = jax.random.uniform(ks[4], (FF,), jnp.float32, 0.01, 0.1)
        up_s = jax.random.uniform(ks[5], (FF,), jnp.float32, 0.01, 0.1)
        down_s = jax.random.uniform(ks[6], (H,), jnp.float32, 0.01, 0.1)
        return {'x': x, 'gate_t': gate_t, 'up_t': up_t, 'down_t': down_t, 'gate_s': gate_s, 'up_s': up_s, 'down_s': down_s}
    _L0_ffn_all = _L0_ffn_setup()
    _L0_ffn_in = {k: v for k, v in _L0_ffn_all.items() if k in ('gate_t', 'up_t', 'down_t', 'gate_s', 'up_s', 'down_s')}
    del _L0_ffn_all

    def _L1_xattn_setup():
        import jax, jax.numpy as jnp
        import numpy as np
        W = 128
        H = 8
        D = 128
        DK = D // 2

        def _to_patches(x):
            b, d, s = x.shape
            np_ = s // W
            return x.reshape(b, d, np_, W).transpose(0, 2, 1, 3).reshape(b * np_, d, W)
        key = jax.random.key(seed)
        ks = jax.random.split(key, 10)
        B, S = (8, 512)
        qk = jax.random.normal(ks[0], (B, D, S), dtype=jnp.float32)
        v = jax.random.normal(ks[1], (B, D, S), dtype=jnp.float32)
        masks = jnp.ones((B, 1, S), dtype=jnp.float32)
        sc = 1.0 / np.sqrt(D)
        Wq = jax.random.normal(ks[2], (DK, D), dtype=jnp.float32) * sc
        bq = jnp.zeros((DK,), dtype=jnp.float32)
        Wk = jax.random.normal(ks[3], (DK, D), dtype=jnp.float32) * sc
        bk = jnp.zeros((DK,), dtype=jnp.float32)
        Wv = jax.random.normal(ks[4], (DK, D), dtype=jnp.float32) * sc
        bv = jnp.zeros((DK,), dtype=jnp.float32)
        Wo = jax.random.normal(ks[5], (D, DK), dtype=jnp.float32) * (1.0 / np.sqrt(DK))
        bo = jnp.zeros((D,), dtype=jnp.float32)
        return dict(qk=qk, v=v, masks=masks, Wq=Wq, bq=bq, Wk=Wk, bk=bk, Wv=Wv, bv=bv, Wo=Wo, bo=bo)
    _L1_xattn_all = _L1_xattn_setup()
    _L1_xattn_in = {k: v for k, v in _L1_xattn_all.items() if k in ('Wq', 'bq', 'Wk', 'bk', 'Wv', 'bv', 'Wo', 'bo')}
    del _L1_xattn_all

    def _L1_ffn_setup():
        import jax, jax.numpy as jnp
        import numpy as np
        key = jax.random.key(seed)
        k = jax.random.split(key, 6)
        x = jax.random.normal(k[0], (4, 256, 512), jnp.float32)
        W = jax.random.normal(k[1], (512, 512), jnp.float32) * 0.02
        bias = jax.random.normal(k[2], (512,), jnp.float32) * 0.02
        A = jax.random.normal(k[3], (16, 16, 512), jnp.float32) * 0.02
        Bf = jax.random.normal(k[4], (16, 512, 16), jnp.float32) * 0.02
        coeffs = jax.random.uniform(k[5], (16,), jnp.float32)
        scales = jnp.full((16,), 0.5, jnp.float32)
        return {'x': x, 'W': W, 'bias': bias, 'A': A, 'Bf': Bf, 'coeffs': coeffs, 'scales': scales}
    _L1_ffn_all = _L1_ffn_setup()
    _L1_ffn_in = {k: v for k, v in _L1_ffn_all.items() if k in ('W', 'bias', 'A', 'Bf', 'coeffs', 'scales')}
    del _L1_ffn_all
    return {'x': x, 'ctx_4096': ctx_4096, 'mask_1x1xSxS2_bk0': mask_1x1xSxS2_bk0, 'mask_Bx1x4096_ff1': mask_Bx1x4096_ff1, 'L0_xattn_Wq': _L0_xattn_in['Wq'], 'L0_xattn_Wk': _L0_xattn_in['Wk'], 'L0_xattn_Wv': _L0_xattn_in['Wv'], 'L0_xattn_Wo': _L0_xattn_in['Wo'], 'L0_ffn_gate_t': _L0_ffn_in['gate_t'], 'L0_ffn_up_t': _L0_ffn_in['up_t'], 'L0_ffn_down_t': _L0_ffn_in['down_t'], 'L0_ffn_gate_s': _L0_ffn_in['gate_s'], 'L0_ffn_up_s': _L0_ffn_in['up_s'], 'L0_ffn_down_s': _L0_ffn_in['down_s'], 'L1_xattn_Wq': _L1_xattn_in['Wq'], 'L1_xattn_bq': _L1_xattn_in['bq'], 'L1_xattn_Wk': _L1_xattn_in['Wk'], 'L1_xattn_bk': _L1_xattn_in['bk'], 'L1_xattn_Wv': _L1_xattn_in['Wv'], 'L1_xattn_bv': _L1_xattn_in['bv'], 'L1_xattn_Wo': _L1_xattn_in['Wo'], 'L1_xattn_bo': _L1_xattn_in['bo'], 'L1_ffn_W': _L1_ffn_in['W'], 'L1_ffn_bias': _L1_ffn_in['bias'], 'L1_ffn_A': _L1_ffn_in['A'], 'L1_ffn_Bf': _L1_ffn_in['Bf'], 'L1_ffn_coeffs': _L1_ffn_in['coeffs'], 'L1_ffn_scales': _L1_ffn_in['scales']}

def reference(x, ctx_4096, mask_1x1xSxS2_bk0, mask_Bx1x4096_ff1, L0_xattn_Wq, L0_xattn_Wk, L0_xattn_Wv, L0_xattn_Wo, L0_ffn_gate_t, L0_ffn_up_t, L0_ffn_down_t, L0_ffn_gate_s, L0_ffn_up_s, L0_ffn_down_s, L1_xattn_Wq, L1_xattn_bq, L1_xattn_Wk, L1_xattn_bk, L1_xattn_Wv, L1_xattn_bv, L1_xattn_Wo, L1_xattn_bo, L1_ffn_W, L1_ffn_bias, L1_ffn_A, L1_ffn_Bf, L1_ffn_coeffs, L1_ffn_scales):
    import jax
    import jax.numpy as jnp

    def _L0_xattn_ref(query, key, value, mask, Wq, Wk, Wv, Wo):
        import jax, jax.numpy as jnp
        import numpy as np
        B, T, D_MODEL = (1, 256, 512)
        NUM_Q_HEADS, NUM_KV_HEADS, KEY_SIZE = (32, 8, 128)
        ATTN_MULT = 0.08838834764831845
        MAX_ATTN_VAL = 30.0

        def rotate_half(x):
            x1, x2 = jnp.split(x, 2, axis=-1)
            return jnp.concatenate((-x2, x1), axis=-1)

        def apply_rope(x):
            b, t, h, d = x.shape
            exponents = jnp.arange(0, d, 2, dtype=jnp.float32)
            inv_freq = 1.0 / 10000.0 ** (exponents / d)
            pos = jnp.arange(t, dtype=jnp.float32)
            phase = pos[:, None] * inv_freq[None, :]
            phase = jnp.tile(phase, (1, 2))[None, :, None, :]
            return (x * jnp.cos(phase) + rotate_half(x) * jnp.sin(phase)).astype(x.dtype)
        b, t, _ = query.shape
        d = KEY_SIZE
        h, kv_h = (NUM_Q_HEADS, NUM_KV_HEADS)
        g = h // kv_h
        q = (query @ Wq).reshape(b, t, h, d)
        k = (key @ Wk).reshape(b, t, kv_h, d)
        v = (value @ Wv).reshape(b, t, kv_h, d)
        q = apply_rope(q)
        k = apply_rope(k)
        q = q.reshape(b, t, kv_h, g, d)
        logits = jnp.einsum('btkgd,bTkd->bkgtT', q, k).astype(jnp.float32)
        logits = logits * ATTN_MULT
        logits = MAX_ATTN_VAL * jnp.tanh(logits / MAX_ATTN_VAL)
        m = mask[:, :, None, :, :]
        logits = jnp.where(m, logits, -1e+30)
        weights = jax.nn.softmax(logits, axis=-1).astype(query.dtype)
        attn = jnp.einsum('bkgtT,bTkd->btkgd', weights, v)
        attn = attn.reshape(b, t, h * d)
        return attn @ Wo

    def _L0_ffn_ref(x, gate_t, up_t, down_t, gate_s, up_s, down_s):
        import jax, jax.numpy as jnp
        import numpy as np
        H, FF = (512, 1792)
        B, S = (4, 256)
        Bb, Ss, Hh = x.shape
        x_flat = x.reshape(Bb * Ss, Hh)
        gate_w = gate_t.astype(jnp.float32) * gate_s[:, None]
        up_w = up_t.astype(jnp.float32) * up_s[:, None]
        down_w = down_t.astype(jnp.float32) * down_s[:, None]
        gate_out = x_flat @ gate_w.T
        up_out = x_flat @ up_w.T
        hidden = jax.nn.silu(gate_out) * up_out
        out_flat = hidden @ down_w.T
        return out_flat.reshape(Bb, Ss, -1)

    def _L1_xattn_ref(qk, v, masks, Wq, bq, Wk, bk, Wv, bv, Wo, bo):
        import jax, jax.numpy as jnp
        import numpy as np
        W = 128
        H = 8
        D = 128
        DK = D // 2

        def _to_patches(x):
            b, d, s = x.shape
            np_ = s // W
            return x.reshape(b, d, np_, W).transpose(0, 2, 1, 3).reshape(b * np_, d, W)
        B, _, S = qk.shape
        np_ = S // W
        qp = _to_patches(qk)
        vp = _to_patches(v)
        mp = _to_patches(masks)
        q = jnp.einsum('ed,bdw->bew', Wq, qp) + bq[:, None]
        k = jnp.einsum('ed,bdw->bew', Wk, qp) + bk[:, None]
        val = jnp.einsum('ed,bdw->bew', Wv, vp) + bv[:, None]
        BN = q.shape[0]
        dh = DK // H
        qh = q.reshape(BN, H, dh, W)
        kh = k.reshape(BN, H, dh, W)
        vh = val.reshape(BN, H, dh, W)
        scores = jnp.einsum('bhdi,bhdj->bhij', qh, kh) / jnp.sqrt(jnp.asarray(dh, qh.dtype))
        scores = jnp.where(mp[:, :, None, :] > 0, scores, jnp.asarray(-1000000000.0, scores.dtype))
        attn = jax.nn.softmax(scores, axis=-1)
        o = jnp.einsum('bhij,bhdj->bhdi', attn, vh).reshape(BN, DK, W)
        o = jax.nn.gelu(o, approximate=False)
        out = jnp.einsum('de,bew->bdw', Wo, o) + bo[:, None]
        out = out.reshape(B, np_, D, W).transpose(0, 2, 1, 3).reshape(B, D, S)
        out = out * masks
        return out

    def _L1_ffn_ref(x, W, bias, A, Bf, coeffs, scales):
        import jax, jax.numpy as jnp
        import numpy as np
        out = jnp.einsum('bsd,od->bso', x, W) + bias
        xa = jnp.einsum('bsd,erd->ebsr', x, A)
        w = coeffs * scales
        upd = jnp.einsum('ebsr,eor,e->bso', xa, Bf, w)
        return out + upd
    x = x + _L0_xattn_ref(_layernorm(x, axis=-1), ctx_4096, ctx_4096, mask_1x1xSxS2_bk0, L0_xattn_Wq, L0_xattn_Wk, L0_xattn_Wv, L0_xattn_Wo)
    x = x + _L0_ffn_ref(_layernorm(x, axis=-1), L0_ffn_gate_t, L0_ffn_up_t, L0_ffn_down_t, L0_ffn_gate_s, L0_ffn_up_s, L0_ffn_down_s)
    x = x + _L1_xattn_ref(_layernorm(x, axis=-1), ctx_4096, mask_Bx1x4096_ff1, L1_xattn_Wq, L1_xattn_bq, L1_xattn_Wk, L1_xattn_bk, L1_xattn_Wv, L1_xattn_bv, L1_xattn_Wo, L1_xattn_bo)
    x = x + _L1_ffn_ref(_layernorm(x, axis=-1), L1_ffn_W, L1_ffn_bias, L1_ffn_A, L1_ffn_Bf, L1_ffn_coeffs, L1_ffn_scales)
    return x

_drawn_inputs = setup_inputs


def setup_inputs(seed=0):
    import zlib

    import numpy as np

    out = dict(_drawn_inputs(seed))
    spreads = {'L1_xattn_bq': (0.0, 0.8),
     'L1_xattn_bk': (0.0, 0.8),
     'L1_xattn_bv': (0.0, 0.306),
     'L1_xattn_bo': (0.0, 0.1),
     'L1_ffn_scales': (0.5, 0.6)}
    factors = {'L1_ffn_bias': 5.84, 'L1_ffn_coeffs': 5.978}
    for name, (base, spread) in spreads.items():
        noise = np.random.default_rng([zlib.crc32(name.encode()), seed]).standard_normal(out[name].shape)
        drawn = base * np.exp(spread * noise) if base else spread * noise
        out[name] = jnp.asarray(drawn.astype(out[name].dtype))
    for name, factor in factors.items():
        out[name] = (out[name] * factor).astype(out[name].dtype)
    return out
```

```python
from contextlib import ExitStack

import concourse.bass as bass
from concourse import mybir

F32 = mybir.dt.float32
F32R = mybir.dt.float32r
F16 = mybir.dt.float16
I32 = mybir.dt.int32
U8 = mybir.dt.uint8
ALU = mybir.AluOpType
ACT = mybir.ActivationFunctionType
AX = mybir.AxisListType

P = 128
B, S, D = 8, 128, 512
KT = D // P
NH, NKV = 32, 8
G = NH // NKV
DH = 128
HB = 4
HR = HB * S
TANH_SCALE = 0.08838834764831845 / 30.0
CAP = 30.0
EPS = 1e-5
BIG = 1e30


def raw(ap):
    return ap.bitcast(F32)


def stage_semaphores(nc, ctx, prefix):
    made = []

    def clear():
        nc.clear_and_free_semaphores(made)
        nc.all_engine_barrier(sem_only=True)

    ctx.callback(clear)

    def sem(name):
        made.append(nc.alloc_semaphore(prefix + name))
        return made[-1]

    return sem


def split_passes(hi_w, lo_w, hi_x, lo_x):
    return ((hi_w, lo_x), (lo_w, hi_x), (hi_w, hi_x))


def row_statistics(nc, mem, sems, ready):
    stat, aggr, eps_added, rstd_done = sems

    def vector(dve):
        for b in range(B):
            ready(dve, b)
            nc.vector.bn_stats(mem["stats"][:, b, :], mem["x_acc"][:, b, :]).then_inc(stat, 1)
        for b in range(B):
            dve.wait_ge(stat, b + 1)
            nc.vector.bn_aggr(mem["mv"][:, b, :], mem["stats"][:, b, :]).then_inc(aggr, 1)

    def pool(eng):
        eng.wait_ge(aggr, B)
        nc.gpsimd.tensor_scalar(mem["rstd"][:], mem["mv"][:, :, 1], EPS, None, ALU.add).then_inc(eps_added, 1)
        eng.wait_ge(eps_added, 1)
        nc.gpsimd.tensor_tensor(mem["rstd"][:], mem["rstd"][:], mem["minus_half"][:], ALU.pow).then_inc(rstd_done, 1)

    return vector, pool


def prepare(nc, io, mem):
    with ExitStack() as ctx:
        sb = lambda name, shape, dt: ctx.enter_context(nc.sbuf_tensor(name, shape, dt))
        sem = stage_semaphores(nc, ctx, "prep_")
        mask_keys = sb("mask_keys", [P, S], U8)
        allowed = sb("allowed", [P, S], F32)
        ones = sb("ones", [P, P], F32)
        keep = sb("keep", [P, S], F32)
        empty = sb("empty", [P, S], F32)
        count_ps = ctx.enter_context(nc.psum_tensor("count_ps", [P, S], F32))
        x_in, tab_in, mask_in = sem("x_in"), sem("tab_in"), sem("mask_in")
        consts, step, counted = sem("consts"), sem("step"), sem("counted")
        ln_sems = [sem(n) for n in ("stat", "aggr", "eps_added", "rstd_done")]
        ln_vector, ln_pool = row_statistics(nc, mem, ln_sems, lambda dve, b: dve.wait_ge(x_in, 16))
        block = ctx.enter_context(nc.Block())

        @block.sync
        def _(sp):
            sp.dma_start(mask_keys[:], io["mask_t"]).then_inc(mask_in, 16)
            sp.dma_start(mem["cos_k"][:], io["cos"]).then_inc(tab_in, 16)
            sp.dma_start(mem["sin_k"][:], io["sin"]).then_inc(tab_in, 16)
            sp.dma_start(mem["x_acc"][:], io["x"].rearrange("b s d -> s b d")).then_inc(x_in, 16)

        @block.gpsimd
        def _(pool):
            nc.gpsimd.memset(mem["ident"][:], 0.0).then_inc(consts, 1)
            nc.gpsimd.memset(ones[:], 1.0).then_inc(consts, 1)
            nc.gpsimd.memset(mem["minus_half"][:], -0.5).then_inc(consts, 1)
            nc.gpsimd.memset(raw(mem["pick"][:]), 0.0).then_inc(consts, 1)
            pool.wait_ge(consts, 4)
            nc.gpsimd.affine_select(out=mem["ident"][:], in_=mem["ident"][:], compare_op=ALU.not_equal,
                                    fill=1.0, base=0, pattern=[[-1, P]], channel_multiplier=1).then_inc(consts, 1)
            for b in range(HB):
                nc.gpsimd.memset(raw(mem["pick"][:, b, b:b + 1]), 1.0).then_inc(consts, 1)
            pool.wait_ge(consts, 5 + HB)
            ln_pool(pool)

        @block.tensor
        def _(pe):
            pe.wait_ge(consts, 2)
            pe.wait_ge(step, 1)
            nc.tensor.matmul(count_ps[:], ones[:], allowed[:], start=True, stop=True).then_inc(counted, 1)

        @block.vector
        def _(dve):
            dve.wait_ge(mask_in, 16)
            nc.vector.tensor_scalar(allowed[:], mask_keys[:], 0, None, ALU.not_equal).then_inc(step, 1)
            dve.wait_ge(counted, 1)
            nc.vector.tensor_scalar(keep[:], count_ps[:], 0.0, None, ALU.is_gt).then_inc(step, 1)
            nc.vector.tensor_scalar(empty[:], count_ps[:], 0.0, None, ALU.is_equal).then_inc(step, 1)
            dve.wait_ge(step, 3)
            nc.vector.tensor_tensor(allowed[:], allowed[:], empty[:], ALU.add).then_inc(step, 1)
            dve.wait_ge(step, 4)
            nc.vector.tensor_scalar(mem["mask_bias"][:], allowed[:], 1.0, BIG, ALU.subtract, ALU.mult).then_inc(step, 1)
            dve.wait_ge(tab_in, 32)
            nc.vector.tensor_tensor(mem["cos_q"][:], mem["cos_k"][:], keep[:], ALU.mult).then_inc(step, 1)
            nc.vector.tensor_tensor(mem["sin_q"][:], mem["sin_k"][:], keep[:], ALU.mult).then_inc(step, 1)
            ln_vector(dve)


def layer0_attention(nc, io, mem):
    RING = 4
    CTX, WV0, WV1, WQ0, LOOP = 0, 4, 8, 12, 16
    PIECES = LOOP + 8 * NKV - 4
    with ExitStack() as ctx:
        sb = lambda name, shape, dt: ctx.enter_context(nc.sbuf_tensor(name, shape, dt))
        ps = lambda name, shape=[P, 512]: ctx.enter_context(nc.psum_tensor(name, shape, F32))
        sem = stage_semaphores(nc, ctx, "l0_")
        ring = sb("ring", [P, RING, 512], F32)
        raw_k = sb("raw_k", [P, KT, DH], F32)
        ctxT = [sb(f"ctxT_{n}", [P, KT, HR], F32R) for n in ("hi", "lo")]
        xnT = [sb(f"xnT_{n}", [P, KT, HR], F32R) for n in ("hi", "lo")]
        v_all = sb("v_all", [P, HB, NKV * DH], F32)
        wa = [sb(f"wa_{n}", [P, KT, 512], F32R) for n in ("hi", "lo")]
        wo = [sb(f"wo_{n}", [P, G, D], F32R) for n in ("hi", "lo")]
        wk = [sb(f"wk_{n}", [P, KT, DH], F32R) for n in ("hi", "lo")]
        kT = [sb(f"kT_{n}", [P, HR], F32R) for n in ("hi", "lo")]
        qT = [sb(f"qT_{n}", [P, G, HR], F32R) for n in ("hi", "lo")]
        vg = [sb(f"vg_{n}", [P, HB, DH], F32R) for n in ("hi", "lo")]
        oT = [sb(f"oT_{n}", [P, HB, G * S], F32R) for n in ("hi", "lo")]
        o_raw = sb("o_raw", [P, HB, G * S], F32)
        rinv = sb("rinv", [P, HB, G * S], F32)
        rinv_rows = sb("rinv_rows", [HB, G * S], F32)
        prob = sb("prob", [P, 2, G * S], F32)
        pT = [sb(f"pT_{n}", [P, 2, G * S], F32R) for n in ("hi", "lo")]
        rope_a = sb("rope_a", [P, 2, HR], F32)
        rope_b = sb("rope_b", [P, 2, HR], F32)
        rinv_dram = nc.dram_tensor("rinv_dram", (HB, G * S), F32).ap()
        xn = o_raw

        proj_ps = [ps("proj0_ps"), ps("proj1_ps")]
        s_ps = [ps("s0_ps"), ps("s1_ps")]
        o_ps = ps("o_ps")
        sum_ps = ps("sum_ps")
        y_ps = [ps("y0_ps"), ps("y1_ps")]
        k_ps = y_ps[1]

        ring_in = [sem(f"ring_in{i}") for i in range(RING)]
        (raw_k_in, piece_hi, piece_lo, xn_done, xn_tr, xn_hi, xn_lo,
         v_mm, v_out, k_mm, k_mul, k_full, k_hi, k_lo, wk_hi, wk_lo, vg_hi, vg_lo,
         q_mm, q_mul, q_full, q_hi, q_lo, s_mm, s_tanh, s_masked, p_exp, p_hi, p_lo,
         o_mm, sum_mm, o_out, rows_done, rows_out, rinv_in, o_norm, o_hi, o_lo, y_mm, y_add) = [
            sem(n) for n in (
                "raw_k_in piece_hi piece_lo xn_done xn_tr xn_hi xn_lo "
                "v_mm v_out k_mm k_mul k_full k_hi k_lo wk_hi wk_lo vg_hi vg_lo "
                "q_mm q_mul q_full q_hi q_lo s_mm s_tanh s_masked p_exp p_hi p_lo "
                "o_mm sum_mm o_out rows_done rows_out rinv_in o_norm o_hi o_lo y_mm y_add").split()]

        half = ctx.enter_context(nc.Fori(0, B // HB))

        def once(n, per):
            return half * per + n

        def head(g, per, n):
            return half * (NKV * per) + g * per + n

        def wq_pieces(g, j):
            return once(WQ0 + j + 1, PIECES) if isinstance(g, int) and g == 0 else half * PIECES + g * 8 + (LOOP - 8 + j + 1)

        def wo_pieces(g, j):
            last = isinstance(g, int) and g == NKV - 1
            return half * PIECES + g * 8 + ((LOOP if last else LOOP + 4) + j + 1)

        block = ctx.enter_context(nc.Block())

        def heads(eng, body):
            body(0, True, False)
            with eng.Fori(1, NKV - 1) as g:
                body(g, False, False)
            body(NKV - 1, False, True)

        wq_d = io["Wq0"].rearrange("(k p) n -> p k n", p=P)
        wk_d = io["Wk0"].rearrange("(k p) n -> p k n", p=P)
        wv_d = io["Wv0"].rearrange("(k p) n -> p k n", p=P)
        wo_d = io["Wo0"].rearrange("(k p) n -> p k n", p=P)
        ctx_d = io["ctx_t"].rearrange("(k p) n -> p k n", p=P)

        @block.sync
        def _(sp):
            def piece(src, slot, uses_before, free):
                if free is not None:
                    sp.wait_ge(piece_hi, free)
                    sp.wait_ge(piece_lo, free)
                sp.dma_start(ring[:, slot:slot + 1, :], src).then_inc(ring_in[slot], 16)

            for j in range(4):
                piece(ctx_d[:, j:j + 1, bass.ds(half * HR, HR)], j, 0, None)
            for c in range(2):
                for j in range(4):
                    piece(wv_d[:, j:j + 1, c * 512:(c + 1) * 512], j, 1 + c, once(4 * c + j + 1, PIECES))
            sp.dma_start(raw_k[:], wk_d[:, :, 0:DH]).then_inc(raw_k_in, 16)
            for j in range(4):
                piece(wq_d[:, j:j + 1, 0:512], j, 3, once(WV1 + j + 1, PIECES))

            def rinv_of(g):
                sp.wait_ge(rows_done, head(g, 1, 1))
                sp.dma_start(rinv_dram, rinv_rows[:]).then_inc(rows_out, 16)
                sp.wait_ge(rows_out, head(g, 16, 16))
                sp.dma_start(rinv[:].rearrange("p b n -> p (b n)"),
                             rinv_dram.rearrange("b n -> (b n)").rearrange("(o n) -> o n", o=1)
                             .to_broadcast([P, HB * G * S])).then_inc(rinv_in, 16)

            def body(g, first, last):
                if not first:
                    rinv_of(g - 1)
                if not last:
                    sp.wait_ge(wk_hi, head(g, 1, 1))
                    sp.wait_ge(wk_lo, head(g, 1, 1))
                    sp.dma_start(raw_k[:], wk_d[:, :, bass.ds(g * DH + DH, DH)]).then_inc(raw_k_in, 16)
                    for j in range(4):
                        free = once(WQ0 + j + 1, PIECES) if first else wo_pieces(g - 1, j)
                        piece(wq_d[:, j:j + 1, bass.ds(g * 512 + 512, 512)], j, None, free)
                for j in range(4):
                    free = wo_pieces(g - 1, j) if last else wq_pieces(g + 1, j)
                    piece(wo_d[:, bass.ds(g * G + j, 1), :], j, None, free)

            heads(sp, body)
            rinv_of(NKV - 1)

        def slot_uses(nth):
            return half * (16 * PIECES // RING) + nth * 16

        def landed_wq(g):
            return slot_uses(4) if isinstance(g, int) and g == 0 else half * (16 * PIECES // RING) + g * 32 + 48

        def landed_wo(g, last):
            return half * (16 * PIECES // RING) + g * 32 + (80 if last else 96)

        @block.gpsimd
        def _(pool):
            def lo_of(dst, j, landed, hi_count, free=()):
                for s, v in free:
                    pool.wait_ge(s, v)
                pool.wait_ge(ring_in[j], landed)
                pool.wait_ge(piece_hi, hi_count)
                nc.gpsimd.tensor_tensor(dst[1][:, j, :], ring[:, j, :], raw(dst[0][:, j, :]), ALU.subtract).then_inc(piece_lo, 1)

            for j in range(4):
                lo_of(ctxT, j, slot_uses(1), once(CTX + j + 1, PIECES))
            for c in range(2):
                for j in range(4):
                    lo_of(wa, j, slot_uses(2 + c), once(WV0 + 4 * c + j + 1, PIECES))
            for j in range(4):
                lo_of(wa, j, slot_uses(4), once(WQ0 + j + 1, PIECES))

            def body(g, first, last):
                for h in range(G):
                    pool.wait_ge(q_mul, head(g, G, h + 1))
                    nc.gpsimd.tensor_tensor(rope_a[:, h % 2, :], rope_a[:, h % 2, :], rope_b[:, h % 2, :], ALU.add).then_inc(q_full, 1)
                if not last:
                    for j in range(4):
                        lo_of(wa, j, landed_wq(g + 1), wq_pieces(g + 1, j))
                for b in range(HB):
                    pool.wait_ge(s_tanh, head(g, HB, b + 1))
                    nc.gpsimd.tensor_tensor(prob[:, b % 2, :].rearrange("p (h t) -> p h t", h=G),
                                            prob[:, b % 2, :].rearrange("p (h t) -> p h t", h=G),
                                            mem["mask_bias"][:].unsqueeze(1).to_broadcast([P, G, S]), ALU.add).then_inc(s_masked, 1)
                    lo_of(wo, b, landed_wo(g, last), wo_pieces(g, b))
            heads(pool, body)

        @block.scalar
        def _(act):
            def hi_of(dst, j, landed, free=()):
                for s, v in free:
                    act.wait_ge(s, v)
                act.wait_ge(ring_in[j], landed)
                nc.scalar.activation(dst[0][:, j, :], ring[:, j, :], ACT.Copy).then_inc(piece_hi, 1)

            for j in range(4):
                hi_of(ctxT, j, slot_uses(1))
            for b in range(HB):
                act.wait_ge(xn_tr, once(b + 1, HB))
                nc.scalar.activation(xnT[0][:, :, b * S:(b + 1) * S], s_ps[b % 2][:].rearrange("p (k s) -> p k s", k=KT),
                                     ACT.Copy).then_inc(xn_hi, 1)
            for j in range(4):
                hi_of(wa, j, slot_uses(2))

            def v_from(c, b):
                act.wait_ge(v_mm, once(4 * c + b + 1, 8))
                nc.scalar.activation(v_all[:, b, c * 512:(c + 1) * 512], proj_ps[b % 2][:], ACT.Copy).then_inc(v_out, 1)

            def wk_split(g):
                if not (isinstance(g, int) and g == 0):
                    act.wait_ge(k_mm, head(g, 1, 0))
                act.wait_ge(raw_k_in, head(g, 16, 16))
                nc.scalar.activation(wk[0][:], raw_k[:], ACT.Copy).then_inc(wk_hi, 1)

            for c in range(2):
                for b in range(HB):
                    v_from(c, b)
                for j in range(4):
                    hi_of(wa, j, slot_uses(3 + c), [(v_mm, once(4 * c + 4, 8))])
            wk_split(0)

            def norm_hi(g):
                for b in range(HB):
                    act.wait_ge(o_norm, head(g, HB, b + 1))
                    nc.scalar.activation(oT[0][:, b, :], o_raw[:, b, :], ACT.Copy).then_inc(o_hi, 1)

            def body(g, first, last):
                act.wait_ge(k_full, head(g, 1, 1))
                if not first:
                    act.wait_ge(s_mm, head(g, HB, 0))
                nc.scalar.activation(kT[0][:], rope_a[:, 1, :], ACT.Copy).then_inc(k_hi, 1)
                for h in range(G):
                    act.wait_ge(q_full, head(g, G, h + 1))
                    nc.scalar.activation(qT[0][:, h, :], rope_a[:, h % 2, :], ACT.Copy).then_inc(q_hi, 1)
                if not first:
                    norm_hi(g - 1)
                if not last:
                    wk_split(g + 1)
                    for j in range(4):
                        hi_of(wa, j, landed_wq(g + 1), [(q_mm, head(g, G, G))])

                def tanh(b):
                    act.wait_ge(s_mm, head(g, HB, b + 1))
                    if not (first and b < 2):
                        act.wait_ge(p_lo, head(g, HB, b - 1))
                    nc.scalar.activation(prob[:, b % 2, :], s_ps[b % 2][:], ACT.Tanh, scale=TANH_SCALE).then_inc(s_tanh, 1)

                def exp(b):
                    act.wait_ge(s_masked, head(g, HB, b + 1))
                    nc.scalar.activation(prob[:, b % 2, :], prob[:, b % 2, :], ACT.Exp, scale=CAP).then_inc(p_exp, 1)
                    act.wait_ge(p_exp, head(g, HB, b + 1))
                    if not (first and b < 2):
                        act.wait_ge(o_mm, head(g, HB, b - 1))
                    nc.scalar.activation(pT[0][:, b % 2, :], prob[:, b % 2, :], ACT.Copy).then_inc(p_hi, 1)

                def out(b):
                    act.wait_ge(o_mm, head(g, HB, b + 1))
                    if not first:
                        act.wait_ge(o_lo, head(g, HB, b + 1 - HB))
                    nc.scalar.activation(o_raw[:, b, :], o_ps[:], ACT.Copy).then_inc(o_out, 1)

                def wo_hi(j):
                    free = [] if first else [(y_mm, head(g, HB, 0))]
                    hi_of(wo, j, landed_wo(g, last), free)

                tanh(0)
                wo_hi(0)
                tanh(1)
                exp(0)
                wo_hi(1)
                tanh(2)
                exp(1)
                out(0)
                wo_hi(2)
                tanh(3)
                exp(2)
                out(1)
                wo_hi(3)
                exp(3)
                out(2)
                out(3)

            heads(act, body)
            norm_hi(NKV - 1)

        @block.vector
        def _(dve):
            for b in range(HB):
                nc.vector.tensor_scalar(xn[:, b:b + 1, :], mem["x_acc"][:, bass.ds(half * HB + b, 1), :],
                                        mem["mv"][:].rearrange("p b s -> p (b s)")[:, bass.ds((half * HB + b) * 2, 1)],
                                        mem["rstd"][:, bass.ds(half * HB + b, 1)], ALU.subtract, ALU.mult).then_inc(xn_done, 1)
            for b in range(HB):
                dve.wait_ge(xn_hi, once(b + 1, HB))
                nc.vector.tensor_tensor(xnT[1][:, :, b * S:(b + 1) * S], s_ps[b % 2][:].rearrange("p (k s) -> p k s", k=KT),
                                        raw(xnT[0][:, :, b * S:(b + 1) * S]), ALU.subtract).then_inc(xn_lo, 1)

            def wk_lo_of(g):
                dve.wait_ge(wk_hi, head(g, 1, 1))
                nc.vector.tensor_tensor(wk[1][:], raw_k[:], raw(wk[0][:]), ALU.subtract).then_inc(wk_lo, 1)

            wk_lo_of(0)

            def reciprocal(g):
                dve.wait_ge(sum_mm, head(g, 1, 1))
                if not (isinstance(g, int) and g == 0):
                    dve.wait_ge(rows_out, head(g, 16, 0))
                nc.vector.reciprocal(rinv_rows[:], sum_ps[0:HB, :]).then_inc(rows_done, 1)

            def rotary(slot, src, cos, sin, done):
                a = rope_a[:, slot, :].rearrange("p (b t) -> p b t", b=HB)
                r = rope_b[:, slot, :].rearrange("p (b t) -> p b t", b=HB)
                s = src[:].rearrange("p (b t) -> p b t", b=HB)
                wide = lambda t, lo, hi: t[lo:hi, :].unsqueeze(1).to_broadcast([hi - lo, HB, S])
                nc.vector.tensor_tensor(a, s, wide(cos, 0, P), ALU.mult)
                nc.vector.tensor_tensor(r[0:64], s[64:128], wide(sin, 0, 64), ALU.mult)
                nc.vector.tensor_tensor(r[64:128], s[0:64], wide(sin, 64, 128), ALU.mult).then_inc(done, 1)

            def norm(g, b):
                dve.wait_ge(rinv_in, head(g, 16, 16))
                dve.wait_ge(o_out, head(g, HB, b + 1))
                nc.vector.tensor_tensor(o_raw[:, b, :], o_raw[:, b, :], rinv[:, b, :], ALU.mult).then_inc(o_norm, 1)

            def norm_lo(g, b):
                dve.wait_ge(o_hi, head(g, HB, b + 1))
                nc.vector.tensor_tensor(oT[1][:, b, :], o_raw[:, b, :], raw(oT[0][:, b, :]), ALU.subtract).then_inc(o_lo, 1)

            def add_y(g, b):
                dve.wait_ge(y_mm, head(g, HB, b + 1))
                nc.vector.tensor_tensor(mem["x_acc"][:, bass.ds(half * HB + b, 1), :], mem["x_acc"][:, bass.ds(half * HB + b, 1), :],
                                        y_ps[b % 2][:].unsqueeze(1), ALU.add).then_inc(y_add, 1)

            def body(g, first, last):
                if not first:
                    reciprocal(g - 1)
                dve.wait_ge(k_mm, head(g, 1, 1))
                if not first:
                    dve.wait_ge(q_lo, head(g, G, 0))
                rotary(1, k_ps, mem["cos_k"], mem["sin_k"], k_mul)
                dve.wait_ge(k_mul, head(g, 1, 1))
                nc.vector.tensor_tensor(rope_a[:, 1, :], rope_a[:, 1, :], rope_b[:, 1, :], ALU.add).then_inc(k_full, 1)

                def queries(h):
                    dve.wait_ge(q_mm, head(g, G, h + 1))
                    if h >= 2:
                        dve.wait_ge(q_lo, head(g, G, h - 1))
                    elif h == 1:
                        dve.wait_ge(k_lo, head(g, 1, 1))
                    rotary(h % 2, proj_ps[h % 2], mem["cos_q"], mem["sin_q"], q_mul)

                def queries_lo(h):
                    dve.wait_ge(q_hi, head(g, G, h + 1))
                    nc.vector.tensor_tensor(qT[1][:, h, :], rope_a[:, h % 2, :], raw(qT[0][:, h, :]), ALU.subtract).then_inc(q_lo, 1)

                queries(0)
                dve.wait_ge(k_hi, head(g, 1, 1))
                nc.vector.tensor_tensor(kT[1][:], rope_a[:, 1, :], raw(kT[0][:]), ALU.subtract).then_inc(k_lo, 1)
                if not first:
                    dve.wait_ge(o_mm, head(g, HB, 0))
                else:
                    dve.wait_ge(v_out, once(8, 8))
                nc.vector.tensor_scalar(vg[0][:], v_all[:, :, bass.ds(g * DH, DH)], 1.0, None, ALU.mult).then_inc(vg_hi, 1)
                queries(1)
                queries_lo(0)
                dve.wait_ge(vg_hi, head(g, 1, 1))
                nc.vector.tensor_tensor(vg[1][:], v_all[:, :, bass.ds(g * DH, DH)], raw(vg[0][:]), ALU.subtract).then_inc(vg_lo, 1)
                queries(2)
                queries_lo(1)
                queries(3)
                queries_lo(2)
                if not first:
                    norm(g - 1, 0)
                queries_lo(3)
                if not first:
                    norm(g - 1, 1)
                    norm_lo(g - 1, 0)
                    norm(g - 1, 2)
                    norm_lo(g - 1, 1)
                    norm(g - 1, 3)
                    norm_lo(g - 1, 2)
                    norm_lo(g - 1, 3)
                if not last:
                    wk_lo_of(g + 1)
                if not first:
                    add_y(g - 1, 0)
                    add_y(g - 1, 1)
                    add_y(g - 1, 2)
                    add_y(g - 1, 3)
                for b in range(HB):
                    dve.wait_ge(p_hi, head(g, HB, b + 1))
                    nc.vector.tensor_tensor(pT[1][:, b % 2, :], prob[:, b % 2, :], raw(pT[0][:, b % 2, :]), ALU.subtract).then_inc(p_lo, 1)

            heads(dve, body)
            g = NKV - 1
            reciprocal(g)
            for b in range(HB):
                norm(g, b)
            for b in range(HB):
                norm_lo(g, b)
            for b in range(HB):
                add_y(g, b)

        @block.tensor
        def _(pe):
            def product(out, w, x, wsl, xsl):
                n = 0
                for k in range(KT):
                    for a, c in split_passes(w[0], w[1], x[0], x[1]):
                        last = nc.tensor.matmul(out, wsl(a, k), xsl(c, k), start=(n == 0), stop=(n == 3 * KT - 1))
                        n += 1
                return last

            for b in range(HB):
                pe.wait_ge(xn_done, once(b + 1, HB))
                if b >= 2:
                    pe.wait_ge(xn_lo, once(b - 1, HB))
                for k in range(KT):
                    last = nc.tensor.transpose(s_ps[b % 2][:, k * S:(k + 1) * S], xn[:, b, k * P:(k + 1) * P], mem["ident"][:])
                last.then_inc(xn_tr, 1)
            for c in range(2):
                pe.wait_ge(piece_hi, once(WV0 + 4 * c + 4, PIECES))
                pe.wait_ge(piece_lo, once(WV0 + 4 * c + 4, PIECES))
                for b in range(HB):
                    if 4 * c + b >= 2:
                        pe.wait_ge(v_out, once(4 * c + b - 1, 8))
                    product(proj_ps[b % 2][:], ctxT, wa, lambda a, k: a[:, k, b * S:(b + 1) * S], lambda a, k: a[:, k, :]).then_inc(v_mm, 1)

            def y_of(g, b, first, last):
                pe.wait_ge(o_lo, head(g, HB, b + 1))
                if b == 0:
                    pe.wait_ge(piece_hi, wo_pieces(g, 3))
                    pe.wait_ge(piece_lo, wo_pieces(g, 3))
                if b >= 2:
                    pe.wait_ge(y_add, head(g, HB, b - 1))
                n = 0
                for h in range(G):
                    for a, c in split_passes(oT[0], oT[1], wo[0], wo[1]):
                        last_mm = nc.tensor.matmul(y_ps[b % 2][:], a[:, b, h * S:(h + 1) * S], c[:, h, :],
                                                   start=(n == 0), stop=(n == 3 * G - 1))
                        n += 1
                last_mm.then_inc(y_mm, 1)

            def body(g, first, last):
                pe.wait_ge(wk_lo, head(g, 1, 1))
                if first:
                    pe.wait_ge(xn_lo, once(HB, HB))
                product(k_ps[:], wk, ctxT, lambda a, k: a[:, k, :], lambda a, k: a[:, k, :]).then_inc(k_mm, 1)
                pe.wait_ge(piece_hi, wq_pieces(g, 3))
                pe.wait_ge(piece_lo, wq_pieces(g, 3))
                for h in range(G):
                    if h >= 2 or not first:
                        pe.wait_ge(q_mul, head(g, G, h - 1))
                    else:
                        pe.wait_ge(v_out, once(7 + h, 8))
                    product(proj_ps[h % 2][:], wa, xnT, lambda a, k: a[:, k, h * DH:(h + 1) * DH], lambda a, k: a[:, k, :]).then_inc(q_mm, 1)

                def scores(b):
                    if b == 0:
                        pe.wait_ge(k_lo, head(g, 1, 1))
                        pe.wait_ge(q_lo, head(g, G, G))
                    if b >= 2 or not first:
                        pe.wait_ge(s_tanh, head(g, HB, b - 1))
                    for n, (a, c) in enumerate(split_passes(kT[0], kT[1], qT[0], qT[1])):
                        last = nc.tensor.matmul(s_ps[b % 2][:], a[:, b * S:(b + 1) * S], c[:, :, b * S:(b + 1) * S],
                                                start=(n == 0), stop=(n == 2))
                    last.then_inc(s_mm, 1)

                def outputs(b):
                    pe.wait_ge(p_lo, head(g, HB, b + 1))
                    if b == 0:
                        pe.wait_ge(vg_lo, head(g, 1, 1))
                        if not first:
                            pe.wait_ge(rows_done, head(g, 1, 0))
                    if b > 0 or not first:
                        pe.wait_ge(o_out, head(g, HB, b))
                    for n, part in enumerate((pT[1], pT[0])):
                        last = nc.tensor.matmul(sum_ps[:], mem["pick"][:, b, :], part[:, b % 2, :],
                                                start=(b == 0 and n == 0), stop=(b == HB - 1 and n == 1))
                    if b == HB - 1:
                        last.then_inc(sum_mm, 1)
                    for n, (a, c) in enumerate(split_passes(vg[0], vg[1], pT[0], pT[1])):
                        last = nc.tensor.matmul(o_ps[:], a[:, b, :], c[:, b % 2, :], start=(n == 0), stop=(n == 2))
                    last.then_inc(o_mm, 1)

                if not first:
                    pe.wait_ge(k_mul, head(g, 1, 1))
                    y_of(g - 1, 0, False, last)
                    y_of(g - 1, 1, False, last)
                    scores(0)
                    y_of(g - 1, 2, False, last)
                    scores(1)
                    y_of(g - 1, 3, False, last)
                else:
                    scores(0)
                    scores(1)
                scores(2)
                outputs(0)
                scores(3)
                outputs(1)
                outputs(2)
                outputs(3)

            heads(pe, body)
            for b in range(HB):
                y_of(NKV - 1, b, False, True)


def normalised_columns(nc, mem, xn, xnT, banks, sem):
    ln_sems = [sem(n) for n in ("stat", "aggr", "eps_added", "rstd_done")]
    xn_done, xn_tr, xn_hi, xn_lo = (sem(n) for n in ("xn_done", "xn_tr", "xn_hi", "xn_lo"))
    ln_vector, ln_pool = row_statistics(nc, mem, ln_sems, lambda dve, b: None)
    columns = lambda part, b: part[:, :, b * S:(b + 1) * S]
    bank = lambda b: banks[b % 2][:].rearrange("p (k s) -> p k s", k=KT)

    def vector(dve):
        ln_vector(dve)
        dve.wait_ge(ln_sems[3], 1)

        def lo(b):
            dve.wait_ge(xn_hi, b + 1)
            nc.vector.tensor_tensor(columns(xnT[1], b), bank(b), raw(columns(xnT[0], b)), ALU.subtract).then_inc(xn_lo, 1)

        for b in range(B):
            nc.vector.tensor_scalar(xn[:, b, :], mem["x_acc"][:, b, :], mem["mv"][:, b, 0:1], mem["rstd"][:, b:b + 1],
                                    ALU.subtract, ALU.mult).then_inc(xn_done, 1)
            if b >= 2:
                lo(b - 2)
        lo(B - 2)
        lo(B - 1)

    def scalar(act):
        for b in range(B):
            act.wait_ge(xn_tr, b + 1)
            nc.scalar.activation(columns(xnT[0], b), bank(b), ACT.Copy).then_inc(xn_hi, 1)

    def tensor(pe):
        for b in range(B):
            pe.wait_ge(xn_done, b + 1)
            if b >= 2:
                pe.wait_ge(xn_lo, b - 1)
            for k in range(KT):
                last = nc.tensor.transpose(banks[b % 2][:, k * S:(k + 1) * S], xn[:, b, k * P:(k + 1) * P], mem["ident"][:])
            last.then_inc(xn_tr, 1)

    return vector, ln_pool, scalar, tensor, xn_lo


FF = 1792
FG = 2
NG = FF // (P * FG)


def layer0_ffn(nc, io, mem):
    with ExitStack() as ctx:
        sb = lambda name, shape, dt=F32: ctx.enter_context(nc.sbuf_tensor(f"ffn_{name}", shape, dt))
        ps = lambda name: ctx.enter_context(nc.psum_tensor(f"ffn_{name}", [P, 512], F32))
        sem = stage_semaphores(nc, ctx, "ffn_")
        FW = FG * P
        xnT = [sb(f"xnT_{n}", [P, KT, B * S], F32R) for n in ("hi", "lo")]
        w_raw = {"gate": sb("gate_raw", [P, KT, FW], I32), "up": sb("up_raw", [P, KT, FW], I32), "down": sb("down_raw", [P, FG, D], I32)}
        w = {n: [sb(f"{n}_{part}", list(w_raw[n].shape), F32R) for part in ("hi", "lo")] for n in w_raw}
        y_acc = sb("y_acc", [P, B, D])
        hT = [sb(f"hT_{n}", [P, FG, B * S], F32R) for n in ("hi", "lo")]
        silu = sb("silu", [P, 2, HR])
        hidden = sb("hidden", [P, 2, HR])
        scales = sb("scales", [P, NG, 2 * FG])
        now = sb("now", [P, 2 * FG])
        down_s = sb("down_s", [P, D])
        xn = y_acc
        gate_ps, up_ps, y_ps = ([ps(f"{n}{i}_ps") for i in range(2)] for n in ("gate", "up", "y"))
        vector_ln, pool_ln, scalar_ln, tensor_ln, xn_lo = normalised_columns(nc, mem, xn, xnT, y_ps, sem)
        w_in = {n: sem(f"{n}_in") for n in w}
        w_hi = {n: sem(f"{n}_hi") for n in w}
        w_lo = {n: sem(f"{n}_lo") for n in w}
        (scales_in, down_s_in, now_set, gu_mm, silu_done, h_full, h_hi, h_lo, y_mm, y_add, y_scaled, cleared) = [sem(n) for n in (
            "scales_in down_s_in now_set gu_mm silu_done h_full h_hi h_lo y_mm y_add y_scaled cleared").split()]
        block = ctx.enter_context(nc.Block())

        def groups(eng, body):
            body(0, True, False)
            with eng.Fori(1, NG - 1) as i:
                body(i, False, False)
            body(NG - 1, False, True)

        gate_d = io["gate_t"].rearrange("(k p) f -> p k f", p=P)
        up_d = io["up_t"].rearrange("(k p) f -> p k f", p=P)
        down_d = io["down_t"].rearrange("(k p) n -> p k n", p=P)

        @block.sync
        def _(sp):
            sp.dma_start(w_raw["gate"][:], gate_d[:, :, 0:FW]).then_inc(w_in["gate"], 16)
            sp.dma_start(w_raw["up"][:], up_d[:, :, 0:FW]).then_inc(w_in["up"], 16)
            sp.dma_start(w_raw["down"][:], down_d[:, 0:FG, :]).then_inc(w_in["down"], 16)
            sp.dma_start(scales[:], io["gu_s"].rearrange("p (i s) -> p i s", i=NG)).then_inc(scales_in, 16)
            sp.dma_start(down_s[:], io["down_s"].rearrange("(o n) -> o n", o=1).to_broadcast([P, D])).then_inc(down_s_in, 16)
            with sp.Fori(0, NG - 1) as i:
                for name, src in (("gate", gate_d[:, :, bass.ds(i * FW + FW, FW)]), ("up", up_d[:, :, bass.ds(i * FW + FW, FW)]),
                                  ("down", down_d[:, bass.ds(i * FG + FG, FG), :])):
                    sp.wait_ge(w_lo[name], i + 1)
                    sp.dma_start(w_raw[name][:], src).then_inc(w_in[name], 16)

        @block.gpsimd
        def _(pool):
            pool_ln(pool)
            pool.wait_ge(xn_lo, B)
            nc.gpsimd.memset(y_acc[:], 0.0).then_inc(cleared, 1)

        @block.scalar
        def _(act):
            def split(name, i):
                act.wait_ge(w_in[name], i * 16 + 16)
                nc.scalar.activation(w[name][0][:], w_raw[name][:], ACT.Copy).then_inc(w_hi[name], 1)

            split("gate", 0)
            split("up", 0)
            split("down", 0)
            scalar_ln(act)

            def body(i, first, last):
                act.wait_ge(now_set, i + 1)

                def gate(n):
                    act.wait_ge(gu_mm, i * 4 + (n + 1))
                    if n >= 2 or not first:
                        act.wait_ge(h_full, i * 4 + (n - 1))
                    t = n % 2
                    nc.scalar.activation(silu[:, n % 2, :], gate_ps[n % 2][:], ACT.Silu, scale=now[:, t:t + 1]).then_inc(silu_done, 1)

                def hi(n):
                    r, t = n // 2, n % 2
                    act.wait_ge(h_full, i * 4 + (n + 1))
                    if not first:
                        act.wait_ge(y_mm, i * B + (HB * (r + 1) - B))
                    nc.scalar.activation(hT[0][:, t, r * HR:(r + 1) * HR], hidden[:, n % 2, :], ACT.Copy).then_inc(h_hi, 1)

                gate(0)
                gate(1)
                hi(0)
                gate(2)
                hi(1)
                gate(3)
                hi(2)
                hi(3)
                if not last:
                    act.wait_ge(gu_mm, i * 4 + 4)
                    split("gate", i + 1)
                    split("up", i + 1)
                    act.wait_ge(y_mm, i * B + B)
                    split("down", i + 1)
            groups(act, body)

        @block.vector
        def _(dve):
            def split(name, i):
                dve.wait_ge(w_hi[name], i + 1)
                nc.vector.tensor_tensor(w[name][1][:], w_raw[name][:], raw(w[name][0][:]), ALU.subtract).then_inc(w_lo[name], 1)

            vector_ln(dve)
            split("gate", 0)
            split("up", 0)
            split("down", 0)
            dve.wait_ge(scales_in, 16)

            def body(i, first, last):
                nc.vector.tensor_scalar(now[:].unsqueeze(1), scales[:, bass.ds(i, 1), :] if not isinstance(i, int) else scales[:, i:i + 1, :],
                                        1.0, None, ALU.mult).then_inc(now_set, 1)
                dve.wait_ge(now_set, i + 1)

                def product(n):
                    dve.wait_ge(silu_done, i * 4 + (n + 1))
                    if n >= 2 or not first:
                        dve.wait_ge(h_lo, i * 4 + (n - 1))
                    t = n % 2
                    nc.vector.scalar_tensor_tensor(hidden[:, n % 2, :], up_ps[n % 2][:], now[:, FG + t:FG + t + 1], silu[:, n % 2, :],
                                                   ALU.mult, ALU.mult).then_inc(h_full, 1)

                def lo(n):
                    r, t = n // 2, n % 2
                    dve.wait_ge(h_hi, i * 4 + (n + 1))
                    nc.vector.tensor_tensor(hT[1][:, t, r * HR:(r + 1) * HR], hidden[:, n % 2, :],
                                            raw(hT[0][:, t, r * HR:(r + 1) * HR]), ALU.subtract).then_inc(h_lo, 1)

                product(0)
                product(1)
                lo(0)
                product(2)
                lo(1)
                product(3)
                lo(2)
                lo(3)
                if not last:
                    split("gate", i + 1)
                    split("up", i + 1)
                if first:
                    dve.wait_ge(cleared, 1)
                for b in range(B):
                    dve.wait_ge(y_mm, i * B + (b + 1))
                    nc.vector.tensor_tensor(y_acc[:, b, :], y_acc[:, b, :], y_ps[b % 2][:], ALU.add).then_inc(y_add, 1)
                if not last:
                    split("down", i + 1)
            groups(dve, body)
            dve.wait_ge(down_s_in, 16)
            dve.wait_ge(y_add, NG * B)
            for b in range(B):
                nc.vector.tensor_tensor(y_acc[:, b, :], y_acc[:, b, :], down_s[:], ALU.mult).then_inc(y_scaled, 1)
            for b in range(B):
                dve.wait_ge(y_scaled, b + 1)
                nc.vector.tensor_tensor(mem["x_acc"][:, b, :], mem["x_acc"][:, b, :], y_acc[:, b, :], ALU.add)

        @block.tensor
        def _(pe):
            tensor_ln(pe)

            def body(i, first, last):
                pe.wait_ge(w_lo["gate"], i + 1)
                pe.wait_ge(w_lo["up"], i + 1)
                if first:
                    pe.wait_ge(xn_lo, B)
                for n in range(4):
                    r, t = n // 2, n % 2
                    if n >= 2 or not first:
                        pe.wait_ge(h_full, i * 4 + (n - 1))
                    for name, bank in (("gate", gate_ps), ("up", up_ps)):
                        m = 0
                        for k in range(KT):
                            for a, c in split_passes(w[name][0], w[name][1], xnT[0], xnT[1]):
                                last_mm = nc.tensor.matmul(bank[n % 2][:], a[:, k, t * P:(t + 1) * P], c[:, k, r * HR:(r + 1) * HR],
                                                           start=(m == 0), stop=(m == 3 * KT - 1))
                                m += 1
                    last_mm.then_inc(gu_mm, 1)
                pe.wait_ge(w_lo["down"], i + 1)
                for b in range(B):
                    if b % HB == 0:
                        pe.wait_ge(h_lo, i * 4 + (2 if b == 0 else 4))
                    if b >= 2 or not first:
                        pe.wait_ge(y_add, i * B + (b - 1))
                    m = 0
                    for t in range(FG):
                        for a, c in split_passes(hT[0], hT[1], w["down"][0], w["down"][1]):
                            last_mm = nc.tensor.matmul(y_ps[b % 2][:], a[:, t, b * S:(b + 1) * S], c[:, t, :],
                                                       start=(m == 0), stop=(m == 3 * FG - 1))
                            m += 1
                    last_mm.then_inc(y_mm, 1)
            groups(pe, body)


H1, DH1 = 8, 8
E1 = H1 * DH1
NP = D // P
HG = 4
PICKED = 3
VW = 32
NO_KEY = 1e9 * 8 ** 0.5


def layer1_attention(nc, io, mem):
    with ExitStack() as ctx:
        sb = lambda name, shape, dt=F32: ctx.enter_context(nc.sbuf_tensor(f"att_{name}", shape, dt))
        ps = lambda name, shape, dt=F32: ctx.enter_context(nc.psum_tensor(f"att_{name}", shape, dt))
        sem = stage_semaphores(nc, ctx, "att_")
        BF16 = mybir.dt.bfloat16
        ctx_raw = sb("ctx_raw", [P, D])
        ctx_s = [sb(f"ctx_{n}", [P, D], F32R) for n in ("hi", "lo")]
        xn = sb("xn", [P, 1, D])
        xn_s = [sb(f"xn_{n}", [P, D], F32R) for n in ("hi", "lo")]
        seen = sb("seen", [P, D])
        qk_raw = sb("qk_raw", [P, 2, E1])
        qk_wide = sb("qk_wide", [P, 4, 4, 32])
        qk_s = [sb(f"qk_{n}", [P, 4, P], F32R) for n in ("hi", "lo")]
        wv_raw = sb("wv_raw", [P, E1])
        wv_s = [sb(f"wv_{n}", [P, E1], F32R) for n in ("hi", "lo")]
        bias = sb("bias", [P, 4])
        bv = sb("bv", [P, E1])
        own = sb("own", [P, HG + 1])
        ident16 = sb("ident16", [P, P], F16)
        q_full = sb("q_full", [P, 2, D])
        q_s = sb("q_s", [P, 2, D], F32R)
        k_full = sb("k_full", [P, 2, D])
        k_s = sb("k_s", [P, 2, D], F32R)
        k_own = sb("k_own", [P, 2, NP, HG, P], F32R)
        v_full = sb("v_full", [P, NP, H1, DH1])
        v_rest = sb("v_rest", [P, NP, H1, DH1])
        vT = sb("vT", [P, NP, H1, VW], BF16)
        top = sb("top", [P, 2, H1])
        prob = sb("prob", [P, 2, H1, P])
        prob_s = [sb(f"prob_{n}", [P, 2, H1, P], F16) for n in ("hi", "lo")]
        pT = [sb(f"pT_{n}", [P, 2, H1, P], F16) for n in ("hi", "lo")]
        o_sum = sb("o_sum", [P, NP * H1, DH1])
        rsum = sb("rsum", [P, NP * H1])
        sc_ps = [ps(f"sc{i}", [P, 2, 512]) for i in range(2)]
        t_ps = [ps(f"t{i}", [P, H1, P], F16) for i in range(2)]
        o_ps = ps("o", [P, NP, H1, VW])
        v_ps = o_ps[:].rearrange("p a h c -> p (a h c)")[:, 0:NP * E1]
        ln_sems = [sem(n) for n in ("stat", "aggr", "eps_added", "rstd_done")]
        vector_ln, pool_ln = row_statistics(nc, mem, ln_sems, lambda dve, b: None)
        (w_in, seen_in, ctx_in, prep, wide, wide_hi, wide_lo, wv_hi, wv_lo, ones_set, id16, is_seen, xn_full, xn_hi, xn_lo,
         ctx_hi, ctx_lo, q_mm, k_mm, v_mm, q_out, q_hi, q_lo, k_out, k_hi, k_lo, k_mask, own_a, own_b,
         v_out, v1, v2, v3, rest, s_mm, top_done, s_sub, p_exp, p_hi, p_lo, t_mm, t_hi, t_lo, o_mm, o_added, o_inv, o_done) = [
            sem(n) for n in (
                "w_in seen_in ctx_in prep wide wide_hi wide_lo wv_hi wv_lo ones_set id16 is_seen xn_full xn_hi xn_lo "
                "ctx_hi ctx_lo q_mm k_mm v_mm q_out q_hi q_lo k_out k_hi k_lo k_mask own_a own_b "
                "v_out v1 v2 v3 rest s_mm top_done s_sub p_exp p_hi p_lo t_mm t_hi t_lo o_mm o_added o_inv o_done").split()]
        block = ctx.enter_context(nc.Block())

        def batches(eng, body):
            body(0, True)
            with eng.Fori(1, B) as b:
                body(b, False)

        @block.sync
        def _(sp):
            sp.dma_start(qk_raw[:], io["qk1_t"]).then_inc(w_in, 16)
            sp.dma_start(wv_raw[:], io["wv1_t"]).then_inc(w_in, 16)
            sp.dma_start(bias[:], io["qk1_bias"]).then_inc(w_in, 16)
            sp.dma_start(bv[:], io["bv1"].rearrange("(o n) -> o n", o=1).to_broadcast([P, E1])).then_inc(w_in, 16)
            sp.dma_start(own[:], io["own"]).then_inc(w_in, 16)
            sp.dma_start(ctx_raw[:], io["ctx"][0]).then_inc(ctx_in, 16)
            sp.dma_start(mem["seen_all"][:].rearrange("p b n -> p (b n)"),
                         io["key_mask"].rearrange("b o n -> (b o n)").rearrange("(o n) -> o n", o=1).to_broadcast([P, B * D])).then_inc(seen_in, 16)
            with sp.Fori(0, B - 1) as b:
                sp.wait_ge(ctx_lo, b + 1)
                sp.dma_start(ctx_raw[:].unsqueeze(1), io["ctx"].rearrange("b d s -> d b s")[:, bass.ds(b + 1, 1), :]).then_inc(ctx_in, 16)

        @block.gpsimd
        def _(pool):
            pool_ln(pool)
            nc.gpsimd.memset(qk_wide[:], 0.0).then_inc(prep, 1)
            nc.gpsimd.memset(vT[:], 1.0).then_inc(ones_set, 1)
            nc.gpsimd.tensor_copy(ident16[:], mem["ident"][:]).then_inc(id16, 1)

            def body(b, first):
                pool.wait_ge(ctx_hi, b + 1)
                nc.gpsimd.tensor_tensor(ctx_s[1][:], ctx_raw[:], raw(ctx_s[0][:]), ALU.subtract).then_inc(ctx_lo, 1)
                pool.wait_ge(v1, b + 1)
                nc.gpsimd.tensor_tensor(v_rest[:], v_full[:], vT[:, :, :, 0:DH1], ALU.subtract).then_inc(rest, 1)
                pool.wait_ge(v2, b + 1)
                nc.gpsimd.tensor_tensor(v_rest[:], v_rest[:], vT[:, :, :, DH1:2 * DH1], ALU.subtract).then_inc(rest, 1)
                pool.wait_ge(k_lo, b + 1)
                pool.wait_ge(k_mask, b + 1)
                if not first:
                    pool.wait_ge(s_mm, b * NP)
                for g in range(2):
                    for h in (2, 3):
                        last = nc.gpsimd.tensor_tensor(k_own[:, g, :, h, :], raw(k_s[:, g, :]).rearrange("p (a j) -> p a j", a=NP),
                                                       own[:, h:h + 1].unsqueeze(2).to_broadcast([P, NP, P]), ALU.mult)
                last.then_inc(own_b, 1)
                for p in range(NP):
                    pool.wait_ge(p_hi, b * NP + (p + 1))
                    nc.gpsimd.tensor_tensor(prob_s[1][:, p % 2], prob[:, p % 2], prob_s[0][:, p % 2], ALU.subtract).then_inc(p_lo, 1)
            batches(pool, body)

        @block.scalar
        def _(act):
            act.wait_ge(wide, 2)
            nc.scalar.activation(qk_s[0][:], qk_wide[:].rearrange("p a t e -> p a (t e)"), ACT.Copy).then_inc(wide_hi, 1)
            nc.scalar.activation(wv_s[0][:], wv_raw[:], ACT.Copy).then_inc(wv_hi, 1)

            def body(b, first):
                act.wait_ge(ctx_in, b * 16 + 16)
                if not first:
                    act.wait_ge(v_mm, b)
                nc.scalar.activation(ctx_s[0][:], ctx_raw[:], ACT.Copy).then_inc(ctx_hi, 1)
                act.wait_ge(xn_full, b + 1)
                if not first:
                    act.wait_ge(k_mm, b * 2)
                nc.scalar.activation(xn_s[0][:], xn[:, 0, :], ACT.Copy).then_inc(xn_hi, 1)
                for g in range(2):
                    act.wait_ge(q_mm, b * 2 + (g + 1))
                    if not first:
                        act.wait_ge(s_mm, b * NP)
                        act.wait_ge(q_lo, b)
                    nc.scalar.activation(q_full[:, g, :], sc_ps[0][:, g, :], ACT.Identity, bias=bias[:, g:g + 1]).then_inc(q_out, 1)
                    nc.scalar.activation(q_s[:, g, :], sc_ps[0][:, g, :], ACT.Identity, bias=bias[:, g:g + 1]).then_inc(q_hi, 1)
                act.wait_ge(k_out, b * 2 + 2)
                if not first:
                    act.wait_ge(own_a, b)
                    act.wait_ge(own_b, b)
                nc.scalar.activation(k_s[:], k_full[:], ACT.Copy).then_inc(k_hi, 1)
                act.wait_ge(v_out, b + 1)
                if not first:
                    act.wait_ge(o_mm, b * NP)
                nc.scalar.activation(vT[:, :, :, 0:DH1], v_full[:], ACT.Copy).then_inc(v1, 1)
                act.wait_ge(rest, b * 2 + 1)
                nc.scalar.activation(vT[:, :, :, DH1:2 * DH1], v_rest[:], ACT.Copy).then_inc(v2, 1)
                act.wait_ge(rest, b * 2 + 2)
                nc.scalar.activation(vT[:, :, :, 2 * DH1:3 * DH1], v_rest[:], ACT.Copy).then_inc(v3, 1)

                def exp(p):
                    act.wait_ge(s_sub, b * NP + (p + 1))
                    nc.scalar.activation(prob[:, p % 2], prob[:, p % 2], ACT.Exp, scale=DH1 ** -0.5).then_inc(p_exp, 1)
                    act.wait_ge(p_exp, b * NP + (p + 1))
                    if p >= 2 or not first:
                        act.wait_ge(t_mm, b * NP + (p - 1))
                    nc.scalar.activation(prob_s[0][:, p % 2], prob[:, p % 2], ACT.Copy).then_inc(p_hi, 1)

                def turned(p):
                    act.wait_ge(t_mm, b * NP + (p + 1))
                    if p >= 2 or not first:
                        act.wait_ge(o_mm, b * NP + (p - 1))
                    nc.scalar.activation(pT[0][:, p % 2], t_ps[0][:], ACT.Copy).then_inc(t_hi, 1)

                exp(0)
                for p in range(1, NP):
                    exp(p)
                    turned(p - 1)
                turned(NP - 1)
            batches(act, body)

        @block.vector
        def _(dve):
            vector_ln(dve)
            dve.wait_ge(w_in, 80)
            dve.wait_ge(prep, 1)
            for n in range(2):
                nc.vector.tensor_copy(qk_wide[:, 2 * n:2 * n + 2, 0:3, :],
                                      qk_raw[:, n, :].rearrange("p (g e) -> p g e", g=2).unsqueeze(2).to_broadcast([P, 2, 3, 32])).then_inc(wide, 1)
            dve.wait_ge(wide_hi, 1)
            nc.vector.tensor_tensor(qk_s[1][:], qk_wide[:].rearrange("p a t e -> p a (t e)"), raw(qk_s[0][:]), ALU.subtract).then_inc(wide_lo, 1)
            dve.wait_ge(wv_hi, 1)
            nc.vector.tensor_tensor(wv_s[1][:], wv_raw[:], raw(wv_s[0][:]), ALU.subtract).then_inc(wv_lo, 1)
            dve.wait_ge(ln_sems[3], 1)
            dve.wait_ge(seen_in, 16)

            def body(b, first):
                at = bass.ds(b, 1)
                if not first:
                    dve.wait_ge(xn_lo, b)
                    dve.wait_ge(k_mask, b)
                nc.vector.tensor_scalar(xn[:], mem["x_acc"][:, at, :], mem["mv"][:].rearrange("p b s -> p (b s)")[:, bass.ds(b * 2, 1)],
                                        mem["rstd"][:, at], ALU.subtract, ALU.mult).then_inc(xn_full, 1)
                nc.vector.tensor_scalar(seen[:].unsqueeze(1), mem["seen_all"][:, at, :], 0.0, None, ALU.is_gt).then_inc(is_seen, 1)
                dve.wait_ge(xn_hi, b + 1)
                nc.vector.tensor_tensor(xn_s[1][:], xn[:, 0, :], raw(xn_s[0][:]), ALU.subtract).then_inc(xn_lo, 1)
                dve.wait_ge(is_seen, b + 1)
                for g in range(2):
                    dve.wait_ge(k_mm, b * 2 + (g + 1))
                    nc.vector.scalar_tensor_tensor(k_full[:, g, :], sc_ps[1][:, g, :], bias[:, 2 + g:3 + g], seen[:], ALU.add, ALU.mult).then_inc(k_out, 1)
                dve.wait_ge(v_mm, b + 1)
                if not first:
                    dve.wait_ge(v3, b)
                nc.vector.tensor_tensor(v_full[:], v_ps.rearrange("p (a h c) -> p a h c", a=NP, h=H1),
                                        bv[:].rearrange("p (h c) -> p h c", h=H1).unsqueeze(1).to_broadcast([P, NP, H1, DH1]), ALU.add).then_inc(v_out, 1)
                dve.wait_ge(q_hi, b * 2 + 2)
                nc.vector.tensor_tensor(q_s[64:96], q_full[64:96], raw(q_s[64:96]), ALU.subtract).then_inc(q_lo, 1)
                dve.wait_ge(k_hi, b + 1)
                nc.vector.tensor_tensor(k_s[32:64], k_full[32:64], raw(k_s[32:64]), ALU.subtract).then_inc(k_lo, 1)
                nc.vector.tensor_scalar(k_s[96:128], seen[96:128].unsqueeze(1).to_broadcast([32, 2, D]), 1.0,
                                        own[96:128, HG:HG + 1], ALU.subtract, ALU.mult).then_inc(k_mask, 1)
                dve.wait_ge(k_lo, b + 1)
                dve.wait_ge(k_mask, b + 1)
                for g in range(2):
                    for h in (0, 1):
                        last = nc.vector.tensor_scalar(k_own[:, g, :, h, :], raw(k_s[:, g, :]).rearrange("p (a j) -> p a j", a=NP),
                                                       own[:, h:h + 1], None, ALU.mult)
                last.then_inc(own_a, 1)

                def centre(p):
                    dve.wait_ge(s_mm, b * NP + (p + 1))
                    scores = sc_ps[p % 2][:].rearrange("p g (h j) -> p (g h) j", h=HG)
                    if p >= 2 or not first:
                        dve.wait_ge(s_sub, b * NP + (p - 1))
                    nc.vector.tensor_reduce(top[:, p % 2, :], scores, AX.X, ALU.max).then_inc(top_done, 1)
                    dve.wait_ge(top_done, b * NP + (p + 1))
                    if p >= 2 or not first:
                        dve.wait_ge(p_lo, b * NP + (p - 1))
                    nc.vector.tensor_tensor(prob[:, p % 2], scores, top[:, p % 2, :].unsqueeze(2).to_broadcast([P, H1, P]),
                                            ALU.subtract).then_inc(s_sub, 1)

                def turned(p):
                    dve.wait_ge(t_mm, b * NP + (p + 1))
                    if p >= 2 or not first:
                        dve.wait_ge(o_mm, b * NP + (p - 1))
                    nc.vector.tensor_copy(pT[1][:, p % 2], t_ps[1][:]).then_inc(t_lo, 1)

                centre(0)
                for p in range(1, NP):
                    centre(p)
                    turned(p - 1)
                turned(NP - 1)
                dve.wait_ge(o_mm, b * NP + NP)
                if not first:
                    dve.wait_ge(o_done, b)
                outputs = o_ps[:].rearrange("p a h c -> p (a h) c")
                nc.vector.tensor_reduce(o_sum[:], outputs[:, :, 0:PICKED * DH1].rearrange("p n (t c) -> p n c t", t=PICKED),
                                        AX.X, ALU.add).then_inc(o_added, 1)
                nc.vector.reciprocal(rsum[:], outputs[:, :, PICKED * DH1]).then_inc(o_inv, 1)
                dve.wait_ge(o_added, b + 1)
                dve.wait_ge(o_inv, b + 1)
                nc.vector.tensor_tensor(mem["o_all"][:, bass.ds(b * NP * H1, NP * H1), :], o_sum[:],
                                        rsum[:].unsqueeze(2).to_broadcast([P, NP * H1, DH1]), ALU.mult).then_inc(o_done, 1)
            batches(dve, body)

        @block.tensor
        def _(pe):
            pe.wait_ge(wide_lo, 1)
            pe.wait_ge(wv_lo, 1)
            pe.wait_ge(id16, 1)
            pe.wait_ge(ones_set, 1)

            def body(b, first):
                pe.wait_ge(xn_lo, b + 1)
                if not first:
                    pe.wait_ge(s_sub, b * NP)
                for n in range(4):
                    for m, (a, c) in enumerate(split_passes(qk_s[0], qk_s[1], xn_s[0], xn_s[1])):
                        last = nc.tensor.matmul(sc_ps[n // 2][:, n % 2, :], a[:, n, :], c[:], start=(m == 0), stop=(m == 2))
                    last.then_inc(q_mm if n < 2 else k_mm, 1)
                pe.wait_ge(ctx_lo, b + 1)
                if not first:
                    pe.wait_ge(o_done, b)
                for p in range(NP):
                    for m, (a, c) in enumerate(split_passes(ctx_s[0], ctx_s[1], wv_s[0], wv_s[1])):
                        last = nc.tensor.matmul(v_ps[:, p * E1:(p + 1) * E1], a[:, p * P:(p + 1) * P], c[:], start=(m == 0), stop=(m == 2))
                last.then_inc(v_mm, 1)

                def scores(p):
                    if p == 0:
                        pe.wait_ge(q_lo, b + 1)
                        pe.wait_ge(own_a, b + 1)
                        pe.wait_ge(own_b, b + 1)
                    if p >= 2:
                        pe.wait_ge(s_sub, b * NP + (p - 1))
                    for g in range(2):
                        last = nc.tensor.matmul(sc_ps[p % 2][:, g, :], q_s[:, g, p * P:(p + 1) * P], k_own[:, g, p],
                                                start=True, stop=True)
                    last.then_inc(s_mm, 1)

                def turn(p):
                    pe.wait_ge(p_lo, b * NP + (p + 1))
                    if p >= 1 or not first:
                        pe.wait_ge(t_hi, b * NP + p)
                        pe.wait_ge(t_lo, b * NP + p)
                    for n in range(2):
                        for h in range(H1):
                            last = nc.tensor.transpose(t_ps[n][:, h, :], prob_s[n][:, p % 2, h, :], ident16[:])
                    last.then_inc(t_mm, 1)

                def outputs(p):
                    pe.wait_ge(t_hi, b * NP + (p + 1))
                    pe.wait_ge(t_lo, b * NP + (p + 1))
                    if p == 0:
                        pe.wait_ge(v3, b + 1)
                    for h in range(H1):
                        for n in range(2):
                            last = nc.tensor.matmul(o_ps[:, p, h, 0:PICKED * DH1 + 1], pT[n][:, p % 2, h, :], vT[:, p, h, 0:PICKED * DH1 + 1],
                                                    start=(n == 0), stop=(n == 1))
                    last.then_inc(o_mm, 1)

                scores(0)
                scores(1)
                turn(0)
                scores(2)
                outputs(0)
                turn(1)
                scores(3)
                outputs(1)
                turn(2)
                outputs(2)
                turn(3)
                outputs(3)
            batches(pe, body)


def layer1_rest(nc, io, mem, out):
    NE = 2
    with ExitStack() as ctx:
        sb = lambda name, shape, dt=F32: ctx.enter_context(nc.sbuf_tensor(f"rest_{name}", shape, dt))
        ps = lambda name: ctx.enter_context(nc.psum_tensor(f"rest_{name}", [P, 512], F32))
        sem = stage_semaphores(nc, ctx, "rest_")
        wo_raw = sb("wo_raw", [E1, P])
        wo_s = [sb(f"wo_{n}", [E1, P], F32R) for n in ("hi", "lo")]
        bo = sb("bo", [P, 1])
        gelu = sb("gelu", [E1, 2, D])
        gelu_s = [sb(f"gelu_{n}", [E1, 2, D], F32R) for n in ("hi", "lo")]
        masked = sb("masked", [P, 2, D])
        a_raw = sb("a_raw", [P, NE, D])
        a_s = [sb(f"a_{n}", [P, NE, D], F32R) for n in ("hi", "lo")]
        b_raw = sb("b_raw", [P, NE, D])
        b_s = [sb(f"b_{n}", [P, NE, D], F32R) for n in ("hi", "lo")]
        cs = sb("cs", [P, 2, NE])
        w_exp = sb("w_exp", [P, NE])
        w1 = sb("w1", [P, KT, D])
        w1_s = [sb(f"w1_{n}", [P, KT, D], F32R) for n in ("hi", "lo")]
        bias = sb("bias", [P, D])
        xn = sb("xn", [P, B, D])
        xnT = [sb(f"xnT_{n}", [P, KT, B * S], F32R) for n in ("hi", "lo")]
        o_t_ps = [ps("o_t0"), ps("o_t1")]
        y_ps = [ps("y0"), ps("y1")]
        tr_ps = [ps("tr0"), ps("tr1")]
        m_ps = [ps("m0"), ps("m1")]
        vector_ln, pool_ln, scalar_ln, tensor_ln, xn_lo = normalised_columns(nc, mem, xn, xnT, tr_ps, sem)
        (wo_in, lora_in, w_in, bias_in, wo_hi, wo_lo, a_hi, a_lo, w_set, b_set, b_hi, b_lo, m_mm, w_add, w_hi, w_lo,
         o_t, g_done, g_hi, g_lo, p_mm, p_mask, x_done, z_mm, z_add, z_bias, stored) = [sem(n) for n in (
            "wo_in lora_in w_in bias_in wo_hi wo_lo a_hi a_lo w_set b_set b_hi b_lo m_mm w_add w_hi w_lo "
            "o_t g_done g_hi g_lo p_mm p_mask x_done z_mm z_add z_bias stored").split()]
        block = ctx.enter_context(nc.Block())

        @block.sync
        def _(sp):
            sp.dma_start(wo_raw[:], io["wo1_t"]).then_inc(wo_in, 16)
            sp.dma_start(bo[:], io["bo1"].rearrange("(p o) -> p o", o=1)).then_inc(wo_in, 16)
            sp.dma_start(a_raw[:], io["lora_a"].rearrange("(t p) d -> p t d", p=P)).then_inc(lora_in, 16)
            sp.dma_start(b_raw[:], io["lora_b"].rearrange("(t p) d -> p t d", p=P)).then_inc(lora_in, 16)
            sp.dma_start(cs[:], io["lora_cs"]).then_inc(lora_in, 16)
            sp.dma_start(w1[:], io["w1_t"].rearrange("(k p) n -> p k n", p=P)).then_inc(w_in, 16)
            sp.dma_start(bias[:], io["bias1"].rearrange("(o n) -> o n", o=1).to_broadcast([P, D])).then_inc(bias_in, 16)
            for b in range(B):
                sp.wait_ge(z_bias, b + 1)
                sp.dma_start(out[b], mem["x_acc"][:, b, :]).then_inc(stored, 16)
            sp.wait_ge(stored, 16 * B)

        @block.gpsimd
        def _(pool):
            pool_ln(pool)

        @block.scalar
        def _(act):
            act.wait_ge(wo_in, 32)
            nc.scalar.activation(wo_s[0][:], wo_raw[:], ACT.Copy).then_inc(wo_hi, 1)
            act.wait_ge(lora_in, 48)
            nc.scalar.activation(a_s[0][:], a_raw[:], ACT.Copy).then_inc(a_hi, 1)
            act.wait_ge(b_set, NE)
            nc.scalar.activation(b_s[0][:], b_raw[:], ACT.Copy).then_inc(b_hi, 1)

            def project(b):
                act.wait_ge(o_t, b + 1)
                if b >= 2:
                    act.wait_ge(g_lo, b - 1)
                nc.scalar.activation(gelu[:, b % 2, :], o_t_ps[b % 2][0:E1, :], ACT.Gelu).then_inc(g_done, 1)
                act.wait_ge(g_done, b + 1)
                if b >= 2:
                    act.wait_ge(p_mm, b - 1)
                nc.scalar.activation(gelu_s[0][:, b % 2, :], gelu[:, b % 2, :], ACT.Copy).then_inc(g_hi, 1)
            for b in range(B):
                project(b)
            for k in range(KT):
                act.wait_ge(w_add, k + 1)
                nc.scalar.activation(w1_s[0][:, k, :], w1[:, k, :], ACT.Copy).then_inc(w_hi, 1)
            scalar_ln(act)

        @block.vector
        def _(dve):
            dve.wait_ge(wo_hi, 1)
            nc.vector.tensor_tensor(wo_s[1][:], wo_raw[:], raw(wo_s[0][:]), ALU.subtract).then_inc(wo_lo, 1)
            dve.wait_ge(lora_in, 48)
            nc.vector.tensor_tensor(w_exp[:], cs[:, 0, :], cs[:, 1, :], ALU.mult).then_inc(w_set, 1)
            dve.wait_ge(w_set, 1)
            for t in range(NE):
                nc.vector.tensor_scalar(b_raw[:, t, :], b_raw[:, t, :], w_exp[:, t:t + 1], None, ALU.mult).then_inc(b_set, 1)
            dve.wait_ge(a_hi, 1)
            nc.vector.tensor_tensor(a_s[1][:], a_raw[:], raw(a_s[0][:]), ALU.subtract).then_inc(a_lo, 1)
            dve.wait_ge(b_hi, 1)
            nc.vector.tensor_tensor(b_s[1][:], b_raw[:], raw(b_s[0][:]), ALU.subtract).then_inc(b_lo, 1)
            dve.wait_ge(w_in, 16)
            for k in range(KT):
                dve.wait_ge(m_mm, k + 1)
                nc.vector.tensor_tensor(w1[:, k, :], w1[:, k, :], m_ps[k % 2][:], ALU.add).then_inc(w_add, 1)

            def lo(b):
                dve.wait_ge(g_hi, b + 1)
                nc.vector.tensor_tensor(gelu_s[1][:, b % 2, :], gelu[:, b % 2, :], raw(gelu_s[0][:, b % 2, :]), ALU.subtract).then_inc(g_lo, 1)

            def add(b):
                dve.wait_ge(p_mm, b + 1)
                if b >= 2:
                    dve.wait_ge(x_done, b - 1)
                nc.vector.scalar_tensor_tensor(masked[:, b % 2, :], y_ps[b % 2][:], bo[:, 0:1], mem["seen_all"][:, b, :], ALU.add, ALU.mult).then_inc(p_mask, 1)
                dve.wait_ge(p_mask, b + 1)
                nc.vector.tensor_tensor(mem["x_acc"][:, b, :], mem["x_acc"][:, b, :], masked[:, b % 2, :], ALU.add).then_inc(x_done, 1)
            lo(0)
            for b in range(1, B):
                lo(b)
                add(b - 1)
            add(B - 1)
            for k in range(KT):
                dve.wait_ge(w_hi, k + 1)
                nc.vector.tensor_tensor(w1_s[1][:, k, :], w1[:, k, :], raw(w1_s[0][:, k, :]), ALU.subtract).then_inc(w_lo, 1)
            dve.wait_ge(x_done, B)
            vector_ln(dve)
            dve.wait_ge(bias_in, 16)
            for b in range(B):
                dve.wait_ge(z_mm, b + 1)
                nc.vector.tensor_tensor(mem["x_acc"][:, b, :], mem["x_acc"][:, b, :], y_ps[b % 2][:], ALU.add).then_inc(z_add, 1)
                dve.wait_ge(z_add, b + 1)
                nc.vector.tensor_tensor(mem["x_acc"][:, b, :], mem["x_acc"][:, b, :], bias[:], ALU.add).then_inc(z_bias, 1)

        @block.tensor
        def _(pe):
            def turn(b):
                if b >= 2:
                    pe.wait_ge(g_done, b - 1)
                for p in range(NP):
                    last = nc.tensor.transpose(o_t_ps[b % 2][0:E1, p * P:(p + 1) * P],
                                               mem["o_all"][:, (b * NP + p) * H1:(b * NP + p + 1) * H1, :].rearrange("p h c -> p (h c)"),
                                               mem["ident"][:])
                last.then_inc(o_t, 1)

            def project(b):
                pe.wait_ge(g_lo, b + 1)
                if b >= 2:
                    pe.wait_ge(p_mask, b - 1)
                for m, (a, c) in enumerate(split_passes(wo_s[0], wo_s[1], gelu_s[0], gelu_s[1])):
                    last = nc.tensor.matmul(y_ps[b % 2][:], a[:], c[:, b % 2, :], start=(m == 0), stop=(m == 2))
                last.then_inc(p_mm, 1)

            turn(0)
            turn(1)
            pe.wait_ge(a_lo, 1)
            pe.wait_ge(b_lo, 1)
            for k in range(KT):
                if k >= 2:
                    pe.wait_ge(w_add, k - 1)
                n = 0
                for t in range(NE):
                    for a, c in split_passes(a_s[0], a_s[1], b_s[0], b_s[1]):
                        last = nc.tensor.matmul(m_ps[k % 2][:], a[:, t, k * P:(k + 1) * P], c[:, t, :], start=(n == 0), stop=(n == 3 * NE - 1))
                        n += 1
                last.then_inc(m_mm, 1)
            pe.wait_ge(wo_lo, 1)
            for b in range(B):
                if b >= 2:
                    turn(b)
                project(b)
            tensor_ln(pe)
            pe.wait_ge(w_lo, KT)
            for b in range(B):
                pe.wait_ge(xn_lo, b + 1)
                if b >= 2:
                    pe.wait_ge(z_add, b - 1)
                else:
                    pe.wait_ge(p_mask, B - 1 + b)
                n = 0
                for k in range(KT):
                    for a, c in split_passes(xnT[0], xnT[1], w1_s[0], w1_s[1]):
                        last = nc.tensor.matmul(y_ps[b % 2][:], a[:, k, b * S:(b + 1) * S], c[:, k, :], start=(n == 0), stop=(n == 3 * KT - 1))
                        n += 1
                last.then_inc(z_mm, 1)


def build(nc, io, out):
    with ExitStack() as ctx:
        sb = lambda name, shape, dt=F32: ctx.enter_context(nc.sbuf_tensor(name, shape, dt))
        mem = {
            "x_acc": sb("x_acc", [P, B, D]),
            "cos_k": sb("cos_k", [P, S]), "sin_k": sb("sin_k", [P, S]),
            "cos_q": sb("cos_q", [P, S]), "sin_q": sb("sin_q", [P, S]),
            "mask_bias": sb("mask_bias", [P, S]), "ident": sb("ident", [P, P]),
            "minus_half": sb("minus_half", [P, B]), "pick": sb("pick", [P, HB, P], F32R),
            "stats": sb("stats", [P, B, 6]), "mv": sb("mv", [P, B, 2]), "rstd": sb("rstd", [P, B]),
        }
        prepare(nc, io, mem)
        layer0_attention(nc, io, mem)
        layer0_ffn(nc, io, mem)
        mem["seen_all"] = sb("seen_all", [P, B, D])
        mem["o_all"] = sb("o_all", [P, B * NP * H1, DH1])
        layer1_attention(nc, io, mem)
        layer1_rest(nc, io, mem, out)


def score_rows():
    import numpy as np
    own = np.zeros((P, HG + 1), np.float32)
    for part in range(3):
        for h in range(HG):
            own[part * 32 + h * DH1:part * 32 + (h + 1) * DH1, h] = 1.0
    own[96, :] = 1.0
    own[96, HG] = NO_KEY
    return own


def rotary_tables():
    import numpy as np
    inv = (1.0 / (np.float32(10000.0) ** (np.arange(0, DH, 2, dtype=np.float32) / np.float32(DH)))).astype(np.float32)
    phase = (np.arange(S, dtype=np.float32)[:, None] * inv[None, :]).astype(np.float32)
    c, s = np.cos(phase).astype(np.float32).T, np.sin(phase).astype(np.float32).T
    return np.ascontiguousarray(np.concatenate([c, c])), np.ascontiguousarray(np.concatenate([-s, s]))


def kernel(**inputs):
    import numpy as np
    import concourse.bacc as bacc
    from concourse.bass_utils import run_bass_kernel_spmd as run

    nc = bacc.Bacc("TRN2", target_bir_lowering=False, num_devices=1)
    get = lambda n: np.ascontiguousarray(inputs[n])
    cos, sin = rotary_tables()
    bias = np.zeros((P, 4), np.float32)
    for n, name in enumerate(("L1_xattn_bq", "L1_xattn_bk")):
        for part in range(3):
            bias[part * 32:part * 32 + 32, 2 * n:2 * n + 2] = get(name).reshape(2, 32).T
    bias[96, 0:2] = 1.0
    arrays = {
        "x": get("x"),
        "ctx_t": np.ascontiguousarray(get("ctx_4096").reshape(B * S, D).T),
        "mask_t": np.ascontiguousarray(get("mask_1x1xSxS2_bk0").reshape(S, S).T),
        "cos": cos, "sin": sin,
        "gate_t": np.ascontiguousarray(get("L0_ffn_gate_t").T), "up_t": np.ascontiguousarray(get("L0_ffn_up_t").T),
        "down_t": np.ascontiguousarray(get("L0_ffn_down_t").T),
        "gu_s": np.ascontiguousarray(np.stack([get("L0_ffn_gate_s").reshape(NG, FG, P), get("L0_ffn_up_s").reshape(NG, FG, P)], 1)
                                     .reshape(NG * 2 * FG, P).T),
        "down_s": get("L0_ffn_down_s"),
        "ctx": get("ctx_4096"), "key_mask": get("mask_Bx1x4096_ff1"),
        "qk1_t": np.ascontiguousarray(np.stack([get("L1_xattn_Wq").T, get("L1_xattn_Wk").T], 1)),
        "wv1_t": np.ascontiguousarray(get("L1_xattn_Wv").T), "bv1": get("L1_xattn_bv"),
        "qk1_bias": np.ascontiguousarray(bias), "own": score_rows(),
        "wo1_t": np.ascontiguousarray(get("L1_xattn_Wo").T), "bo1": get("L1_xattn_bo"),
        "lora_a": get("L1_ffn_A").reshape(256, D), "lora_b": np.ascontiguousarray(get("L1_ffn_Bf").transpose(0, 2, 1)).reshape(256, D),
        "lora_cs": np.ascontiguousarray(np.stack([np.repeat(get("L1_ffn_coeffs"), 16).reshape(2, P).T,
                                                  np.repeat(get("L1_ffn_scales"), 16).reshape(2, P).T], 1)),
        "w1_t": np.ascontiguousarray(get("L1_ffn_W").T), "bias1": get("L1_ffn_bias"),
        "Wq0": get("L0_xattn_Wq"), "Wk0": get("L0_xattn_Wk"), "Wv0": get("L0_xattn_Wv"), "Wo0": get("L0_xattn_Wo"),
    }
    io = {n: nc.dram_tensor(f"in_{n}", a.shape, mybir.dt.from_np(a.dtype), kind="ExternalInput").ap()
          for n, a in arrays.items()}
    out = nc.dram_tensor("out", (B, S, D), F32, kind="ExternalOutput").ap()
    build(nc, io, out)
    r = run(nc, [{f"in_{n}": a for n, a in arrays.items()}], core_ids=[0])
    return r.results[0]["out"]
```

```python
from contextlib import ExitStack

import concourse.bass as bass
from concourse import mybir

F32 = mybir.dt.float32
F32R = mybir.dt.float32r
F16 = mybir.dt.float16
I32 = mybir.dt.int32
U8 = mybir.dt.uint8
ALU = mybir.AluOpType
ACT = mybir.ActivationFunctionType
AX = mybir.AxisListType

P = 128
B, S, D = 8, 128, 512
KT = D // P
NH, NKV = 32, 8
G = NH // NKV
DH = 128
HB = 4
HR = HB * S
TANH_SCALE = 0.08838834764831845 / 30.0
CAP = 30.0
EPS = 1e-5
BIG = 1e30


def raw(ap):
    return ap.bitcast(F32)


def stage_semaphores(nc, ctx, prefix):
    made = []

    def clear():
        nc.clear_and_free_semaphores(made)
        nc.all_engine_barrier(sem_only=True)

    ctx.callback(clear)

    def sem(name):
        made.append(nc.alloc_semaphore(prefix + name))
        return made[-1]

    return sem


def split_passes(hi_w, lo_w, hi_x, lo_x):
    return ((hi_w, lo_x), (lo_w, hi_x), (hi_w, hi_x))


def row_statistics(nc, mem, sems, ready):
    stat, aggr, eps_added, rstd_done = sems

    def vector(dve):
        for b in range(B):
            ready(dve, b)
            nc.vector.bn_stats(mem["stats"][:, b, :], mem["x_acc"][:, b, :]).then_inc(stat, 1)
        for b in range(B):
            dve.wait_ge(stat, b + 1)
            nc.vector.bn_aggr(mem["mv"][:, b, :], mem["stats"][:, b, :]).then_inc(aggr, 1)

    def pool(eng):
        eng.wait_ge(aggr, B)
        nc.gpsimd.tensor_scalar(mem["rstd"][:], mem["mv"][:, :, 1], EPS, None, ALU.add).then_inc(eps_added, 1)
        eng.wait_ge(eps_added, 1)
        nc.gpsimd.tensor_tensor(mem["rstd"][:], mem["rstd"][:], mem["minus_half"][:], ALU.pow).then_inc(rstd_done, 1)

    return vector, pool


def prepare(nc, io, mem):
    with ExitStack() as ctx:
        sb = lambda name, shape, dt: ctx.enter_context(nc.sbuf_tensor(name, shape, dt))
        sem = stage_semaphores(nc, ctx, "prep_")
        mask_keys = sb("mask_keys", [P, S], U8)
        allowed = sb("allowed", [P, S], F32)
        ones = sb("ones", [P, P], F32)
        keep = sb("keep", [P, S], F32)
        empty = sb("empty", [P, S], F32)
        count_ps = ctx.enter_context(nc.psum_tensor("count_ps", [P, S], F32))
        x_in, tab_in, mask_in = sem("x_in"), sem("tab_in"), sem("mask_in")
        consts, step, counted = sem("consts"), sem("step"), sem("counted")
        ln_sems = [sem(n) for n in ("stat", "aggr", "eps_added", "rstd_done")]
        ln_vector, ln_pool = row_statistics(nc, mem, ln_sems, lambda dve, b: dve.wait_ge(x_in, 16))
        block = ctx.enter_context(nc.Block())

        @block.sync
        def _(sp):
            sp.dma_start(mask_keys[:], io["mask_t"]).then_inc(mask_in, 16)
            sp.dma_start(mem["cos_k"][:], io["cos"]).then_inc(tab_in, 16)
            sp.dma_start(mem["sin_k"][:], io["sin"]).then_inc(tab_in, 16)
            sp.dma_start(mem["x_acc"][:], io["x"].rearrange("b s d -> s b d")).then_inc(x_in, 16)

        @block.gpsimd
        def _(pool):
            nc.gpsimd.memset(mem["ident"][:], 0.0).then_inc(consts, 1)
            nc.gpsimd.memset(ones[:], 1.0).then_inc(consts, 1)
            nc.gpsimd.memset(mem["minus_half"][:], -0.5).then_inc(consts, 1)
            nc.gpsimd.memset(raw(mem["pick"][:]), 0.0).then_inc(consts, 1)
            pool.wait_ge(consts, 4)
            nc.gpsimd.affine_select(out=mem["ident"][:], in_=mem["ident"][:], compare_op=ALU.not_equal,
                                    fill=1.0, base=0, pattern=[[-1, P]], channel_multiplier=1).then_inc(consts, 1)
            for b in range(HB):
                nc.gpsimd.memset(raw(mem["pick"][:, b, b:b + 1]), 1.0).then_inc(consts, 1)
            pool.wait_ge(consts, 5 + HB)
            ln_pool(pool)

        @block.tensor
        def _(pe):
            pe.wait_ge(consts, 2)
            pe.wait_ge(step, 1)
            nc.tensor.matmul(count_ps[:], ones[:], allowed[:], start=True, stop=True).then_inc(counted, 1)

        @block.vector
        def _(dve):
            dve.wait_ge(mask_in, 16)
            nc.vector.tensor_scalar(allowed[:], mask_keys[:], 0, None, ALU.not_equal).then_inc(step, 1)
            dve.wait_ge(counted, 1)
            nc.vector.tensor_scalar(keep[:], count_ps[:], 0.0, None, ALU.is_gt).then_inc(step, 1)
            nc.vector.tensor_scalar(empty[:], count_ps[:], 0.0, None, ALU.is_equal).then_inc(step, 1)
            dve.wait_ge(step, 3)
            nc.vector.tensor_tensor(allowed[:], allowed[:], empty[:], ALU.add).then_inc(step, 1)
            dve.wait_ge(step, 4)
            nc.vector.tensor_scalar(mem["mask_bias"][:], allowed[:], 1.0, BIG, ALU.subtract, ALU.mult).then_inc(step, 1)
            dve.wait_ge(consts, 5)
            nc.vector.tensor_scalar(mem["row"][:], mem["ident"][0:HB, 0:HB].unsqueeze(2).to_broadcast([HB, HB, P]), 1.0, None, ALU.mult).then_inc(step, 1)
            dve.wait_ge(tab_in, 32)
            nc.vector.tensor_tensor(mem["cos_q"][:], mem["cos_k"][:], keep[:], ALU.mult).then_inc(step, 1)
            nc.vector.tensor_tensor(mem["sin_q"][:], mem["sin_k"][:], keep[:], ALU.mult).then_inc(step, 1)
            ln_vector(dve)


def layer0_attention(nc, io, mem):
    RING = 4
    FILLS = 4 * (NKV + 1)
    USES = 3 + 2 * NKV
    with ExitStack() as ctx:
        sb = lambda name, shape, dt: ctx.enter_context(nc.sbuf_tensor(name, shape, dt))
        ps = lambda name, shape=[P, 512]: ctx.enter_context(nc.psum_tensor(name, shape, F32))
        sem = stage_semaphores(nc, ctx, "l0_")
        ring = sb("ring", [P, RING, 512], F32)
        raw_k = sb("raw_k", [P, KT, DH], F32)
        ctxT = [sb(f"ctxT_{n}", [P, KT, HR], F32R) for n in ("hi", "lo")]
        xnT = [sb(f"xnT_{n}", [P, KT, HR], F32R) for n in ("hi", "lo")]
        v_all = sb("v_all", [P, HB, NKV * DH], F32)
        wa = [sb(f"wa_{n}", [P, KT, 512], F32R) for n in ("hi", "lo")]
        wo = [sb(f"wo_{n}", [P, G, D], F32R) for n in ("hi", "lo")]
        wk = [sb(f"wk_{n}", [P, KT, DH], F32R) for n in ("hi", "lo")]
        kT = [sb(f"kT_{n}", [P, HR], F32R) for n in ("hi", "lo")]
        qT = [sb(f"qT_{n}", [P, G, HR], F32R) for n in ("hi", "lo")]
        vg = [sb(f"vg_{n}", [P, HB, DH], F32R) for n in ("hi", "lo")]
        oT = [sb(f"oT_{n}", [P, HB, G * S], F32R) for n in ("hi", "lo")]
        o_raw = sb("o_raw", [P, HB, G * S], F32)
        rinv = sb("rinv", [HB, G * S], F32)
        rinv_s = [sb(f"rinv_{n}", [HB, G * S], F32R) for n in ("hi", "lo")]
        prob = sb("prob", [P, 2, G * S], F32)
        pT = [sb(f"pT_{n}", [P, 2, G * S], F32R) for n in ("hi", "lo")]
        rope_a = sb("rope_a", [P, 2, HR], F32)
        rope_b = sb("rope_b", [P, 2, HR], F32)
        xn = o_raw

        proj_ps = [ps("proj0_ps"), ps("proj1_ps")]
        s_ps = [ps("s0_ps"), ps("s1_ps")]
        o_ps = ps("o_ps")
        sum_ps = ps("sum_ps")
        y_ps = [ps("y0_ps"), ps("y1_ps")]
        k_ps = y_ps[1]
        out_ps = [o_ps, proj_ps[1]]
        rinv_ps = [y_ps[0], y_ps[1], sum_ps, o_ps]

        ring_in = [sem(f"ring_in{i}") for i in range(RING)]
        (raw_k_in, ctx_hi, ctx_lo, wa_hi, wa_lo, wo_hi, wo_lo, xn_done, xn_tr, xn_hi, xn_lo,
         v_mm, v_out, k_mm, k_mul, k_full, k_hi, k_lo, wk_hi, wk_lo, vg_hi, vg_lo,
         q_mm, q_mul, q_shift, q_sin, q_full, q_hi, q_lo, s_mm, s_tanh, s_masked, p_exp, p_hi, p_lo,
         o_mm, sum_mm, o_out, inv_done, inv_hi, inv_lo, rinv_mm, o_norm, o_hi, o_lo, y_mm, y_add) = [
            sem(n) for n in (
                "raw_k_in ctx_hi ctx_lo wa_hi wa_lo wo_hi wo_lo xn_done xn_tr xn_hi xn_lo "
                "v_mm v_out k_mm k_mul k_full k_hi k_lo wk_hi wk_lo vg_hi vg_lo "
                "q_mm q_mul q_shift q_sin q_full q_hi q_lo s_mm s_tanh s_masked p_exp p_hi p_lo "
                "o_mm sum_mm o_out inv_done inv_hi inv_lo rinv_mm o_norm o_hi o_lo y_mm y_add").split()]

        half = ctx.enter_context(nc.Fori(0, B // HB))

        def once(n, per):
            return half * per + n

        def head(g, per, n):
            return half * (NKV * per) + g * per + n

        def fill(g, n):
            return half * FILLS + 4 * g + (4 + n)

        block = ctx.enter_context(nc.Block())

        def heads(eng, body):
            body(0, True, False)
            with eng.Fori(1, NKV - 1) as g:
                body(g, False, False)
            body(NKV - 1, False, True)

        wq_d = io["Wq0"].rearrange("(k p) n -> p k n", p=P)
        wk_d = io["Wk0"].rearrange("(k p) n -> p k n", p=P)
        wv_d = io["Wv0"].rearrange("(k p) n -> p k n", p=P)
        wo_d = io["Wo0"].rearrange("(k p) n -> p k n", p=P)
        ctx_d = io["ctx_t"].rearrange("(k p) n -> p k n", p=P)

        @block.sync
        def _(sp):
            def piece(src, slot, before=None, done=None):
                if before is not None:
                    sp.wait_ge(before[0], done)
                    sp.wait_ge(before[1], done)
                sp.dma_start(ring[:, slot:slot + 1, :], src).then_inc(ring_in[slot], 16)

            in_ctx, in_wa, in_wo = (ctx_hi, ctx_lo), (wa_hi, wa_lo), (wo_hi, wo_lo)
            for j in range(4):
                piece(ctx_d[:, j:j + 1, bass.ds(half * HR, HR)], j)
            for j in range(4):
                piece(wv_d[:, j:j + 1, 0:512], j, in_ctx, once(j + 1, 4))
            sp.dma_start(raw_k[:], wk_d[:, :, 0:DH]).then_inc(raw_k_in, 16)
            for j in range(4):
                piece(wv_d[:, j:j + 1, 512:1024], j, in_wa, once(j + 1, FILLS))
            for j in range(4):
                piece(wq_d[:, j:j + 1, 0:512], j, in_wo, once(j + 1, FILLS))

            def body(g, first, last):
                if not last:
                    sp.wait_ge(wk_hi, head(g, 1, 1))
                    sp.wait_ge(wk_lo, head(g, 1, 1))
                    sp.dma_start(raw_k[:], wk_d[:, :, bass.ds(g * DH + DH, DH)]).then_inc(raw_k_in, 16)
                    for j in range(4):
                        piece(wq_d[:, j:j + 1, bass.ds(g * 512 + 512, 512)], j, *((in_wa, fill(0, j + 1)) if first else (in_wo, fill(g - 1, j + 1))))
                for j in range(4):
                    piece(wo_d[:, bass.ds(g * G + j, 1), :], j, *((in_wo, fill(g - 1, j + 1)) if last else (in_wa, fill(g + 1, j + 1))))

            heads(sp, body)

        def landed(nth, g=0):
            return half * (16 * USES) + g * 32 + nth * 16

        def landed_wo(g, last):
            return landed(5 if last else 6, g)

        @block.gpsimd
        def _(pool):
            def wq_lo(g, j):
                pool.wait_ge(ring_in[j], landed(3, g))
                pool.wait_ge(wa_hi, fill(g, j + 1))
                nc.gpsimd.tensor_tensor(wa[1][:, j, :], ring[:, j, :], raw(wa[0][:, j, :]), ALU.subtract).then_inc(wa_lo, 1)

            def body(g, first, last):
                for h in range(G):
                    pool.wait_ge(q_shift, head(g, G, h + 1))
                    nc.gpsimd.tensor_tensor(rope_b[:, h % 2, :].rearrange("p (b t) -> p b t", b=HB),
                                            rope_b[:, h % 2, :].rearrange("p (b t) -> p b t", b=HB),
                                            mem["sin_q"][:].unsqueeze(1).to_broadcast([P, HB, S]), ALU.mult).then_inc(q_sin, 1)
                    pool.wait_ge(q_sin, head(g, G, h + 1))
                    nc.gpsimd.tensor_tensor(rope_a[:, h % 2, :], rope_a[:, h % 2, :], rope_b[:, h % 2, :], ALU.add).then_inc(q_full, 1)
                if not last:
                    wq_lo(g + 1, 0)
                for b in range(HB):
                    pool.wait_ge(s_tanh, head(g, HB, b + 1))
                    nc.gpsimd.tensor_tensor(prob[:, b % 2, :].rearrange("p (h t) -> p h t", h=G),
                                            prob[:, b % 2, :].rearrange("p (h t) -> p h t", h=G),
                                            mem["mask_bias"][:].unsqueeze(1).to_broadcast([P, G, S]), ALU.add).then_inc(s_masked, 1)
                    if not last and b == 1:
                        wq_lo(g + 1, 1)
                if not last:
                    wq_lo(g + 1, 2)
                    wq_lo(g + 1, 3)
                for j in range(4):
                    pool.wait_ge(ring_in[j], landed_wo(g, last))
                    pool.wait_ge(wo_hi, fill(g, j + 1))
                    nc.gpsimd.tensor_tensor(wo[1][:, j, :], ring[:, j, :], raw(wo[0][:, j, :]), ALU.subtract).then_inc(wo_lo, 1)

            heads(pool, body)

        @block.scalar
        def _(act):
            def hi_of(dst, done, j, use, free=None):
                if free is not None:
                    act.wait_ge(*free)
                act.wait_ge(ring_in[j], use)
                nc.scalar.activation(dst[0][:, j, :], ring[:, j, :], ACT.Copy).then_inc(done, 1)

            for b in range(HB):
                act.wait_ge(xn_tr, once(b + 1, HB))
                nc.scalar.activation(xnT[0][:, :, b * S:(b + 1) * S], s_ps[b % 2][:].rearrange("p (k s) -> p k s", k=KT),
                                     ACT.Copy).then_inc(xn_hi, 1)
            for j in range(4):
                hi_of(ctxT, ctx_hi, j, landed(1))
            for j in range(4):
                hi_of(wa, wa_hi, j, landed(2))
            for j in range(4):
                hi_of(wo, wo_hi, j, landed(3))

            def v_from(c, b):
                act.wait_ge(v_mm, once(4 * c + b + 1, 8))
                nc.scalar.activation(v_all[:, b, c * 512:(c + 1) * 512], proj_ps[b % 2][:], ACT.Copy).then_inc(v_out, 1)

            def wk_split(g):
                if not (isinstance(g, int) and g == 0):
                    act.wait_ge(k_mm, head(g, 1, 0))
                act.wait_ge(raw_k_in, head(g, 16, 16))
                nc.scalar.activation(wk[0][:], raw_k[:], ACT.Copy).then_inc(wk_hi, 1)

            wk_split(0)
            for b in range(HB):
                v_from(0, b)
            for j in range(4):
                hi_of(wa, wa_hi, j, landed(4), (v_mm, once(4, 8)))
            for b in range(HB):
                v_from(1, b)

            def keys_hi(g):
                act.wait_ge(k_full, head(g, 1, 1))
                if not (isinstance(g, int) and g == 0):
                    act.wait_ge(s_mm, head(g, HB, 0))
                nc.scalar.activation(kT[0][:], rope_a[:, 1, :], ACT.Copy).then_inc(k_hi, 1)

            keys_hi(0)

            def inverse_hi(g):
                act.wait_ge(inv_done, head(g, 1, 1))
                nc.scalar.activation(rinv_s[0][:], rinv[:], ACT.Copy).then_inc(inv_hi, 1)

            def norm_hi(g, b):
                act.wait_ge(o_norm, head(g, HB, b + 1))
                nc.scalar.activation(oT[0][:, b, :], o_raw[:, b, :], ACT.Copy).then_inc(o_hi, 1)

            def body(g, first, last):
                def queries_hi(h):
                    act.wait_ge(q_full, head(g, G, h + 1))
                    nc.scalar.activation(qT[0][:, h, :], rope_a[:, h % 2, :], ACT.Copy).then_inc(q_hi, 1)

                def shift(h):
                    act.wait_ge(q_mul, head(g, G, h + 1))
                    nc.scalar.activation(rope_b[0:64, h % 2, :], proj_ps[h % 2][64:128, :], ACT.Copy)
                    nc.scalar.activation(rope_b[64:128, h % 2, :], proj_ps[h % 2][0:64, :], ACT.Copy).then_inc(q_shift, 1)

                shift(0)
                if not first:
                    inverse_hi(g - 1)
                shift(1)
                queries_hi(0)
                shift(2)
                queries_hi(1)
                if not first:
                    norm_hi(g - 1, 0)
                queries_hi(2)
                if not first:
                    norm_hi(g - 1, 1)
                shift(3)
                queries_hi(3)
                if not first:
                    norm_hi(g - 1, 2)
                    norm_hi(g - 1, 3)

                def wq_hi(j):
                    if not last:
                        hi_of(wa, wa_hi, j, landed(3, g + 1), (q_mm, head(g, G, G)))

                if not last:
                    wk_split(g + 1)
                wq_hi(0)
                wq_hi(1)

                def tanh(b):
                    act.wait_ge(s_mm, head(g, HB, b + 1))
                    if not (first and b < 2):
                        act.wait_ge(p_lo, head(g, HB, b - 1))
                    nc.scalar.activation(prob[:, b % 2, :], s_ps[b % 2][:], ACT.Tanh, scale=TANH_SCALE).then_inc(s_tanh, 1)

                def exp(b):
                    act.wait_ge(s_masked, head(g, HB, b + 1))
                    nc.scalar.activation(prob[:, b % 2, :], prob[:, b % 2, :], ACT.Exp, scale=CAP).then_inc(p_exp, 1)
                    act.wait_ge(p_exp, head(g, HB, b + 1))
                    if not (first and b < 2):
                        act.wait_ge(o_mm, head(g, HB, b - 1))
                    nc.scalar.activation(pT[0][:, b % 2, :], prob[:, b % 2, :], ACT.Copy).then_inc(p_hi, 1)

                def out(b):
                    act.wait_ge(o_mm, head(g, HB, b + 1))
                    if not first:
                        act.wait_ge(o_lo, head(g, HB, b + 1 - HB))
                    nc.scalar.activation(o_raw[:, b, :], out_ps[b % 2][:], ACT.Copy).then_inc(o_out, 1)

                def split_wo(j):
                    hi_of(wo, wo_hi, j, landed_wo(g, last), (v_mm, once(8, 8)) if first else (y_mm, head(g, HB, 0)))

                tanh(0)
                tanh(1)
                exp(0)
                exp(1)
                wq_hi(2)
                wq_hi(3)
                tanh(2)
                tanh(3)
                exp(2)
                out(0)
                exp(3)
                out(1)
                split_wo(0)
                split_wo(1)
                if not last:
                    keys_hi(g + 1)
                split_wo(2)
                split_wo(3)
                out(2)
                out(3)

            heads(act, body)
            inverse_hi(NKV - 1)
            for b in range(HB):
                norm_hi(NKV - 1, b)

        @block.vector
        def _(dve):
            for b in range(HB):
                nc.vector.tensor_scalar(xn[:, b:b + 1, :], mem["x_acc"][:, bass.ds(half * HB + b, 1), :],
                                        mem["mv"][:].rearrange("p b s -> p (b s)")[:, bass.ds((half * HB + b) * 2, 1)],
                                        mem["rstd"][:, bass.ds(half * HB + b, 1)], ALU.subtract, ALU.mult).then_inc(xn_done, 1)
            for b in range(HB):
                dve.wait_ge(xn_hi, once(b + 1, HB))
                nc.vector.tensor_tensor(xnT[1][:, :, b * S:(b + 1) * S], s_ps[b % 2][:].rearrange("p (k s) -> p k s", k=KT),
                                        raw(xnT[0][:, :, b * S:(b + 1) * S]), ALU.subtract).then_inc(xn_lo, 1)

            def wk_lo_of(g):
                dve.wait_ge(wk_hi, head(g, 1, 1))
                nc.vector.tensor_tensor(wk[1][:], raw_k[:], raw(wk[0][:]), ALU.subtract).then_inc(wk_lo, 1)

            def lo_of(dst, hi, done, j, use, count):
                dve.wait_ge(ring_in[j], use)
                dve.wait_ge(hi, count)
                nc.vector.tensor_tensor(dst[1][:, j, :], ring[:, j, :], raw(dst[0][:, j, :]), ALU.subtract).then_inc(done, 1)

            for j in range(4):
                lo_of(ctxT, ctx_hi, ctx_lo, j, landed(1), once(j + 1, 4))
            for j in range(4):
                lo_of(wa, wa_hi, wa_lo, j, landed(2), once(j + 1, FILLS))
            for j in range(4):
                lo_of(wo, wo_hi, wo_lo, j, landed(3), once(j + 1, FILLS))
            wk_lo_of(0)
            for j in range(4):
                lo_of(wa, wa_hi, wa_lo, j, landed(4), fill(0, j + 1))

            def reciprocal(g):
                dve.wait_ge(sum_mm, head(g, 1, 1))
                nc.vector.reciprocal(rinv[:], sum_ps[0:HB, :]).then_inc(inv_done, 1)

            def inverse_lo(g):
                dve.wait_ge(inv_hi, head(g, 1, 1))
                nc.vector.tensor_tensor(rinv_s[1][:], rinv[:], raw(rinv_s[0][:]), ALU.subtract).then_inc(inv_lo, 1)

            def rotary(slot, src, cos, sin, done):
                a = rope_a[:, slot, :].rearrange("p (b t) -> p b t", b=HB)
                r = rope_b[:, slot, :].rearrange("p (b t) -> p b t", b=HB)
                s = src[:].rearrange("p (b t) -> p b t", b=HB)
                wide = lambda t, lo, hi: t[lo:hi, :].unsqueeze(1).to_broadcast([hi - lo, HB, S])
                nc.vector.tensor_tensor(a, s, wide(cos, 0, P), ALU.mult)
                nc.vector.tensor_tensor(r[0:64], s[64:128], wide(sin, 0, 64), ALU.mult)
                nc.vector.tensor_tensor(r[64:128], s[0:64], wide(sin, 64, 128), ALU.mult).then_inc(done, 1)

            def cosine(h):
                nc.vector.tensor_tensor(rope_a[:, h % 2, :].rearrange("p (b t) -> p b t", b=HB),
                                        proj_ps[h % 2][:].rearrange("p (b t) -> p b t", b=HB),
                                        mem["cos_q"][:].unsqueeze(1).to_broadcast([P, HB, S]), ALU.mult).then_inc(q_mul, 1)

            def norm(g, b):
                dve.wait_ge(rinv_mm, head(g, HB, b + 1))
                dve.wait_ge(o_out, head(g, HB, b + 1))
                nc.vector.tensor_tensor(o_raw[:, b, :], o_raw[:, b, :], rinv_ps[b][:], ALU.mult).then_inc(o_norm, 1)

            def norm_lo(g, b):
                dve.wait_ge(o_hi, head(g, HB, b + 1))
                nc.vector.tensor_tensor(oT[1][:, b, :], o_raw[:, b, :], raw(oT[0][:, b, :]), ALU.subtract).then_inc(o_lo, 1)

            def add_y(g, b):
                dve.wait_ge(y_mm, head(g, HB, b + 1))
                nc.vector.tensor_tensor(mem["x_acc"][:, bass.ds(half * HB + b, 1), :], mem["x_acc"][:, bass.ds(half * HB + b, 1), :],
                                        y_ps[b % 2][:].unsqueeze(1), ALU.add).then_inc(y_add, 1)

            def keys(g):
                dve.wait_ge(k_mm, head(g, 1, 1))
                if not (isinstance(g, int) and g == 0):
                    dve.wait_ge(q_lo, head(g, G, 0))
                rotary(1, k_ps, mem["cos_k"], mem["sin_k"], k_mul)

            def keys_add(g):
                dve.wait_ge(k_mul, head(g, 1, 1))
                nc.vector.tensor_tensor(rope_a[:, 1, :], rope_a[:, 1, :], rope_b[:, 1, :], ALU.add).then_inc(k_full, 1)

            def keys_lo(g):
                dve.wait_ge(k_hi, head(g, 1, 1))
                nc.vector.tensor_tensor(kT[1][:], rope_a[:, 1, :], raw(kT[0][:]), ALU.subtract).then_inc(k_lo, 1)

            keys(0)
            keys_add(0)
            keys_lo(0)

            def body(g, first, last):
                def queries(h):
                    dve.wait_ge(q_mm, head(g, G, h + 1))
                    if h >= 2:
                        dve.wait_ge(q_lo, head(g, G, h - 1))
                    elif h == 1:
                        dve.wait_ge(k_lo, head(g, 1, 1))
                    cosine(h)

                def queries_lo(h):
                    dve.wait_ge(q_hi, head(g, G, h + 1))
                    nc.vector.tensor_tensor(qT[1][:, h, :], rope_a[:, h % 2, :], raw(qT[0][:, h, :]), ALU.subtract).then_inc(q_lo, 1)

                def weights_lo(b):
                    dve.wait_ge(p_hi, head(g, HB, b + 1))
                    nc.vector.tensor_tensor(pT[1][:, b % 2, :], prob[:, b % 2, :], raw(pT[0][:, b % 2, :]), ALU.subtract).then_inc(p_lo, 1)

                if not first:
                    reciprocal(g - 1)
                queries(0)
                if not first:
                    dve.wait_ge(o_mm, head(g, HB, 0))
                else:
                    dve.wait_ge(v_out, once(8, 8))
                nc.vector.tensor_scalar(vg[0][:], v_all[:, :, bass.ds(g * DH, DH)], 1.0, None, ALU.mult).then_inc(vg_hi, 1)
                queries(1)
                if not first:
                    inverse_lo(g - 1)
                queries_lo(0)
                queries(2)
                queries_lo(1)
                if not first:
                    norm(g - 1, 0)
                    norm(g - 1, 1)
                    norm_lo(g - 1, 0)
                queries(3)
                queries_lo(2)
                if not first:
                    norm(g - 1, 2)
                    norm_lo(g - 1, 1)
                    norm(g - 1, 3)
                queries_lo(3)
                if not first:
                    norm_lo(g - 1, 2)
                    norm_lo(g - 1, 3)
                dve.wait_ge(vg_hi, head(g, 1, 1))
                nc.vector.tensor_tensor(vg[1][:], v_all[:, :, bass.ds(g * DH, DH)], raw(vg[0][:]), ALU.subtract).then_inc(vg_lo, 1)
                if not last:
                    wk_lo_of(g + 1)
                if not first:
                    add_y(g - 1, 0)
                    add_y(g - 1, 1)
                weights_lo(0)
                weights_lo(1)
                if not first:
                    add_y(g - 1, 2)
                    add_y(g - 1, 3)
                weights_lo(2)
                weights_lo(3)
                if not last:
                    keys(g + 1)
                if not last:
                    keys_add(g + 1)
                if not last:
                    keys_lo(g + 1)

            heads(dve, body)
            g = NKV - 1
            reciprocal(g)
            inverse_lo(g)
            for b in range(HB):
                norm(g, b)
            for b in range(HB):
                norm_lo(g, b)
            for b in range(HB):
                add_y(g, b)

        @block.tensor
        def _(pe):
            def product(out, w, x, wsl, xsl):
                n = 0
                for k in range(KT):
                    for a, c in split_passes(w[0], w[1], x[0], x[1]):
                        last = nc.tensor.matmul(out, wsl(a, k), xsl(c, k), start=(n == 0), stop=(n == 3 * KT - 1))
                        n += 1
                return last

            for b in range(HB):
                pe.wait_ge(xn_done, once(b + 1, HB))
                if b >= 2:
                    pe.wait_ge(xn_lo, once(b - 1, HB))
                for k in range(KT):
                    last = nc.tensor.transpose(s_ps[b % 2][:, k * S:(k + 1) * S], xn[:, b, k * P:(k + 1) * P], mem["ident"][:])
                last.then_inc(xn_tr, 1)
            for c in range(2):
                pe.wait_ge((wa_hi, wo_hi)[c], once(4, FILLS))
                pe.wait_ge((wa_lo, wo_lo)[c], once(4, FILLS))
                for b in range(HB):
                    if 4 * c + b >= 2:
                        pe.wait_ge(v_out, once(4 * c + b - 1, 8))
                    product(proj_ps[b % 2][:], ctxT, (wa, wo)[c], lambda a, k: a[:, k, b * S:(b + 1) * S], lambda a, k: a[:, k, :]).then_inc(v_mm, 1)

            def y_of(g, b, first, last):
                pe.wait_ge(o_lo, head(g, HB, b + 1))
                if b == 0:
                    pe.wait_ge(wo_hi, fill(g, 4))
                    pe.wait_ge(wo_lo, fill(g, 4))
                if b >= 2:
                    pe.wait_ge(y_add, head(g, HB, b - 1))
                n = 0
                for h in range(G):
                    for a, c in split_passes(oT[0], oT[1], wo[0], wo[1]):
                        last_mm = nc.tensor.matmul(y_ps[b % 2][:], a[:, b, h * S:(h + 1) * S], c[:, h, :],
                                                   start=(n == 0), stop=(n == 3 * G - 1))
                        n += 1
                last_mm.then_inc(y_mm, 1)

            def keys(g):
                pe.wait_ge(wk_lo, head(g, 1, 1))
                if not (isinstance(g, int) and g <= 1):
                    pe.wait_ge(y_add, head(g - 1, HB, 0))
                product(k_ps[:], wk, ctxT, lambda a, k: a[:, k, :], lambda a, k: a[:, k, :]).then_inc(k_mm, 1)

            def inverses(g):
                pe.wait_ge(inv_lo, head(g, 1, 1))
                pe.wait_ge(o_out, head(g, HB, HB))
                if not (isinstance(g, int) and g == NKV - 1):
                    pe.wait_ge(k_mul, head(g + 1, 1, 1))
                for b in range(HB):
                    for n, part in enumerate((rinv_s[1], rinv_s[0])):
                        last = nc.tensor.matmul(rinv_ps[b][:], mem["row"][:, b, :], part[:], start=(n == 0), stop=(n == 1))
                    last.then_inc(rinv_mm, 1)

            keys(0)
            pe.wait_ge(xn_lo, once(HB, HB))

            def body(g, first, last):
                pe.wait_ge(wa_hi, fill(g, 4))
                pe.wait_ge(wa_lo, fill(g, 4))
                for h in range(G):
                    if h == 3 and not first:
                        inverses(g - 1)
                    if h >= 2 or not first:
                        pe.wait_ge(q_shift, head(g, G, h - 1))
                        if h == 1:
                            pe.wait_ge(o_out, head(g, HB, 0))
                    else:
                        pe.wait_ge(v_out, once(7 + h, 8))
                    product(proj_ps[h % 2][:], wa, xnT, lambda a, k: a[:, k, h * DH:(h + 1) * DH], lambda a, k: a[:, k, :]).then_inc(q_mm, 1)

                def scores(b):
                    if b == 0:
                        pe.wait_ge(k_lo, head(g, 1, 1))
                        pe.wait_ge(q_lo, head(g, G, G))
                    if b >= 2 or not first:
                        pe.wait_ge(s_tanh, head(g, HB, b - 1))
                    for n, (a, c) in enumerate(split_passes(kT[0], kT[1], qT[0], qT[1])):
                        last = nc.tensor.matmul(s_ps[b % 2][:], a[:, b * S:(b + 1) * S], c[:, :, b * S:(b + 1) * S],
                                                start=(n == 0), stop=(n == 2))
                    last.then_inc(s_mm, 1)

                def outputs(b):
                    pe.wait_ge(p_lo, head(g, HB, b + 1))
                    if b == 0:
                        pe.wait_ge(vg_lo, head(g, 1, 1))
                    if b == 1:
                        pe.wait_ge(q_shift, head(g, G, G))
                    elif b >= 2:
                        pe.wait_ge(o_out, head(g, HB, b - 1))
                    for n, part in enumerate((pT[1], pT[0])):
                        last = nc.tensor.matmul(sum_ps[:], mem["pick"][:, b, :], part[:, b % 2, :],
                                                start=(b == 0 and n == 0), stop=(b == HB - 1 and n == 1))
                    if b == HB - 1:
                        last.then_inc(sum_mm, 1)
                    for n, (a, c) in enumerate(split_passes(vg[0], vg[1], pT[0], pT[1])):
                        last = nc.tensor.matmul(out_ps[b % 2][:], a[:, b, :], c[:, b % 2, :], start=(n == 0), stop=(n == 2))
                    last.then_inc(o_mm, 1)

                if not first:
                    y_of(g - 1, 0, False, last)
                    y_of(g - 1, 1, False, last)
                scores(0)
                scores(1)
                if not first:
                    y_of(g - 1, 2, False, last)
                scores(2)
                scores(3)
                if not first:
                    y_of(g - 1, 3, False, last)
                outputs(0)
                outputs(1)
                if not last:
                    keys(g + 1)
                outputs(2)
                outputs(3)

            heads(pe, body)
            pe.wait_ge(y_add, once(HB * (NKV - 1), HB * NKV))
            inverses(NKV - 1)
            for b in range(HB):
                y_of(NKV - 1, b, False, True)


def normalised_columns(nc, mem, xn, xnT, banks, sem):
    ln_sems = [sem(n) for n in ("stat", "aggr", "eps_added", "rstd_done")]
    xn_done, xn_tr, xn_hi, xn_lo = (sem(n) for n in ("xn_done", "xn_tr", "xn_hi", "xn_lo"))
    ln_vector, ln_pool = row_statistics(nc, mem, ln_sems, lambda dve, b: None)
    columns = lambda part, b: part[:, :, b * S:(b + 1) * S]
    bank = lambda b: banks[b % 2][:].rearrange("p (k s) -> p k s", k=KT)

    def vector(dve):
        ln_vector(dve)
        dve.wait_ge(ln_sems[3], 1)

        def lo(b):
            dve.wait_ge(xn_hi, b + 1)
            nc.vector.tensor_tensor(columns(xnT[1], b), bank(b), raw(columns(xnT[0], b)), ALU.subtract).then_inc(xn_lo, 1)

        for b in range(B):
            nc.vector.tensor_scalar(xn[:, b, :], mem["x_acc"][:, b, :], mem["mv"][:, b, 0:1], mem["rstd"][:, b:b + 1],
                                    ALU.subtract, ALU.mult).then_inc(xn_done, 1)
            if b >= 2:
                lo(b - 2)
        lo(B - 2)
        lo(B - 1)

    def scalar(act):
        for b in range(B):
            act.wait_ge(xn_tr, b + 1)
            nc.scalar.activation(columns(xnT[0], b), bank(b), ACT.Copy).then_inc(xn_hi, 1)

    def tensor(pe):
        for b in range(B):
            pe.wait_ge(xn_done, b + 1)
            if b >= 2:
                pe.wait_ge(xn_lo, b - 1)
            for k in range(KT):
                last = nc.tensor.transpose(banks[b % 2][:, k * S:(k + 1) * S], xn[:, b, k * P:(k + 1) * P], mem["ident"][:])
            last.then_inc(xn_tr, 1)

    return vector, ln_pool, scalar, tensor, xn_lo


FF = 1792
FG = 2
NG = FF // (P * FG)


def layer0_ffn(nc, io, mem):
    with ExitStack() as ctx:
        sb = lambda name, shape, dt=F32: ctx.enter_context(nc.sbuf_tensor(f"ffn_{name}", shape, dt))
        ps = lambda name: ctx.enter_context(nc.psum_tensor(f"ffn_{name}", [P, 512], F32))
        sem = stage_semaphores(nc, ctx, "ffn_")
        FW = FG * P
        xnT = [sb(f"xnT_{n}", [P, KT, B * S], F32R) for n in ("hi", "lo")]
        w_raw = {"gate": sb("gate_raw", [P, KT, FW], I32), "up": sb("up_raw", [P, KT, FW], I32), "down": sb("down_raw", [P, FG, D], I32)}
        w = {n: [sb(f"{n}_{part}", list(w_raw[n].shape), F32R) for part in ("hi", "lo")] for n in w_raw}
        y_acc = sb("y_acc", [P, B, D])
        hT = [sb(f"hT_{n}", [P, FG, B * S], F32R) for n in ("hi", "lo")]
        silu = sb("silu", [P, 2, HR])
        hidden = sb("hidden", [P, 2, HR])
        scales = sb("scales", [P, NG, 2 * FG])
        now = sb("now", [P, 2 * FG])
        down_s = sb("down_s", [P, D])
        xn = y_acc
        gate_ps, up_ps, y_ps = ([ps(f"{n}{i}_ps") for i in range(2)] for n in ("gate", "up", "y"))
        vector_ln, pool_ln, scalar_ln, tensor_ln, xn_lo = normalised_columns(nc, mem, xn, xnT, y_ps, sem)
        w_in = {n: sem(f"{n}_in") for n in w}
        w_hi = {n: sem(f"{n}_hi") for n in w}
        w_lo = {n: sem(f"{n}_lo") for n in w}
        (scales_in, down_s_in, now_set, gu_mm, silu_done, h_full, h_hi, h_lo, y_mm, y_add, y_scaled, cleared) = [sem(n) for n in (
            "scales_in down_s_in now_set gu_mm silu_done h_full h_hi h_lo y_mm y_add y_scaled cleared").split()]
        block = ctx.enter_context(nc.Block())

        def groups(eng, body):
            body(0, True, False)
            with eng.Fori(1, NG - 1) as i:
                body(i, False, False)
            body(NG - 1, False, True)

        gate_d = io["gate_t"].rearrange("(k p) f -> p k f", p=P)
        up_d = io["up_t"].rearrange("(k p) f -> p k f", p=P)
        down_d = io["down_t"].rearrange("(k p) n -> p k n", p=P)

        @block.sync
        def _(sp):
            sp.dma_start(w_raw["gate"][:], gate_d[:, :, 0:FW]).then_inc(w_in["gate"], 16)
            sp.dma_start(w_raw["up"][:], up_d[:, :, 0:FW]).then_inc(w_in["up"], 16)
            sp.dma_start(w_raw["down"][:], down_d[:, 0:FG, :]).then_inc(w_in["down"], 16)
            sp.dma_start(scales[:], io["gu_s"].rearrange("p (i s) -> p i s", i=NG)).then_inc(scales_in, 16)
            sp.dma_start(down_s[:], io["down_s"].rearrange("(o n) -> o n", o=1).to_broadcast([P, D])).then_inc(down_s_in, 16)
            with sp.Fori(0, NG - 1) as i:
                for name, src in (("gate", gate_d[:, :, bass.ds(i * FW + FW, FW)]), ("up", up_d[:, :, bass.ds(i * FW + FW, FW)]),
                                  ("down", down_d[:, bass.ds(i * FG + FG, FG), :])):
                    sp.wait_ge(w_lo[name], i + 1)
                    sp.dma_start(w_raw[name][:], src).then_inc(w_in[name], 16)

        @block.gpsimd
        def _(pool):
            pool_ln(pool)
            pool.wait_ge(xn_lo, B)
            nc.gpsimd.memset(y_acc[:], 0.0).then_inc(cleared, 1)

        @block.scalar
        def _(act):
            def split(name, i):
                act.wait_ge(w_in[name], i * 16 + 16)
                nc.scalar.activation(w[name][0][:], w_raw[name][:], ACT.Copy).then_inc(w_hi[name], 1)

            split("gate", 0)
            split("up", 0)
            split("down", 0)
            scalar_ln(act)

            def body(i, first, last):
                act.wait_ge(now_set, i + 1)

                def gate(n):
                    act.wait_ge(gu_mm, i * 4 + (n + 1))
                    if n >= 2 or not first:
                        act.wait_ge(h_full, i * 4 + (n - 1))
                    t = n % 2
                    nc.scalar.activation(silu[:, n % 2, :], gate_ps[n % 2][:], ACT.Silu, scale=now[:, t:t + 1]).then_inc(silu_done, 1)

                def hi(n):
                    r, t = n // 2, n % 2
                    act.wait_ge(h_full, i * 4 + (n + 1))
                    if not first:
                        act.wait_ge(y_mm, i * B + (HB * (r + 1) - B))
                    nc.scalar.activation(hT[0][:, t, r * HR:(r + 1) * HR], hidden[:, n % 2, :], ACT.Copy).then_inc(h_hi, 1)

                gate(0)
                gate(1)
                hi(0)
                gate(2)
                hi(1)
                gate(3)
                hi(2)
                hi(3)
                if not last:
                    act.wait_ge(gu_mm, i * 4 + 4)
                    split("gate", i + 1)
                    split("up", i + 1)
                    act.wait_ge(y_mm, i * B + B)
                    split("down", i + 1)
            groups(act, body)

        @block.vector
        def _(dve):
            def split(name, i):
                dve.wait_ge(w_hi[name], i + 1)
                nc.vector.tensor_tensor(w[name][1][:], w_raw[name][:], raw(w[name][0][:]), ALU.subtract).then_inc(w_lo[name], 1)

            vector_ln(dve)
            split("gate", 0)
            split("up", 0)
            split("down", 0)
            dve.wait_ge(scales_in, 16)

            def body(i, first, last):
                nc.vector.tensor_scalar(now[:].unsqueeze(1), scales[:, bass.ds(i, 1), :] if not isinstance(i, int) else scales[:, i:i + 1, :],
                                        1.0, None, ALU.mult).then_inc(now_set, 1)
                dve.wait_ge(now_set, i + 1)

                def product(n):
                    dve.wait_ge(silu_done, i * 4 + (n + 1))
                    if n >= 2 or not first:
                        dve.wait_ge(h_lo, i * 4 + (n - 1))
                    t = n % 2
                    nc.vector.scalar_tensor_tensor(hidden[:, n % 2, :], up_ps[n % 2][:], now[:, FG + t:FG + t + 1], silu[:, n % 2, :],
                                                   ALU.mult, ALU.mult).then_inc(h_full, 1)

                def lo(n):
                    r, t = n // 2, n % 2
                    dve.wait_ge(h_hi, i * 4 + (n + 1))
                    nc.vector.tensor_tensor(hT[1][:, t, r * HR:(r + 1) * HR], hidden[:, n % 2, :],
                                            raw(hT[0][:, t, r * HR:(r + 1) * HR]), ALU.subtract).then_inc(h_lo, 1)

                product(0)
                product(1)
                lo(0)
                product(2)
                lo(1)
                product(3)
                lo(2)
                lo(3)
                if not last:
                    split("gate", i + 1)
                    split("up", i + 1)
                if first:
                    dve.wait_ge(cleared, 1)
                for b in range(B):
                    dve.wait_ge(y_mm, i * B + (b + 1))
                    nc.vector.tensor_tensor(y_acc[:, b, :], y_acc[:, b, :], y_ps[b % 2][:], ALU.add).then_inc(y_add, 1)
                if not last:
                    split("down", i + 1)
            groups(dve, body)
            dve.wait_ge(down_s_in, 16)
            dve.wait_ge(y_add, NG * B)
            for b in range(B):
                nc.vector.tensor_tensor(y_acc[:, b, :], y_acc[:, b, :], down_s[:], ALU.mult).then_inc(y_scaled, 1)
            for b in range(B):
                dve.wait_ge(y_scaled, b + 1)
                nc.vector.tensor_tensor(mem["x_acc"][:, b, :], mem["x_acc"][:, b, :], y_acc[:, b, :], ALU.add)

        @block.tensor
        def _(pe):
            tensor_ln(pe)

            def body(i, first, last):
                pe.wait_ge(w_lo["gate"], i + 1)
                pe.wait_ge(w_lo["up"], i + 1)
                if first:
                    pe.wait_ge(xn_lo, B)
                for n in range(4):
                    r, t = n // 2, n % 2
                    if n >= 2 or not first:
                        pe.wait_ge(h_full, i * 4 + (n - 1))
                    for name, bank in (("gate", gate_ps), ("up", up_ps)):
                        m = 0
                        for k in range(KT):
                            for a, c in split_passes(w[name][0], w[name][1], xnT[0], xnT[1]):
                                last_mm = nc.tensor.matmul(bank[n % 2][:], a[:, k, t * P:(t + 1) * P], c[:, k, r * HR:(r + 1) * HR],
                                                           start=(m == 0), stop=(m == 3 * KT - 1))
                                m += 1
                    last_mm.then_inc(gu_mm, 1)
                pe.wait_ge(w_lo["down"], i + 1)
                for b in range(B):
                    if b % HB == 0:
                        pe.wait_ge(h_lo, i * 4 + (2 if b == 0 else 4))
                    if b >= 2 or not first:
                        pe.wait_ge(y_add, i * B + (b - 1))
                    m = 0
                    for t in range(FG):
                        for a, c in split_passes(hT[0], hT[1], w["down"][0], w["down"][1]):
                            last_mm = nc.tensor.matmul(y_ps[b % 2][:], a[:, t, b * S:(b + 1) * S], c[:, t, :],
                                                       start=(m == 0), stop=(m == 3 * FG - 1))
                            m += 1
                    last_mm.then_inc(y_mm, 1)
            groups(pe, body)


H1, DH1 = 8, 8
E1 = H1 * DH1
NP = D // P
HG = 4
PICKED = 3
VW = 32
NO_KEY = 1e9 * 8 ** 0.5


def layer1_attention(nc, io, mem):
    with ExitStack() as ctx:
        sb = lambda name, shape, dt=F32: ctx.enter_context(nc.sbuf_tensor(f"att_{name}", shape, dt))
        ps = lambda name, shape, dt=F32: ctx.enter_context(nc.psum_tensor(f"att_{name}", shape, dt))
        sem = stage_semaphores(nc, ctx, "att_")
        BF16 = mybir.dt.bfloat16
        ctx_raw = sb("ctx_raw", [P, D])
        ctx_s = [sb(f"ctx_{n}", [P, D], F32R) for n in ("hi", "lo")]
        xn = sb("xn", [P, 1, D])
        xn_s = [sb(f"xn_{n}", [P, D], F32R) for n in ("hi", "lo")]
        seen = sb("seen", [P, D])
        qk_raw = sb("qk_raw", [P, 2, E1])
        qk_wide = sb("qk_wide", [P, 4, 4, 32])
        qk_s = [sb(f"qk_{n}", [P, 4, P], F32R) for n in ("hi", "lo")]
        wv_raw = sb("wv_raw", [P, E1])
        wv_s = [sb(f"wv_{n}", [P, E1], F32R) for n in ("hi", "lo")]
        bias = sb("bias", [P, 4])
        bv = sb("bv", [P, E1])
        own = sb("own", [P, HG + 1])
        ident16 = sb("ident16", [P, P], F16)
        q_full = sb("q_full", [P, 2, D])
        q_s = sb("q_s", [P, 2, D], F32R)
        k_full = sb("k_full", [P, 2, D])
        k_s = sb("k_s", [P, 2, D], F32R)
        k_own = sb("k_own", [P, 2, NP, HG, P], F32R)
        v_full = sb("v_full", [P, NP, H1, DH1])
        v_rest = sb("v_rest", [P, NP, H1, DH1])
        vT = sb("vT", [P, NP, H1, VW], BF16)
        top = sb("top", [P, 2, H1])
        prob = sb("prob", [P, 2, H1, P])
        prob_s = [sb(f"prob_{n}", [P, 2, H1, P], F16) for n in ("hi", "lo")]
        pT = [sb(f"pT_{n}", [P, 2, H1, P], F16) for n in ("hi", "lo")]
        o_sum = sb("o_sum", [P, NP * H1, DH1])
        rsum = sb("rsum", [P, NP * H1])
        sc_ps = [ps(f"sc{i}", [P, 2, 512]) for i in range(2)]
        t_ps = [ps(f"t{i}", [P, H1, P], F16) for i in range(2)]
        o_ps = ps("o", [P, NP, H1, VW])
        v_ps = o_ps[:].rearrange("p a h c -> p (a h c)")[:, 0:NP * E1]
        ln_sems = [sem(n) for n in ("stat", "aggr", "eps_added", "rstd_done")]
        vector_ln, pool_ln = row_statistics(nc, mem, ln_sems, lambda dve, b: None)
        (w_in, seen_in, ctx_in, prep, wide, wide_hi, wide_lo, wv_hi, wv_lo, ones_set, id16, is_seen, xn_full, xn_hi, xn_lo,
         ctx_hi, ctx_lo, q_mm, k_mm, v_mm, q_out, q_hi, q_lo, k_out, k_hi, k_lo, k_mask, own_a, own_b,
         v_out, v1, v2, v3, rest, s_mm, top_done, s_sub, p_exp, p_hi, p_lo, t_mm, t_hi, t_lo, o_mm, o_added, o_inv, o_done) = [
            sem(n) for n in (
                "w_in seen_in ctx_in prep wide wide_hi wide_lo wv_hi wv_lo ones_set id16 is_seen xn_full xn_hi xn_lo "
                "ctx_hi ctx_lo q_mm k_mm v_mm q_out q_hi q_lo k_out k_hi k_lo k_mask own_a own_b "
                "v_out v1 v2 v3 rest s_mm top_done s_sub p_exp p_hi p_lo t_mm t_hi t_lo o_mm o_added o_inv o_done").split()]
        block = ctx.enter_context(nc.Block())

        def batches(eng, body):
            body(0, True)
            with eng.Fori(1, B) as b:
                body(b, False)

        @block.sync
        def _(sp):
            sp.dma_start(qk_raw[:], io["qk1_t"]).then_inc(w_in, 16)
            sp.dma_start(wv_raw[:], io["wv1_t"]).then_inc(w_in, 16)
            sp.dma_start(bias[:], io["qk1_bias"]).then_inc(w_in, 16)
            sp.dma_start(bv[:], io["bv1"].rearrange("(o n) -> o n", o=1).to_broadcast([P, E1])).then_inc(w_in, 16)
            sp.dma_start(own[:], io["own"]).then_inc(w_in, 16)
            sp.dma_start(ctx_raw[:], io["ctx"][0]).then_inc(ctx_in, 16)
            sp.dma_start(mem["seen_all"][:].rearrange("p b n -> p (b n)"),
                         io["key_mask"].rearrange("b o n -> (b o n)").rearrange("(o n) -> o n", o=1).to_broadcast([P, B * D])).then_inc(seen_in, 16)
            with sp.Fori(0, B - 1) as b:
                sp.wait_ge(ctx_lo, b + 1)
                sp.dma_start(ctx_raw[:].unsqueeze(1), io["ctx"].rearrange("b d s -> d b s")[:, bass.ds(b + 1, 1), :]).then_inc(ctx_in, 16)

        @block.gpsimd
        def _(pool):
            pool_ln(pool)
            nc.gpsimd.memset(qk_wide[:], 0.0).then_inc(prep, 1)
            nc.gpsimd.memset(vT[:], 1.0).then_inc(ones_set, 1)
            nc.gpsimd.tensor_copy(ident16[:], mem["ident"][:]).then_inc(id16, 1)

            def body(b, first):
                pool.wait_ge(ctx_hi, b + 1)
                nc.gpsimd.tensor_tensor(ctx_s[1][:], ctx_raw[:], raw(ctx_s[0][:]), ALU.subtract).then_inc(ctx_lo, 1)
                pool.wait_ge(v1, b + 1)
                nc.gpsimd.tensor_tensor(v_rest[:], v_full[:], vT[:, :, :, 0:DH1], ALU.subtract).then_inc(rest, 1)
                pool.wait_ge(v2, b + 1)
                nc.gpsimd.tensor_tensor(v_rest[:], v_rest[:], vT[:, :, :, DH1:2 * DH1], ALU.subtract).then_inc(rest, 1)
                pool.wait_ge(k_lo, b + 1)
                pool.wait_ge(k_mask, b + 1)
                if not first:
                    pool.wait_ge(s_mm, b * NP)
                for g in range(2):
                    for h in (2, 3):
                        last = nc.gpsimd.tensor_tensor(k_own[:, g, :, h, :], raw(k_s[:, g, :]).rearrange("p (a j) -> p a j", a=NP),
                                                       own[:, h:h + 1].unsqueeze(2).to_broadcast([P, NP, P]), ALU.mult)
                last.then_inc(own_b, 1)
                for p in range(NP):
                    pool.wait_ge(p_hi, b * NP + (p + 1))
                    nc.gpsimd.tensor_tensor(prob_s[1][:, p % 2], prob[:, p % 2], prob_s[0][:, p % 2], ALU.subtract).then_inc(p_lo, 1)
            batches(pool, body)

        @block.scalar
        def _(act):
            act.wait_ge(wide, 2)
            nc.scalar.activation(qk_s[0][:], qk_wide[:].rearrange("p a t e -> p a (t e)"), ACT.Copy).then_inc(wide_hi, 1)
            nc.scalar.activation(wv_s[0][:], wv_raw[:], ACT.Copy).then_inc(wv_hi, 1)

            def body(b, first):
                act.wait_ge(ctx_in, b * 16 + 16)
                if not first:
                    act.wait_ge(v_mm, b)
                nc.scalar.activation(ctx_s[0][:], ctx_raw[:], ACT.Copy).then_inc(ctx_hi, 1)
                act.wait_ge(xn_full, b + 1)
                if not first:
                    act.wait_ge(k_mm, b * 2)
                nc.scalar.activation(xn_s[0][:], xn[:, 0, :], ACT.Copy).then_inc(xn_hi, 1)
                for g in range(2):
                    act.wait_ge(q_mm, b * 2 + (g + 1))
                    if not first:
                        act.wait_ge(s_mm, b * NP)
                        act.wait_ge(q_lo, b)
                    nc.scalar.activation(q_full[:, g, :], sc_ps[0][:, g, :], ACT.Identity, bias=bias[:, g:g + 1]).then_inc(q_out, 1)
                    nc.scalar.activation(q_s[:, g, :], sc_ps[0][:, g, :], ACT.Identity, bias=bias[:, g:g + 1]).then_inc(q_hi, 1)
                act.wait_ge(k_out, b * 2 + 2)
                if not first:
                    act.wait_ge(own_a, b)
                    act.wait_ge(own_b, b)
                nc.scalar.activation(k_s[:], k_full[:], ACT.Copy).then_inc(k_hi, 1)
                act.wait_ge(v_out, b + 1)
                if not first:
                    act.wait_ge(o_mm, b * NP)
                nc.scalar.activation(vT[:, :, :, 0:DH1], v_full[:], ACT.Copy).then_inc(v1, 1)
                act.wait_ge(rest, b * 2 + 1)
                nc.scalar.activation(vT[:, :, :, DH1:2 * DH1], v_rest[:], ACT.Copy).then_inc(v2, 1)
                act.wait_ge(rest, b * 2 + 2)
                nc.scalar.activation(vT[:, :, :, 2 * DH1:3 * DH1], v_rest[:], ACT.Copy).then_inc(v3, 1)

                def exp(p):
                    act.wait_ge(s_sub, b * NP + (p + 1))
                    nc.scalar.activation(prob[:, p % 2], prob[:, p % 2], ACT.Exp, scale=DH1 ** -0.5).then_inc(p_exp, 1)
                    act.wait_ge(p_exp, b * NP + (p + 1))
                    if p >= 2 or not first:
                        act.wait_ge(t_mm, b * NP + (p - 1))
                    nc.scalar.activation(prob_s[0][:, p % 2], prob[:, p % 2], ACT.Copy).then_inc(p_hi, 1)

                def turned(p):
                    act.wait_ge(t_mm, b * NP + (p + 1))
                    if p >= 2 or not first:
                        act.wait_ge(o_mm, b * NP + (p - 1))
                    nc.scalar.activation(pT[0][:, p % 2], t_ps[0][:], ACT.Copy).then_inc(t_hi, 1)

                exp(0)
                for p in range(1, NP):
                    exp(p)
                    turned(p - 1)
                turned(NP - 1)
            batches(act, body)

        @block.vector
        def _(dve):
            vector_ln(dve)
            dve.wait_ge(w_in, 80)
            dve.wait_ge(prep, 1)
            for n in range(2):
                nc.vector.tensor_copy(qk_wide[:, 2 * n:2 * n + 2, 0:3, :],
                                      qk_raw[:, n, :].rearrange("p (g e) -> p g e", g=2).unsqueeze(2).to_broadcast([P, 2, 3, 32])).then_inc(wide, 1)
            dve.wait_ge(wide_hi, 1)
            nc.vector.tensor_tensor(qk_s[1][:], qk_wide[:].rearrange("p a t e -> p a (t e)"), raw(qk_s[0][:]), ALU.subtract).then_inc(wide_lo, 1)
            dve.wait_ge(wv_hi, 1)
            nc.vector.tensor_tensor(wv_s[1][:], wv_raw[:], raw(wv_s[0][:]), ALU.subtract).then_inc(wv_lo, 1)
            dve.wait_ge(ln_sems[3], 1)
            dve.wait_ge(seen_in, 16)

            def body(b, first):
                at = bass.ds(b, 1)
                if not first:
                    dve.wait_ge(xn_lo, b)
                    dve.wait_ge(k_mask, b)
                nc.vector.tensor_scalar(xn[:], mem["x_acc"][:, at, :], mem["mv"][:].rearrange("p b s -> p (b s)")[:, bass.ds(b * 2, 1)],
                                        mem["rstd"][:, at], ALU.subtract, ALU.mult).then_inc(xn_full, 1)
                nc.vector.tensor_scalar(seen[:].unsqueeze(1), mem["seen_all"][:, at, :], 0.0, None, ALU.is_gt).then_inc(is_seen, 1)
                dve.wait_ge(xn_hi, b + 1)
                nc.vector.tensor_tensor(xn_s[1][:], xn[:, 0, :], raw(xn_s[0][:]), ALU.subtract).then_inc(xn_lo, 1)
                dve.wait_ge(is_seen, b + 1)
                for g in range(2):
                    dve.wait_ge(k_mm, b * 2 + (g + 1))
                    nc.vector.scalar_tensor_tensor(k_full[:, g, :], sc_ps[1][:, g, :], bias[:, 2 + g:3 + g], seen[:], ALU.add, ALU.mult).then_inc(k_out, 1)
                dve.wait_ge(v_mm, b + 1)
                if not first:
                    dve.wait_ge(v3, b)
                nc.vector.tensor_tensor(v_full[:], v_ps.rearrange("p (a h c) -> p a h c", a=NP, h=H1),
                                        bv[:].rearrange("p (h c) -> p h c", h=H1).unsqueeze(1).to_broadcast([P, NP, H1, DH1]), ALU.add).then_inc(v_out, 1)
                dve.wait_ge(q_hi, b * 2 + 2)
                nc.vector.tensor_tensor(q_s[64:96], q_full[64:96], raw(q_s[64:96]), ALU.subtract).then_inc(q_lo, 1)
                dve.wait_ge(k_hi, b + 1)
                nc.vector.tensor_tensor(k_s[32:64], k_full[32:64], raw(k_s[32:64]), ALU.subtract).then_inc(k_lo, 1)
                nc.vector.tensor_scalar(k_s[96:128], seen[96:128].unsqueeze(1).to_broadcast([32, 2, D]), 1.0,
                                        own[96:128, HG:HG + 1], ALU.subtract, ALU.mult).then_inc(k_mask, 1)
                dve.wait_ge(k_lo, b + 1)
                dve.wait_ge(k_mask, b + 1)
                for g in range(2):
                    for h in (0, 1):
                        last = nc.vector.tensor_scalar(k_own[:, g, :, h, :], raw(k_s[:, g, :]).rearrange("p (a j) -> p a j", a=NP),
                                                       own[:, h:h + 1], None, ALU.mult)
                last.then_inc(own_a, 1)

                def centre(p):
                    dve.wait_ge(s_mm, b * NP + (p + 1))
                    scores = sc_ps[p % 2][:].rearrange("p g (h j) -> p (g h) j", h=HG)
                    if p >= 2 or not first:
                        dve.wait_ge(s_sub, b * NP + (p - 1))
                    nc.vector.tensor_reduce(top[:, p % 2, :], scores, AX.X, ALU.max).then_inc(top_done, 1)
                    dve.wait_ge(top_done, b * NP + (p + 1))
                    if p >= 2 or not first:
                        dve.wait_ge(p_lo, b * NP + (p - 1))
                    nc.vector.tensor_tensor(prob[:, p % 2], scores, top[:, p % 2, :].unsqueeze(2).to_broadcast([P, H1, P]),
                                            ALU.subtract).then_inc(s_sub, 1)

                def turned(p):
                    dve.wait_ge(t_mm, b * NP + (p + 1))
                    if p >= 2 or not first:
                        dve.wait_ge(o_mm, b * NP + (p - 1))
                    nc.vector.tensor_copy(pT[1][:, p % 2], t_ps[1][:]).then_inc(t_lo, 1)

                centre(0)
                for p in range(1, NP):
                    centre(p)
                    turned(p - 1)
                turned(NP - 1)
                dve.wait_ge(o_mm, b * NP + NP)
                if not first:
                    dve.wait_ge(o_done, b)
                outputs = o_ps[:].rearrange("p a h c -> p (a h) c")
                nc.vector.tensor_reduce(o_sum[:], outputs[:, :, 0:PICKED * DH1].rearrange("p n (t c) -> p n c t", t=PICKED),
                                        AX.X, ALU.add).then_inc(o_added, 1)
                nc.vector.reciprocal(rsum[:], outputs[:, :, PICKED * DH1]).then_inc(o_inv, 1)
                dve.wait_ge(o_added, b + 1)
                dve.wait_ge(o_inv, b + 1)
                nc.vector.tensor_tensor(mem["o_all"][:, bass.ds(b * NP * H1, NP * H1), :], o_sum[:],
                                        rsum[:].unsqueeze(2).to_broadcast([P, NP * H1, DH1]), ALU.mult).then_inc(o_done, 1)
            batches(dve, body)

        @block.tensor
        def _(pe):
            pe.wait_ge(wide_lo, 1)
            pe.wait_ge(wv_lo, 1)
            pe.wait_ge(id16, 1)
            pe.wait_ge(ones_set, 1)

            def body(b, first):
                pe.wait_ge(xn_lo, b + 1)
                if not first:
                    pe.wait_ge(s_sub, b * NP)
                for n in range(4):
                    for m, (a, c) in enumerate(split_passes(qk_s[0], qk_s[1], xn_s[0], xn_s[1])):
                        last = nc.tensor.matmul(sc_ps[n // 2][:, n % 2, :], a[:, n, :], c[:], start=(m == 0), stop=(m == 2))
                    last.then_inc(q_mm if n < 2 else k_mm, 1)
                pe.wait_ge(ctx_lo, b + 1)
                if not first:
                    pe.wait_ge(o_done, b)
                for p in range(NP):
                    for m, (a, c) in enumerate(split_passes(ctx_s[0], ctx_s[1], wv_s[0], wv_s[1])):
                        last = nc.tensor.matmul(v_ps[:, p * E1:(p + 1) * E1], a[:, p * P:(p + 1) * P], c[:], start=(m == 0), stop=(m == 2))
                last.then_inc(v_mm, 1)

                def scores(p):
                    if p == 0:
                        pe.wait_ge(q_lo, b + 1)
                        pe.wait_ge(own_a, b + 1)
                        pe.wait_ge(own_b, b + 1)
                    if p >= 2:
                        pe.wait_ge(s_sub, b * NP + (p - 1))
                    for g in range(2):
                        last = nc.tensor.matmul(sc_ps[p % 2][:, g, :], q_s[:, g, p * P:(p + 1) * P], k_own[:, g, p],
                                                start=True, stop=True)
                    last.then_inc(s_mm, 1)

                def turn(p):
                    pe.wait_ge(p_lo, b * NP + (p + 1))
                    if p >= 1 or not first:
                        pe.wait_ge(t_hi, b * NP + p)
                        pe.wait_ge(t_lo, b * NP + p)
                    for n in range(2):
                        for h in range(H1):
                            last = nc.tensor.transpose(t_ps[n][:, h, :], prob_s[n][:, p % 2, h, :], ident16[:])
                    last.then_inc(t_mm, 1)

                def outputs(p):
                    pe.wait_ge(t_hi, b * NP + (p + 1))
                    pe.wait_ge(t_lo, b * NP + (p + 1))
                    if p == 0:
                        pe.wait_ge(v3, b + 1)
                    for h in range(H1):
                        for n in range(2):
                            last = nc.tensor.matmul(o_ps[:, p, h, 0:PICKED * DH1 + 1], pT[n][:, p % 2, h, :], vT[:, p, h, 0:PICKED * DH1 + 1],
                                                    start=(n == 0), stop=(n == 1))
                    last.then_inc(o_mm, 1)

                scores(0)
                scores(1)
                turn(0)
                scores(2)
                outputs(0)
                turn(1)
                scores(3)
                outputs(1)
                turn(2)
                outputs(2)
                turn(3)
                outputs(3)
            batches(pe, body)


def layer1_rest(nc, io, mem, out):
    NE = 2
    with ExitStack() as ctx:
        sb = lambda name, shape, dt=F32: ctx.enter_context(nc.sbuf_tensor(f"rest_{name}", shape, dt))
        ps = lambda name: ctx.enter_context(nc.psum_tensor(f"rest_{name}", [P, 512], F32))
        sem = stage_semaphores(nc, ctx, "rest_")
        wo_raw = sb("wo_raw", [E1, P])
        wo_s = [sb(f"wo_{n}", [E1, P], F32R) for n in ("hi", "lo")]
        bo = sb("bo", [P, 1])
        gelu = sb("gelu", [E1, 2, D])
        gelu_s = [sb(f"gelu_{n}", [E1, 2, D], F32R) for n in ("hi", "lo")]
        masked = sb("masked", [P, 2, D])
        a_raw = sb("a_raw", [P, NE, D])
        a_s = [sb(f"a_{n}", [P, NE, D], F32R) for n in ("hi", "lo")]
        b_raw = sb("b_raw", [P, NE, D])
        b_s = [sb(f"b_{n}", [P, NE, D], F32R) for n in ("hi", "lo")]
        cs = sb("cs", [P, 2, NE])
        w_exp = sb("w_exp", [P, NE])
        w1 = sb("w1", [P, KT, D])
        w1_s = [sb(f"w1_{n}", [P, KT, D], F32R) for n in ("hi", "lo")]
        bias = sb("bias", [P, D])
        xn = sb("xn", [P, B, D])
        xnT = [sb(f"xnT_{n}", [P, KT, B * S], F32R) for n in ("hi", "lo")]
        o_t_ps = [ps("o_t0"), ps("o_t1")]
        y_ps = [ps("y0"), ps("y1")]
        tr_ps = [ps("tr0"), ps("tr1")]
        m_ps = [ps("m0"), ps("m1")]
        vector_ln, pool_ln, scalar_ln, tensor_ln, xn_lo = normalised_columns(nc, mem, xn, xnT, tr_ps, sem)
        (wo_in, lora_in, w_in, bias_in, wo_hi, wo_lo, a_hi, a_lo, w_set, b_set, b_hi, b_lo, m_mm, w_add, w_hi, w_lo,
         o_t, g_done, g_hi, g_lo, p_mm, p_mask, x_done, z_mm, z_add, z_bias, stored) = [sem(n) for n in (
            "wo_in lora_in w_in bias_in wo_hi wo_lo a_hi a_lo w_set b_set b_hi b_lo m_mm w_add w_hi w_lo "
            "o_t g_done g_hi g_lo p_mm p_mask x_done z_mm z_add z_bias stored").split()]
        block = ctx.enter_context(nc.Block())

        @block.sync
        def _(sp):
            sp.dma_start(wo_raw[:], io["wo1_t"]).then_inc(wo_in, 16)
            sp.dma_start(bo[:], io["bo1"].rearrange("(p o) -> p o", o=1)).then_inc(wo_in, 16)
            sp.dma_start(a_raw[:], io["lora_a"].rearrange("(t p) d -> p t d", p=P)).then_inc(lora_in, 16)
            sp.dma_start(b_raw[:], io["lora_b"].rearrange("(t p) d -> p t d", p=P)).then_inc(lora_in, 16)
            sp.dma_start(cs[:], io["lora_cs"]).then_inc(lora_in, 16)
            sp.dma_start(w1[:], io["w1_t"].rearrange("(k p) n -> p k n", p=P)).then_inc(w_in, 16)
            sp.dma_start(bias[:], io["bias1"].rearrange("(o n) -> o n", o=1).to_broadcast([P, D])).then_inc(bias_in, 16)
            for b in range(B):
                sp.wait_ge(z_bias, b + 1)
                sp.dma_start(out[b], mem["x_acc"][:, b, :]).then_inc(stored, 16)
            sp.wait_ge(stored, 16 * B)

        @block.gpsimd
        def _(pool):
            pool_ln(pool)

        @block.scalar
        def _(act):
            act.wait_ge(wo_in, 32)
            nc.scalar.activation(wo_s[0][:], wo_raw[:], ACT.Copy).then_inc(wo_hi, 1)
            act.wait_ge(lora_in, 48)
            nc.scalar.activation(a_s[0][:], a_raw[:], ACT.Copy).then_inc(a_hi, 1)
            act.wait_ge(b_set, NE)
            nc.scalar.activation(b_s[0][:], b_raw[:], ACT.Copy).then_inc(b_hi, 1)

            def project(b):
                act.wait_ge(o_t, b + 1)
                if b >= 2:
                    act.wait_ge(g_lo, b - 1)
                nc.scalar.activation(gelu[:, b % 2, :], o_t_ps[b % 2][0:E1, :], ACT.Gelu).then_inc(g_done, 1)
                act.wait_ge(g_done, b + 1)
                if b >= 2:
                    act.wait_ge(p_mm, b - 1)
                nc.scalar.activation(gelu_s[0][:, b % 2, :], gelu[:, b % 2, :], ACT.Copy).then_inc(g_hi, 1)
            for b in range(B):
                project(b)
            for k in range(KT):
                act.wait_ge(w_add, k + 1)
                nc.scalar.activation(w1_s[0][:, k, :], w1[:, k, :], ACT.Copy).then_inc(w_hi, 1)
            scalar_ln(act)

        @block.vector
        def _(dve):
            dve.wait_ge(wo_hi, 1)
            nc.vector.tensor_tensor(wo_s[1][:], wo_raw[:], raw(wo_s[0][:]), ALU.subtract).then_inc(wo_lo, 1)
            dve.wait_ge(lora_in, 48)
            nc.vector.tensor_tensor(w_exp[:], cs[:, 0, :], cs[:, 1, :], ALU.mult).then_inc(w_set, 1)
            dve.wait_ge(w_set, 1)
            for t in range(NE):
                nc.vector.tensor_scalar(b_raw[:, t, :], b_raw[:, t, :], w_exp[:, t:t + 1], None, ALU.mult).then_inc(b_set, 1)
            dve.wait_ge(a_hi, 1)
            nc.vector.tensor_tensor(a_s[1][:], a_raw[:], raw(a_s[0][:]), ALU.subtract).then_inc(a_lo, 1)
            dve.wait_ge(b_hi, 1)
            nc.vector.tensor_tensor(b_s[1][:], b_raw[:], raw(b_s[0][:]), ALU.subtract).then_inc(b_lo, 1)
            dve.wait_ge(w_in, 16)
            for k in range(KT):
                dve.wait_ge(m_mm, k + 1)
                nc.vector.tensor_tensor(w1[:, k, :], w1[:, k, :], m_ps[k % 2][:], ALU.add).then_inc(w_add, 1)

            def lo(b):
                dve.wait_ge(g_hi, b + 1)
                nc.vector.tensor_tensor(gelu_s[1][:, b % 2, :], gelu[:, b % 2, :], raw(gelu_s[0][:, b % 2, :]), ALU.subtract).then_inc(g_lo, 1)

            def add(b):
                dve.wait_ge(p_mm, b + 1)
                if b >= 2:
                    dve.wait_ge(x_done, b - 1)
                nc.vector.scalar_tensor_tensor(masked[:, b % 2, :], y_ps[b % 2][:], bo[:, 0:1], mem["seen_all"][:, b, :], ALU.add, ALU.mult).then_inc(p_mask, 1)
                dve.wait_ge(p_mask, b + 1)
                nc.vector.tensor_tensor(mem["x_acc"][:, b, :], mem["x_acc"][:, b, :], masked[:, b % 2, :], ALU.add).then_inc(x_done, 1)
            lo(0)
            for b in range(1, B):
                lo(b)
                add(b - 1)
            add(B - 1)
            for k in range(KT):
                dve.wait_ge(w_hi, k + 1)
                nc.vector.tensor_tensor(w1_s[1][:, k, :], w1[:, k, :], raw(w1_s[0][:, k, :]), ALU.subtract).then_inc(w_lo, 1)
            dve.wait_ge(x_done, B)
            vector_ln(dve)
            dve.wait_ge(bias_in, 16)
            for b in range(B):
                dve.wait_ge(z_mm, b + 1)
                nc.vector.tensor_tensor(mem["x_acc"][:, b, :], mem["x_acc"][:, b, :], y_ps[b % 2][:], ALU.add).then_inc(z_add, 1)
                dve.wait_ge(z_add, b + 1)
                nc.vector.tensor_tensor(mem["x_acc"][:, b, :], mem["x_acc"][:, b, :], bias[:], ALU.add).then_inc(z_bias, 1)

        @block.tensor
        def _(pe):
            def turn(b):
                if b >= 2:
                    pe.wait_ge(g_done, b - 1)
                for p in range(NP):
                    last = nc.tensor.transpose(o_t_ps[b % 2][0:E1, p * P:(p + 1) * P],
                                               mem["o_all"][:, (b * NP + p) * H1:(b * NP + p + 1) * H1, :].rearrange("p h c -> p (h c)"),
                                               mem["ident"][:])
                last.then_inc(o_t, 1)

            def project(b):
                pe.wait_ge(g_lo, b + 1)
                if b >= 2:
                    pe.wait_ge(p_mask, b - 1)
                for m, (a, c) in enumerate(split_passes(wo_s[0], wo_s[1], gelu_s[0], gelu_s[1])):
                    last = nc.tensor.matmul(y_ps[b % 2][:], a[:], c[:, b % 2, :], start=(m == 0), stop=(m == 2))
                last.then_inc(p_mm, 1)

            turn(0)
            turn(1)
            pe.wait_ge(a_lo, 1)
            pe.wait_ge(b_lo, 1)
            for k in range(KT):
                if k >= 2:
                    pe.wait_ge(w_add, k - 1)
                n = 0
                for t in range(NE):
                    for a, c in split_passes(a_s[0], a_s[1], b_s[0], b_s[1]):
                        last = nc.tensor.matmul(m_ps[k % 2][:], a[:, t, k * P:(k + 1) * P], c[:, t, :], start=(n == 0), stop=(n == 3 * NE - 1))
                        n += 1
                last.then_inc(m_mm, 1)
            pe.wait_ge(wo_lo, 1)
            for b in range(B):
                if b >= 2:
                    turn(b)
                project(b)
            tensor_ln(pe)
            pe.wait_ge(w_lo, KT)
            for b in range(B):
                pe.wait_ge(xn_lo, b + 1)
                if b >= 2:
                    pe.wait_ge(z_add, b - 1)
                else:
                    pe.wait_ge(p_mask, B - 1 + b)
                n = 0
                for k in range(KT):
                    for a, c in split_passes(xnT[0], xnT[1], w1_s[0], w1_s[1]):
                        last = nc.tensor.matmul(y_ps[b % 2][:], a[:, k, b * S:(b + 1) * S], c[:, k, :], start=(n == 0), stop=(n == 3 * KT - 1))
                        n += 1
                last.then_inc(z_mm, 1)


def build(nc, io, out):
    with ExitStack() as ctx:
        sb = lambda name, shape, dt=F32: ctx.enter_context(nc.sbuf_tensor(name, shape, dt))
        mem = {
            "x_acc": sb("x_acc", [P, B, D]),
            "cos_k": sb("cos_k", [P, S]), "sin_k": sb("sin_k", [P, S]),
            "cos_q": sb("cos_q", [P, S]), "sin_q": sb("sin_q", [P, S]),
            "mask_bias": sb("mask_bias", [P, S]), "ident": sb("ident", [P, P]),
            "minus_half": sb("minus_half", [P, B]), "pick": sb("pick", [P, HB, P], F32R),
            "row": sb("row", [HB, HB, P], F32R),
            "stats": sb("stats", [P, B, 6]), "mv": sb("mv", [P, B, 2]), "rstd": sb("rstd", [P, B]),
        }
        prepare(nc, io, mem)
        layer0_attention(nc, io, mem)
        layer0_ffn(nc, io, mem)
        mem["seen_all"] = sb("seen_all", [P, B, D])
        mem["o_all"] = sb("o_all", [P, B * NP * H1, DH1])
        layer1_attention(nc, io, mem)
        layer1_rest(nc, io, mem, out)


def score_rows():
    import numpy as np
    own = np.zeros((P, HG + 1), np.float32)
    for part in range(3):
        for h in range(HG):
            own[part * 32 + h * DH1:part * 32 + (h + 1) * DH1, h] = 1.0
    own[96, :] = 1.0
    own[96, HG] = NO_KEY
    return own


def rotary_tables():
    import numpy as np
    inv = (1.0 / (np.float32(10000.0) ** (np.arange(0, DH, 2, dtype=np.float32) / np.float32(DH)))).astype(np.float32)
    phase = (np.arange(S, dtype=np.float32)[:, None] * inv[None, :]).astype(np.float32)
    c, s = np.cos(phase).astype(np.float32).T, np.sin(phase).astype(np.float32).T
    return np.ascontiguousarray(np.concatenate([c, c])), np.ascontiguousarray(np.concatenate([-s, s]))


def kernel(**inputs):
    import numpy as np
    import concourse.bacc as bacc
    from concourse.bass_utils import run_bass_kernel_spmd as run

    nc = bacc.Bacc("TRN2", target_bir_lowering=False, num_devices=1)
    get = lambda n: np.ascontiguousarray(inputs[n])
    cos, sin = rotary_tables()
    bias = np.zeros((P, 4), np.float32)
    for n, name in enumerate(("L1_xattn_bq", "L1_xattn_bk")):
        for part in range(3):
            bias[part * 32:part * 32 + 32, 2 * n:2 * n + 2] = get(name).reshape(2, 32).T
    bias[96, 0:2] = 1.0
    arrays = {
        "x": get("x"),
        "ctx_t": np.ascontiguousarray(get("ctx_4096").reshape(B * S, D).T),
        "mask_t": np.ascontiguousarray(get("mask_1x1xSxS2_bk0").reshape(S, S).T),
        "cos": cos, "sin": sin,
        "gate_t": np.ascontiguousarray(get("L0_ffn_gate_t").T), "up_t": np.ascontiguousarray(get("L0_ffn_up_t").T),
        "down_t": np.ascontiguousarray(get("L0_ffn_down_t").T),
        "gu_s": np.ascontiguousarray(np.stack([get("L0_ffn_gate_s").reshape(NG, FG, P), get("L0_ffn_up_s").reshape(NG, FG, P)], 1)
                                     .reshape(NG * 2 * FG, P).T),
        "down_s": get("L0_ffn_down_s"),
        "ctx": get("ctx_4096"), "key_mask": get("mask_Bx1x4096_ff1"),
        "qk1_t": np.ascontiguousarray(np.stack([get("L1_xattn_Wq").T, get("L1_xattn_Wk").T], 1)),
        "wv1_t": np.ascontiguousarray(get("L1_xattn_Wv").T), "bv1": get("L1_xattn_bv"),
        "qk1_bias": np.ascontiguousarray(bias), "own": score_rows(),
        "wo1_t": np.ascontiguousarray(get("L1_xattn_Wo").T), "bo1": get("L1_xattn_bo"),
        "lora_a": get("L1_ffn_A").reshape(256, D), "lora_b": np.ascontiguousarray(get("L1_ffn_Bf").transpose(0, 2, 1)).reshape(256, D),
        "lora_cs": np.ascontiguousarray(np.stack([np.repeat(get("L1_ffn_coeffs"), 16).reshape(2, P).T,
                                                  np.repeat(get("L1_ffn_scales"), 16).reshape(2, P).T], 1)),
        "w1_t": np.ascontiguousarray(get("L1_ffn_W").T), "bias1": get("L1_ffn_bias"),
        "Wq0": get("L0_xattn_Wq"), "Wk0": get("L0_xattn_Wk"), "Wv0": get("L0_xattn_Wv"), "Wo0": get("L0_xattn_Wo"),
    }
    io = {n: nc.dram_tensor(f"in_{n}", a.shape, mybir.dt.from_np(a.dtype), kind="ExternalInput").ap()
          for n, a in arrays.items()}
    out = nc.dram_tensor("out", (B, S, D), F32, kind="ExternalOutput").ap()
    build(nc, io, out)
    r = run(nc, [{f"in_{n}": a for n, a in arrays.items()}], core_ids=[0])
    return r.results[0]["out"]
```

```python
from contextlib import ExitStack

import concourse.bass as bass
from concourse import mybir

F32 = mybir.dt.float32
F32R = mybir.dt.float32r
F16 = mybir.dt.float16
I32 = mybir.dt.int32
U8 = mybir.dt.uint8
ALU = mybir.AluOpType
ACT = mybir.ActivationFunctionType
AX = mybir.AxisListType

P = 128
B, S, D = 8, 128, 512
KT = D // P
NH, NKV = 32, 8
G = NH // NKV
DH = 128
HB = 4
HR = HB * S
RL = 32
TANH_SCALE = 0.08838834764831845 / 30.0
CAP = 30.0
EPS = 1e-5
BIG = 1e30


def raw(ap):
    return ap.bitcast(F32)


def stage_semaphores(nc, ctx, prefix):
    made = []

    def clear():
        nc.clear_and_free_semaphores(made)
        nc.all_engine_barrier(sem_only=True)

    ctx.callback(clear)

    def sem(name):
        made.append(nc.alloc_semaphore(prefix + name))
        return made[-1]

    return sem


def split_passes(hi_w, lo_w, hi_x, lo_x):
    return ((hi_w, lo_x), (lo_w, hi_x), (hi_w, hi_x))


def take_statistics(nc, mem, at):
    return nc.vector.bn_stats(mem["stats"][:, at, :], mem["x_acc"][:, at, :])


def row_statistics(nc, mem, sems, in_block):
    stat, aggr, eps_added, rstd_done = sems

    def vector(dve):
        for b in range(B):
            if in_block:
                dve.wait_ge(stat, b + 1)
            nc.vector.bn_aggr(mem["mv"][:, b, :], mem["stats"][:, b, :]).then_inc(aggr, 1)

    def pool(eng):
        eng.wait_ge(aggr, B)
        nc.gpsimd.tensor_scalar(mem["rstd"][:], mem["mv"][:, :, 1], EPS, None, ALU.add).then_inc(eps_added, 1)
        eng.wait_ge(eps_added, 1)
        nc.gpsimd.tensor_tensor(mem["rstd"][:], mem["rstd"][:], mem["minus_half"][:], ALU.pow).then_inc(rstd_done, 1)

    return vector, pool


def prepare(nc, io, mem):
    with ExitStack() as ctx:
        sb = lambda name, shape, dt: ctx.enter_context(nc.sbuf_tensor(name, shape, dt))
        sem = stage_semaphores(nc, ctx, "prep_")
        mask_keys = sb("mask_keys", [P, S], U8)
        allowed = sb("allowed", [P, S], F32)
        ones = sb("ones", [P, P], F32)
        keep = sb("keep", [P, S], F32)
        empty = sb("empty", [P, S], F32)
        count_ps = ctx.enter_context(nc.psum_tensor("count_ps", [P, S], F32))
        x_in, tab_in, mask_in, early_in = sem("x_in"), sem("tab_in"), sem("mask_in"), sem("early_in")
        consts, step, counted = sem("consts"), sem("step"), sem("counted")
        ln_sems = [sem(n) for n in ("stat", "aggr", "eps_added", "rstd_done")]
        ln_vector, ln_pool = row_statistics(nc, mem, ln_sems, True)
        block = ctx.enter_context(nc.Block())

        @block.sync
        def _(sp):
            sp.dma_start(mask_keys[:], io["mask_t"]).then_inc(mask_in, 16)
            sp.dma_start(mem["cos_k"][:], io["cos"]).then_inc(tab_in, 16)
            sp.dma_start(mem["sin_k"][:], io["sin"]).then_inc(tab_in, 16)
            sp.dma_start(mem["x_acc"][:], io["x"].rearrange("b s d -> s b d")).then_inc(x_in, 16)
            sp.dma_start(mem["v_all"][:, :, 0:512], io["ctx_t"].rearrange("(k p) n -> p k n", p=P)[:, :, 0:HR]).then_inc(early_in, 16)
            sp.dma_start(mem["v_all"][:, :, 512:1024], io["Wv0"].rearrange("(k p) n -> p k n", p=P)[:, :, 0:512]).then_inc(early_in, 16)
            sp.wait_ge(early_in, 32)

        @block.gpsimd
        def _(pool):
            nc.gpsimd.memset(mem["ident"][:], 0.0).then_inc(consts, 1)
            nc.gpsimd.memset(ones[:], 1.0).then_inc(consts, 1)
            nc.gpsimd.memset(mem["minus_half"][:], -0.5).then_inc(consts, 1)
            nc.gpsimd.memset(raw(mem["pick"][:]), 0.0).then_inc(consts, 1)
            pool.wait_ge(consts, 4)
            nc.gpsimd.affine_select(out=mem["ident"][:], in_=mem["ident"][:], compare_op=ALU.not_equal,
                                    fill=1.0, base=0, pattern=[[-1, P]], channel_multiplier=1).then_inc(consts, 1)
            for b in range(HB):
                nc.gpsimd.memset(raw(mem["pick"][:, b, b:b + 1]), 1.0).then_inc(consts, 1)
            pool.wait_ge(consts, 5 + HB)
            ln_pool(pool)

        @block.tensor
        def _(pe):
            pe.wait_ge(consts, 2)
            pe.wait_ge(step, 1)
            nc.tensor.matmul(count_ps[:], ones[:], allowed[:], start=True, stop=True).then_inc(counted, 1)

        @block.vector
        def _(dve):
            dve.wait_ge(mask_in, 16)
            nc.vector.tensor_scalar(allowed[:], mask_keys[:], 0, None, ALU.not_equal).then_inc(step, 1)
            dve.wait_ge(counted, 1)
            nc.vector.tensor_scalar(keep[:], count_ps[:], 0.0, None, ALU.is_gt).then_inc(step, 1)
            nc.vector.tensor_scalar(empty[:], count_ps[:], 0.0, None, ALU.is_equal).then_inc(step, 1)
            dve.wait_ge(step, 3)
            nc.vector.tensor_tensor(allowed[:], allowed[:], empty[:], ALU.add).then_inc(step, 1)
            dve.wait_ge(step, 4)
            nc.vector.tensor_scalar(mem["mask_bias"][:], allowed[:], 1.0, BIG, ALU.subtract, ALU.mult).then_inc(step, 1)
            dve.wait_ge(consts, 5)
            for n in range(P // RL):
                nc.vector.tensor_scalar(mem["row"][n * RL:(n + 1) * RL], mem["ident"][0:RL, 0:HB].unsqueeze(2).to_broadcast([RL, HB, P]),
                                        1.0, None, ALU.mult).then_inc(step, 1)
            dve.wait_ge(tab_in, 32)
            nc.vector.tensor_tensor(mem["cos_q"][:], mem["cos_k"][:], keep[:], ALU.mult).then_inc(step, 1)
            nc.vector.tensor_tensor(mem["sin_q"][:], mem["sin_k"][:], keep[:], ALU.mult).then_inc(step, 1)
            dve.wait_ge(x_in, 16)
            for b in range(B):
                take_statistics(nc, mem, slice(b, b + 1)).then_inc(ln_sems[0], 1)
            ln_vector(dve)


def layer0_attention(nc, io, mem):
    RING = 4
    FILLS = 4 * (NKV + 1)
    USES = 1 + 2 * NKV
    with ExitStack() as ctx:
        sb = lambda name, shape, dt: ctx.enter_context(nc.sbuf_tensor(name, shape, dt))
        ps = lambda name, shape=[P, 512]: ctx.enter_context(nc.psum_tensor(name, shape, F32))
        sem = stage_semaphores(nc, ctx, "l0_")
        ring = sb("ring", [P, RING, 512], F32)
        raw_k = sb("raw_k", [P, KT, DH], F32)
        ctxT = [sb(f"ctxT_{n}", [P, KT, HR], F32R) for n in ("hi", "lo")]
        xnT = [sb(f"xnT_{n}", [P, KT, HR], F32R) for n in ("hi", "lo")]
        v_all = mem["v_all"]
        early = [v_all[:, :, n * 512:(n + 1) * 512] for n in range(2)]
        wa = [sb(f"wa_{n}", [P, KT, 512], F32R) for n in ("hi", "lo")]
        wo = [sb(f"wo_{n}", [P, G, D], F32R) for n in ("hi", "lo")]
        wk = [sb(f"wk_{n}", [P, KT, DH], F32R) for n in ("hi", "lo")]
        kT = [sb(f"kT_{n}", [P, HR], F32R) for n in ("hi", "lo")]
        qT = [sb(f"qT_{n}", [P, G, HR], F32R) for n in ("hi", "lo")]
        vg = [sb(f"vg_{n}", [P, HB, DH], F32R) for n in ("hi", "lo")]
        oT = [sb(f"oT_{n}", [P, HB, G * S], F32R) for n in ("hi", "lo")]
        o_raw = sb("o_raw", [P, HB, G * S], F32)
        rinv = sb("rinv", [HB, G * S], F32)
        rinv_s = sb("rinv_s", [P, G * S], F32R)
        prob = sb("prob", [P, 2, G * S], F32)
        pT = [sb(f"pT_{n}", [P, 2, G * S], F32R) for n in ("hi", "lo")]
        rope_a = sb("rope_a", [P, 2, HR], F32)
        rope_b = sb("rope_b", [P, 2, HR], F32)
        xn = o_raw

        proj_ps = [ps("proj0_ps"), ps("proj1_ps")]
        s_ps = [ps("s0_ps"), ps("s1_ps")]
        o_ps = ps("o_ps")
        sum_ps = ps("sum_ps")
        y_ps = [ps("y0_ps"), ps("y1_ps")]
        k_ps = y_ps[1]
        out_ps = [o_ps, proj_ps[1]]
        rinv_ps = [y_ps[0], y_ps[1], sum_ps, o_ps]

        ring_in = [sem(f"ring_in{i}") for i in range(RING)]
        (rinv_clear, raw_k_in, ahead_in, ctx_hi, ctx_lo, wa_hi, wa_lo, wo_hi, wo_lo, xn_done, xn_tr, xn_hi, xn_lo,
         v_mm, v_out, k_mm, k_mul, k_full, k_hi, k_lo, wk_hi, wk_lo, vg_hi, vg_lo,
         q_mm, q_mul, q_shift, q_sin, q_full, q_hi, q_lo, s_mm, s_tanh, s_masked, p_exp, p_hi, p_lo,
         o_mm, sum_mm, o_out, inv_done, inv_hi, inv_lo, rinv_mm, o_norm, o_hi, o_lo, y_mm, y_add) = [
            sem(n) for n in (
                "rinv_clear raw_k_in ahead_in ctx_hi ctx_lo wa_hi wa_lo wo_hi wo_lo xn_done xn_tr xn_hi xn_lo "
                "v_mm v_out k_mm k_mul k_full k_hi k_lo wk_hi wk_lo vg_hi vg_lo "
                "q_mm q_mul q_shift q_sin q_full q_hi q_lo s_mm s_tanh s_masked p_exp p_hi p_lo "
                "o_mm sum_mm o_out inv_done inv_hi inv_lo rinv_mm o_norm o_hi o_lo y_mm y_add").split()]

        half = ctx.enter_context(nc.Fori(0, B // HB))

        def once(n, per):
            return half * per + n

        def head(g, per, n):
            return half * (NKV * per) + g * per + n

        def fill(g, n):
            return half * FILLS + 4 * g + (4 + n)

        block = ctx.enter_context(nc.Block())

        def heads(eng, body):
            body(0, True, False)
            with eng.Fori(1, NKV - 1) as g:
                body(g, False, False)
            body(NKV - 1, False, True)

        wq_d = io["Wq0"].rearrange("(k p) n -> p k n", p=P)
        wk_d = io["Wk0"].rearrange("(k p) n -> p k n", p=P)
        wv_d = io["Wv0"].rearrange("(k p) n -> p k n", p=P)
        wo_d = io["Wo0"].rearrange("(k p) n -> p k n", p=P)
        ctx_d = io["ctx_t"].rearrange("(k p) n -> p k n", p=P)

        @block.sync
        def _(sp):
            def piece(src, slot, before=None, done=None):
                if before is not None:
                    sp.wait_ge(before[0], done)
                    sp.wait_ge(before[1], done)
                sp.dma_start(ring[:, slot:slot + 1, :], src).then_inc(ring_in[slot], 16)

            in_wa, in_wo = (wa_hi, wa_lo), (wo_hi, wo_lo)
            for j in range(4):
                piece(wv_d[:, j:j + 1, 512:1024], j)
            sp.dma_start(raw_k[:], wk_d[:, :, 0:DH]).then_inc(raw_k_in, 16)
            for j in range(4):
                piece(wq_d[:, j:j + 1, 0:512], j, in_wo, once(j + 1, FILLS))

            def body(g, first, last):
                if not last:
                    sp.wait_ge(wk_hi, head(g, 1, 1))
                    sp.wait_ge(wk_lo, head(g, 1, 1))
                    sp.dma_start(raw_k[:], wk_d[:, :, bass.ds(g * DH + DH, DH)]).then_inc(raw_k_in, 16)
                    for j in range(4):
                        piece(wq_d[:, j:j + 1, bass.ds(g * 512 + 512, 512)], j, *((in_wa, fill(0, j + 1)) if first else (in_wo, fill(g - 1, j + 1))))
                for j in range(4):
                    piece(wo_d[:, bass.ds(g * G + j, 1), :], j, *((in_wo, fill(g - 1, j + 1)) if last else (in_wa, fill(g + 1, j + 1))))

            heads(sp, body)
            sp.wait_ge(vg_hi, once(NKV, NKV))
            sp.wait_ge(vg_lo, once(NKV, NKV))
            sp.dma_start(early[0], ctx_d[:, :, HR:2 * HR]).then_inc(ahead_in, 16)
            sp.dma_start(early[1], wv_d[:, :, 0:512]).then_inc(ahead_in, 16)

        def landed(nth, g=0):
            return half * (16 * USES) + g * 32 + nth * 16

        def landed_wo(g, last):
            return landed(3 if last else 4, g)

        @block.gpsimd
        def _(pool):
            nc.gpsimd.memset(raw(rinv_s[:]), 0.0).then_inc(rinv_clear, 1)
            for dst, src, hi, count, done in ((ctxT, early[0], ctx_hi, once(KT, 4), ctx_lo), (wa, early[1], wa_hi, once(KT, FILLS), wa_lo)):
                pool.wait_ge(hi, count)
                nc.gpsimd.tensor_tensor(dst[1][:, KT - 1, :], src[:, KT - 1, :], raw(dst[0][:, KT - 1, :]), ALU.subtract).then_inc(done, 1)

            def wq_lo(g, j):
                pool.wait_ge(ring_in[j], landed(1, g))
                pool.wait_ge(wa_hi, fill(g, j + 1))
                nc.gpsimd.tensor_tensor(wa[1][:, j, :], ring[:, j, :], raw(wa[0][:, j, :]), ALU.subtract).then_inc(wa_lo, 1)

            def body(g, first, last):
                for h in range(G):
                    pool.wait_ge(q_shift, head(g, G, h + 1))
                    nc.gpsimd.tensor_tensor(rope_b[:, h % 2, :].rearrange("p (b t) -> p b t", b=HB),
                                            rope_b[:, h % 2, :].rearrange("p (b t) -> p b t", b=HB),
                                            mem["sin_q"][:].unsqueeze(1).to_broadcast([P, HB, S]), ALU.mult).then_inc(q_sin, 1)
                    pool.wait_ge(q_sin, head(g, G, h + 1))
                    nc.gpsimd.tensor_tensor(rope_a[:, h % 2, :], rope_a[:, h % 2, :], rope_b[:, h % 2, :], ALU.add).then_inc(q_full, 1)
                if not last:
                    wq_lo(g + 1, 0)
                for b in range(HB):
                    pool.wait_ge(s_tanh, head(g, HB, b + 1))
                    nc.gpsimd.tensor_tensor(prob[:, b % 2, :].rearrange("p (h t) -> p h t", h=G),
                                            prob[:, b % 2, :].rearrange("p (h t) -> p h t", h=G),
                                            mem["mask_bias"][:].unsqueeze(1).to_broadcast([P, G, S]), ALU.add).then_inc(s_masked, 1)
                    if not last and b == 1:
                        wq_lo(g + 1, 1)
                if not last:
                    wq_lo(g + 1, 2)
                    wq_lo(g + 1, 3)
                for j in range(4):
                    pool.wait_ge(ring_in[j], landed_wo(g, last))
                    pool.wait_ge(wo_hi, fill(g, j + 1))
                    nc.gpsimd.tensor_tensor(wo[1][:, j, :], ring[:, j, :], raw(wo[0][:, j, :]), ALU.subtract).then_inc(wo_lo, 1)

            heads(pool, body)
            pool.wait_ge(ahead_in, once(32, 32))

        @block.scalar
        def _(act):
            def hi_of(dst, done, j, use, free=None):
                if free is not None:
                    act.wait_ge(*free)
                act.wait_ge(ring_in[j], use)
                nc.scalar.activation(dst[0][:, j, :], ring[:, j, :], ACT.Copy).then_inc(done, 1)

            def early_hi(dst, src, done):
                for j in range(KT):
                    nc.scalar.activation(dst[0][:, j, :], src[:, j, :], ACT.Copy).then_inc(done, 1)

            def rows_hi(b):
                act.wait_ge(xn_tr, once(b + 1, HB))
                nc.scalar.activation(xnT[0][:, :, b * S:(b + 1) * S], s_ps[b % 2][:].rearrange("p (k s) -> p k s", k=KT),
                                     ACT.Copy).then_inc(xn_hi, 1)

            def v_from(c, b):
                act.wait_ge(v_mm, once(4 * c + b + 1, 8))
                nc.scalar.activation(v_all[:, b, c * 512:(c + 1) * 512], proj_ps[b % 2][:], ACT.Copy).then_inc(v_out, 1)

            def wk_split(g):
                if not (isinstance(g, int) and g == 0):
                    act.wait_ge(k_mm, head(g, 1, 0))
                act.wait_ge(raw_k_in, head(g, 16, 16))
                nc.scalar.activation(wk[0][:], raw_k[:], ACT.Copy).then_inc(wk_hi, 1)

            act.wait_ge(rinv_clear, once(1, 1))
            early_hi(ctxT, early[0], ctx_hi)
            early_hi(wa, early[1], wa_hi)
            for j in range(4):
                if j == 1:
                    wk_split(0)
                hi_of(wo, wo_hi, j, landed(1))
                v_from(0, j)
            for b in range(HB):
                rows_hi(b)
                hi_of(wa, wa_hi, b, landed(2), (v_mm, once(4, 8)))

            def keys_hi(g):
                act.wait_ge(k_full, head(g, 1, 1))
                if not (isinstance(g, int) and g == 0):
                    act.wait_ge(s_mm, head(g, HB, 0))
                nc.scalar.activation(kT[0][:], rope_a[:, 1, :], ACT.Copy).then_inc(k_hi, 1)

            keys_hi(0)

            def inverse_hi(g):
                act.wait_ge(inv_done, head(g, 1, 1))
                nc.scalar.activation(rinv_s[0:HB, :], rinv[:], ACT.Copy).then_inc(inv_hi, 1)

            def norm_hi(g, b):
                act.wait_ge(o_norm, head(g, HB, b + 1))
                nc.scalar.activation(oT[0][:, b, :], o_raw[:, b, :], ACT.Copy).then_inc(o_hi, 1)

            def body(g, first, last):
                def queries_hi(h):
                    act.wait_ge(q_full, head(g, G, h + 1))
                    nc.scalar.activation(qT[0][:, h, :], rope_a[:, h % 2, :], ACT.Copy).then_inc(q_hi, 1)

                def shift(h):
                    act.wait_ge(q_mul, head(g, G, h + 1))
                    nc.scalar.activation(rope_b[0:64, h % 2, :], proj_ps[h % 2][64:128, :], ACT.Copy)
                    nc.scalar.activation(rope_b[64:128, h % 2, :], proj_ps[h % 2][0:64, :], ACT.Copy).then_inc(q_shift, 1)

                shift(0)
                if not first:
                    inverse_hi(g - 1)
                shift(1)
                queries_hi(0)
                shift(2)
                if not first:
                    norm_hi(g - 1, 0)
                queries_hi(1)
                if not first:
                    norm_hi(g - 1, 1)
                shift(3)
                queries_hi(2)
                queries_hi(3)
                if first:
                    for b in range(HB):
                        v_from(1, b)
                if not first:
                    norm_hi(g - 1, 2)
                    norm_hi(g - 1, 3)

                def wq_hi(j):
                    if not last:
                        hi_of(wa, wa_hi, j, landed(1, g + 1), (q_mm, head(g, G, G)))

                if not last:
                    wk_split(g + 1)
                wq_hi(0)
                wq_hi(1)

                def tanh(b):
                    act.wait_ge(s_mm, head(g, HB, b + 1))
                    if not (first and b < 2):
                        act.wait_ge(p_lo, head(g, HB, b - 1))
                    nc.scalar.activation(prob[:, b % 2, :], s_ps[b % 2][:], ACT.Tanh, scale=TANH_SCALE).then_inc(s_tanh, 1)

                def exp(b):
                    act.wait_ge(s_masked, head(g, HB, b + 1))
                    nc.scalar.activation(prob[:, b % 2, :], prob[:, b % 2, :], ACT.Exp, scale=CAP).then_inc(p_exp, 1)
                    act.wait_ge(p_exp, head(g, HB, b + 1))
                    if not (first and b < 2):
                        act.wait_ge(o_mm, head(g, HB, b - 1))
                    nc.scalar.activation(pT[0][:, b % 2, :], prob[:, b % 2, :], ACT.Copy).then_inc(p_hi, 1)

                def out(b):
                    act.wait_ge(o_mm, head(g, HB, b + 1))
                    if not first:
                        act.wait_ge(o_lo, head(g, HB, b + 1 - HB))
                    nc.scalar.activation(o_raw[:, b, :], out_ps[b % 2][:], ACT.Copy).then_inc(o_out, 1)

                def split_wo(j):
                    hi_of(wo, wo_hi, j, landed_wo(g, last), (v_mm, once(8, 8)) if first else (y_mm, head(g, HB, 0)))

                tanh(0)
                tanh(1)
                exp(0)
                exp(1)
                wq_hi(2)
                wq_hi(3)
                tanh(2)
                tanh(3)
                exp(2)
                out(0)
                exp(3)
                out(1)
                split_wo(0)
                split_wo(1)
                if not last:
                    keys_hi(g + 1)
                out(2)
                split_wo(2)
                out(3)
                split_wo(3)

            heads(act, body)
            inverse_hi(NKV - 1)
            for b in range(HB):
                norm_hi(NKV - 1, b)

        @block.vector
        def _(dve):
            def early_lo(dst, src, hi, count, done):
                for j in range(KT - 1):
                    dve.wait_ge(hi, count + j)
                    nc.vector.tensor_tensor(dst[1][:, j, :], src[:, j, :], raw(dst[0][:, j, :]), ALU.subtract).then_inc(done, 1)

            def lo_of(dst, hi, done, j, use, count):
                dve.wait_ge(ring_in[j], use)
                dve.wait_ge(hi, count)
                nc.vector.tensor_tensor(dst[1][:, j, :], ring[:, j, :], raw(dst[0][:, j, :]), ALU.subtract).then_inc(done, 1)

            def wk_lo_of(g):
                dve.wait_ge(wk_hi, head(g, 1, 1))
                nc.vector.tensor_tensor(wk[1][:], raw_k[:], raw(wk[0][:]), ALU.subtract).then_inc(wk_lo, 1)

            early_lo(ctxT, early[0], ctx_hi, once(1, 4), ctx_lo)
            early_lo(wa, early[1], wa_hi, once(1, FILLS), wa_lo)
            for b in range(HB):
                nc.vector.tensor_scalar(xn[:, b:b + 1, :], mem["x_acc"][:, bass.ds(half * HB + b, 1), :],
                                        mem["mv"][:].rearrange("p b s -> p (b s)")[:, bass.ds((half * HB + b) * 2, 1)],
                                        mem["rstd"][:, bass.ds(half * HB + b, 1)], ALU.subtract, ALU.mult).then_inc(xn_done, 1)
            for j in range(4):
                lo_of(wo, wo_hi, wo_lo, j, landed(1), once(j + 1, FILLS))
            wk_lo_of(0)
            for b in range(HB):
                dve.wait_ge(xn_hi, once(b + 1, HB))
                nc.vector.tensor_tensor(xnT[1][:, :, b * S:(b + 1) * S], s_ps[b % 2][:].rearrange("p (k s) -> p k s", k=KT),
                                        raw(xnT[0][:, :, b * S:(b + 1) * S]), ALU.subtract).then_inc(xn_lo, 1)
                lo_of(wa, wa_hi, wa_lo, b, landed(2), fill(0, b + 1))

            def reciprocal(g):
                dve.wait_ge(sum_mm, head(g, 1, 1))
                nc.vector.reciprocal(rinv[:], sum_ps[0:HB, :]).then_inc(inv_done, 1)

            def inverse_lo(g):
                dve.wait_ge(inv_hi, head(g, 1, 1))
                nc.vector.tensor_tensor(rinv_s[RL:RL + HB, :], rinv[:], raw(rinv_s[0:HB, :]), ALU.subtract).then_inc(inv_lo, 1)

            def rotary(slot, src, cos, sin, done):
                a = rope_a[:, slot, :].rearrange("p (b t) -> p b t", b=HB)
                r = rope_b[:, slot, :].rearrange("p (b t) -> p b t", b=HB)
                s = src[:].rearrange("p (b t) -> p b t", b=HB)
                wide = lambda t, lo, hi: t[lo:hi, :].unsqueeze(1).to_broadcast([hi - lo, HB, S])
                nc.vector.tensor_tensor(a, s, wide(cos, 0, P), ALU.mult)
                nc.vector.tensor_tensor(r[0:64], s[64:128], wide(sin, 0, 64), ALU.mult)
                nc.vector.tensor_tensor(r[64:128], s[0:64], wide(sin, 64, 128), ALU.mult).then_inc(done, 1)

            def cosine(h):
                nc.vector.tensor_tensor(rope_a[:, h % 2, :].rearrange("p (b t) -> p b t", b=HB),
                                        proj_ps[h % 2][:].rearrange("p (b t) -> p b t", b=HB),
                                        mem["cos_q"][:].unsqueeze(1).to_broadcast([P, HB, S]), ALU.mult).then_inc(q_mul, 1)

            def norm(g, b):
                dve.wait_ge(rinv_mm, head(g, HB, b + 1))
                dve.wait_ge(o_out, head(g, HB, b + 1))
                nc.vector.tensor_tensor(o_raw[:, b, :], o_raw[:, b, :], rinv_ps[b][:], ALU.mult).then_inc(o_norm, 1)

            def norm_lo(g, b):
                dve.wait_ge(o_hi, head(g, HB, b + 1))
                nc.vector.tensor_tensor(oT[1][:, b, :], o_raw[:, b, :], raw(oT[0][:, b, :]), ALU.subtract).then_inc(o_lo, 1)

            def add_y(g, b):
                dve.wait_ge(y_mm, head(g, HB, b + 1))
                nc.vector.tensor_tensor(mem["x_acc"][:, bass.ds(half * HB + b, 1), :], mem["x_acc"][:, bass.ds(half * HB + b, 1), :],
                                        y_ps[b % 2][:].unsqueeze(1), ALU.add).then_inc(y_add, 1)

            def keys(g):
                dve.wait_ge(k_mm, head(g, 1, 1))
                if not (isinstance(g, int) and g == 0):
                    dve.wait_ge(q_lo, head(g, G, 0))
                rotary(1, k_ps, mem["cos_k"], mem["sin_k"], k_mul)

            def keys_add(g):
                dve.wait_ge(k_mul, head(g, 1, 1))
                nc.vector.tensor_tensor(rope_a[:, 1, :], rope_a[:, 1, :], rope_b[:, 1, :], ALU.add).then_inc(k_full, 1)

            def keys_lo(g):
                dve.wait_ge(k_hi, head(g, 1, 1))
                nc.vector.tensor_tensor(kT[1][:], rope_a[:, 1, :], raw(kT[0][:]), ALU.subtract).then_inc(k_lo, 1)

            keys(0)
            keys_add(0)

            def body(g, first, last):
                def queries(h):
                    dve.wait_ge(q_mm, head(g, G, h + 1))
                    if h >= 2:
                        dve.wait_ge(q_lo, head(g, G, h - 1))
                    elif h == 1:
                        dve.wait_ge(k_lo, head(g, 1, 1))
                    cosine(h)

                def queries_lo(h):
                    dve.wait_ge(q_hi, head(g, G, h + 1))
                    nc.vector.tensor_tensor(qT[1][:, h, :], rope_a[:, h % 2, :], raw(qT[0][:, h, :]), ALU.subtract).then_inc(q_lo, 1)

                def weights_lo(b):
                    dve.wait_ge(p_hi, head(g, HB, b + 1))
                    nc.vector.tensor_tensor(pT[1][:, b % 2, :], prob[:, b % 2, :], raw(pT[0][:, b % 2, :]), ALU.subtract).then_inc(p_lo, 1)

                if not first:
                    reciprocal(g - 1)
                queries(0)
                keys_lo(g)
                if not first:
                    dve.wait_ge(o_mm, head(g, HB, 0))
                else:
                    dve.wait_ge(v_out, once(4, 8))
                nc.vector.tensor_scalar(vg[0][:], v_all[:, :, bass.ds(g * DH, DH)], 1.0, None, ALU.mult).then_inc(vg_hi, 1)
                queries(1)
                if not first:
                    inverse_lo(g - 1)
                queries_lo(0)
                queries(2)
                if not first:
                    norm(g - 1, 0)
                    norm(g - 1, 1)
                    norm_lo(g - 1, 0)
                queries_lo(1)
                queries(3)
                if not first:
                    norm_lo(g - 1, 1)
                queries_lo(2)
                if not first:
                    norm(g - 1, 2)
                    norm(g - 1, 3)
                queries_lo(3)
                if not first:
                    norm_lo(g - 1, 2)
                    add_y(g - 1, 0)
                    norm_lo(g - 1, 3)
                    add_y(g - 1, 1)
                dve.wait_ge(vg_hi, head(g, 1, 1))
                nc.vector.tensor_tensor(vg[1][:], v_all[:, :, bass.ds(g * DH, DH)], raw(vg[0][:]), ALU.subtract).then_inc(vg_lo, 1)
                if not last:
                    wk_lo_of(g + 1)
                weights_lo(0)
                weights_lo(1)
                if not first:
                    add_y(g - 1, 2)
                    add_y(g - 1, 3)
                weights_lo(2)
                weights_lo(3)
                if not last:
                    keys(g + 1)
                    keys_add(g + 1)

            heads(dve, body)
            g = NKV - 1
            reciprocal(g)
            inverse_lo(g)
            for b in range(HB):
                norm(g, b)
            for b in range(HB):
                norm_lo(g, b)
            for b in range(HB):
                add_y(g, b)
                dve.wait_ge(y_add, head(g, HB, b + 1))
                take_statistics(nc, mem, bass.ds(half * HB + b, 1))

        @block.tensor
        def _(pe):
            def product(out, w, x, wsl, xsl):
                n = 0
                for k in range(KT):
                    for a, c in split_passes(w[0], w[1], x[0], x[1]):
                        last = nc.tensor.matmul(out, wsl(a, k), xsl(c, k), start=(n == 0), stop=(n == 3 * KT - 1))
                        n += 1
                return last

            def turn_rows(b):
                pe.wait_ge(xn_done, once(b + 1, HB))
                if b >= 2:
                    pe.wait_ge(xn_lo, once(b - 1, HB))
                for k in range(KT):
                    last = nc.tensor.transpose(s_ps[b % 2][:, k * S:(k + 1) * S], xn[:, b, k * P:(k + 1) * P], mem["ident"][:])
                last.then_inc(xn_tr, 1)

            def values(c):
                if c == 0:
                    pe.wait_ge(ctx_lo, once(4, 4))
                pe.wait_ge((wa_hi, wo_hi)[c], once(4, FILLS))
                pe.wait_ge((wa_lo, wo_lo)[c], once(4, FILLS))
                for b in range(HB):
                    if b >= 2:
                        pe.wait_ge(v_out, once(4 * c + b - 1, 8))
                    elif c == 1:
                        pe.wait_ge(q_shift, head(0, G, 3 + b))
                    product(proj_ps[b % 2][:], ctxT, (wa, wo)[c], lambda a, k: a[:, k, b * S:(b + 1) * S], lambda a, k: a[:, k, :]).then_inc(v_mm, 1)

            def y_of(g, b, first, last):
                pe.wait_ge(o_lo, head(g, HB, b + 1))
                if b == 0:
                    pe.wait_ge(wo_hi, fill(g, 4))
                    pe.wait_ge(wo_lo, fill(g, 4))
                if b >= 2:
                    pe.wait_ge(y_add, head(g, HB, b - 1))
                n = 0
                for h in range(G):
                    for a, c in split_passes(oT[0], oT[1], wo[0], wo[1]):
                        last_mm = nc.tensor.matmul(y_ps[b % 2][:], a[:, b, h * S:(h + 1) * S], c[:, h, :],
                                                   start=(n == 0), stop=(n == 3 * G - 1))
                        n += 1
                last_mm.then_inc(y_mm, 1)

            def keys(g):
                pe.wait_ge(wk_lo, head(g, 1, 1))
                if not (isinstance(g, int) and g <= 1):
                    pe.wait_ge(y_add, head(g - 1, HB, 0))
                product(k_ps[:], wk, ctxT, lambda a, k: a[:, k, :], lambda a, k: a[:, k, :]).then_inc(k_mm, 1)

            def inverses(g):
                pe.wait_ge(inv_lo, head(g, 1, 1))
                pe.wait_ge(o_out, head(g, HB, HB))
                if not (isinstance(g, int) and g == NKV - 1):
                    pe.wait_ge(k_mul, head(g + 1, 1, 1))
                for b in range(HB):
                    nc.tensor.matmul(rinv_ps[b][:], mem["row"][:, b, :], rinv_s[:], start=True, stop=True).then_inc(rinv_mm, 1)

            values(0)
            for b in range(HB):
                turn_rows(b)
            keys(0)
            pe.wait_ge(xn_lo, once(HB, HB))

            def body(g, first, last):
                pe.wait_ge(wa_hi, fill(g, 4))
                pe.wait_ge(wa_lo, fill(g, 4))
                for h in range(G):
                    if h == 3 and not first:
                        inverses(g - 1)
                    if h >= 2 or not first:
                        pe.wait_ge(q_shift, head(g, G, h - 1))
                        if h == 1:
                            pe.wait_ge(o_out, head(g, HB, 0))
                    else:
                        pe.wait_ge(v_out, once(3 + h, 8))
                    product(proj_ps[h % 2][:], wa, xnT, lambda a, k: a[:, k, h * DH:(h + 1) * DH], lambda a, k: a[:, k, :]).then_inc(q_mm, 1)

                def scores(b):
                    if b == 0:
                        pe.wait_ge(k_lo, head(g, 1, 1))
                        pe.wait_ge(q_lo, head(g, G, G))
                    if b >= 2 or not first:
                        pe.wait_ge(s_tanh, head(g, HB, b - 1))
                    for n, (a, c) in enumerate(split_passes(kT[0], kT[1], qT[0], qT[1])):
                        last = nc.tensor.matmul(s_ps[b % 2][:], a[:, b * S:(b + 1) * S], c[:, :, b * S:(b + 1) * S],
                                                start=(n == 0), stop=(n == 2))
                    last.then_inc(s_mm, 1)

                def outputs(b):
                    pe.wait_ge(p_lo, head(g, HB, b + 1))
                    if b == 0:
                        pe.wait_ge(vg_lo, head(g, 1, 1))
                    if b == 1:
                        pe.wait_ge(*((v_out, once(8, 8)) if first else (q_shift, head(g, G, G))))
                    elif b >= 2:
                        pe.wait_ge(o_out, head(g, HB, b - 1))
                    for n, part in enumerate((pT[1], pT[0])):
                        last = nc.tensor.matmul(sum_ps[:], mem["pick"][:, b, :], part[:, b % 2, :],
                                                start=(b == 0 and n == 0), stop=(b == HB - 1 and n == 1))
                    if b == HB - 1:
                        last.then_inc(sum_mm, 1)
                    for n, (a, c) in enumerate(split_passes(vg[0], vg[1], pT[0], pT[1])):
                        last = nc.tensor.matmul(out_ps[b % 2][:], a[:, b, :], c[:, b % 2, :], start=(n == 0), stop=(n == 2))
                    last.then_inc(o_mm, 1)

                if not first:
                    y_of(g - 1, 0, False, last)
                    y_of(g - 1, 1, False, last)
                if first:
                    values(1)
                scores(0)
                scores(1)
                if not first:
                    y_of(g - 1, 2, False, last)
                scores(2)
                scores(3)
                if not first:
                    y_of(g - 1, 3, False, last)
                outputs(0)
                outputs(1)
                if not last:
                    keys(g + 1)
                outputs(2)
                outputs(3)

            heads(pe, body)
            pe.wait_ge(y_add, once(HB * (NKV - 1), HB * NKV))
            inverses(NKV - 1)
            for b in range(HB):
                y_of(NKV - 1, b, False, True)


def normalised_columns(nc, mem, xn, xnT, banks, sem, ln_sems, in_block):
    xn_done, xn_tr, xn_hi, xn_lo = (sem(n) for n in ("xn_done", "xn_tr", "xn_hi", "xn_lo"))
    ln_vector, ln_pool = row_statistics(nc, mem, ln_sems, in_block)
    columns = lambda part, b: part[:, :, b * S:(b + 1) * S]
    bank = lambda b: banks[b % 2][:].rearrange("p (k s) -> p k s", k=KT)

    def vector(dve, between=lambda b: None, meanwhile=lambda: None):
        ln_vector(dve)
        meanwhile()
        dve.wait_ge(ln_sems[3], 1)

        def lo(b):
            dve.wait_ge(xn_hi, b + 1)
            nc.vector.tensor_tensor(columns(xnT[1], b), bank(b), raw(columns(xnT[0], b)), ALU.subtract).then_inc(xn_lo, 1)
            between(b)

        for b in range(B):
            nc.vector.tensor_scalar(xn[:, b, :], mem["x_acc"][:, b, :], mem["mv"][:, b, 0:1], mem["rstd"][:, b:b + 1],
                                    ALU.subtract, ALU.mult).then_inc(xn_done, 1)
            if b >= 2:
                lo(b - 2)
        lo(B - 2)
        lo(B - 1)

    def scalar(act, between=lambda b: None):
        for b in range(B):
            act.wait_ge(xn_tr, b + 1)
            nc.scalar.activation(columns(xnT[0], b), bank(b), ACT.Copy).then_inc(xn_hi, 1)
            between(b)

    def tensor(pe, between=lambda b: None):
        for b in range(B):
            pe.wait_ge(xn_done, b + 1)
            if b >= 2:
                pe.wait_ge(xn_lo, b - 1)
            for k in range(KT):
                last = nc.tensor.transpose(banks[b % 2][:, k * S:(k + 1) * S], xn[:, b, k * P:(k + 1) * P], mem["ident"][:])
            last.then_inc(xn_tr, 1)
            between(b)

    return vector, ln_pool, scalar, tensor, xn_done, xn_lo


FF = 1792
FG = 2
NG = FF // (P * FG)


def layer0_ffn(nc, io, mem):
    WHOLE = 4096.0
    with ExitStack() as ctx:
        sb = lambda name, shape, dt=F32: ctx.enter_context(nc.sbuf_tensor(f"ffn_{name}", shape, dt))
        ps = lambda name: ctx.enter_context(nc.psum_tensor(f"ffn_{name}", [P, 512], F32))
        sem = stage_semaphores(nc, ctx, "ffn_")
        FW = FG * P
        xnT = [sb(f"xnT_{n}", [P, KT, B * S], F32R) for n in ("hi", "lo")]
        w_raw = {"gate": sb("gate_raw", [P, KT, FW], I32), "up": sb("up_raw", [P, KT, FW], I32), "down": sb("down_raw", [P, FG, D], I32)}
        w = {n: [sb(f"{n}_{part}", list(w_raw[n].shape), F32R) for part in ("hi", "lo")] for n in w_raw}
        y_acc = sb("y_acc", [P, B, D])
        hT = [sb(f"hT_{n}", [P, FG, B * S], F32R) for n in ("hi", "lo")]
        silu = sb("silu", [P, 2, HR])
        hidden = sb("hidden", [P, 2, HR])
        scales = sb("scales", [P, NG, 2 * FG])
        now = sb("now", [P, 2 * FG])
        down_s = sb("down_s", [P, D])
        peak = sb("peak", [P, len(w)])
        large = sb("large", [P, len(w)])
        ones = sb("ones", [P, P])
        flag = sb("flag", [1, 1], I32)
        flag_ps = ctx.enter_context(nc.psum_tensor("ffn_flag_ps", [P, len(w)], F32))
        qk_raw = sb("qk_raw", [P, 2, E1])
        qk_wide = sb("qk_wide", [P, 4, 4, 32])
        wv_raw = sb("wv_raw", [P, E1])
        qk_in, wide_set, wide, qk_hi, wv_hi, next_in = (sem(n) for n in ("qk_in", "wide_set", "wide", "qk_hi", "wv_hi", "next_in"))
        xn = y_acc
        gate_ps, up_ps, y_ps = ([ps(f"{n}{i}_ps") for i in range(2)] for n in ("gate", "up", "y"))
        ln_sems = [sem(n) for n in ("stat", "aggr", "eps_added", "rstd_done")]
        y_banks = y_ps + [gate_ps[1], up_ps[1]]
        vector_ln, pool_ln, scalar_ln, tensor_ln, _, xn_lo = normalised_columns(nc, mem, xn, xnT, y_ps, sem, ln_sems, False)
        w_in = {n: sem(f"{n}_in") for n in w}
        w_hi = {n: sem(f"{n}_hi") for n in w}
        w_lo = {n: sem(f"{n}_lo") for n in w}
        (scales_in, down_s_in, now_set, gu_mm, silu_done, h_full, h_hi, h_lo, y_mm, y_add, sums_scaled, sums_added, x_done, ones_set, peaks, large_set, flag_mm, flag_set) = [sem(n) for n in (
            "scales_in down_s_in now_set gu_mm silu_done h_full h_hi h_lo y_mm y_add sums_scaled sums_added x_done ones_set peaks large_set flag_mm flag_set").split()]
        block = ctx.enter_context(nc.Block())

        def groups(eng, body, extra=lambda: None):
            body(0, True, False)
            extra()
            with eng.Fori(1, NG - 1) as i:
                body(i, False, False)
            body(NG - 1, False, True)

        gate_d = io["gate_t"].rearrange("(k p) f -> p k f", p=P)
        up_d = io["up_t"].rearrange("(k p) f -> p k f", p=P)
        down_d = io["down_t"].rearrange("(k p) n -> p k n", p=P)

        @block.sync
        def _(sp):
            sp.dma_start(w_raw["gate"][:], gate_d[:, :, 0:FW]).then_inc(w_in["gate"], 16)
            sp.dma_start(w_raw["up"][:], up_d[:, :, 0:FW]).then_inc(w_in["up"], 16)
            sp.dma_start(w_raw["down"][:], down_d[:, 0:FG, :]).then_inc(w_in["down"], 16)
            sp.dma_start(scales[:], io["gu_s"].rearrange("p (i s) -> p i s", i=NG)).then_inc(scales_in, 16)
            sp.dma_start(down_s[:], io["down_s"].rearrange("(o n) -> o n", o=1).to_broadcast([P, D])).then_inc(down_s_in, 16)
            sp.dma_start(qk_raw[:], io["qk1_t"]).then_inc(qk_in, 16)
            sp.dma_start(wv_raw[:], io["wv1_t"]).then_inc(qk_in, 16)
            with sp.Fori(0, NG - 1) as i:
                for name, src in (("gate", gate_d[:, :, bass.ds(i * FW + FW, FW)]), ("up", up_d[:, :, bass.ds(i * FW + FW, FW)]),
                                  ("down", down_d[:, bass.ds(i * FG + FG, FG), :])):
                    sp.wait_ge(w_lo[name], i + 1)
                    sp.dma_start(w_raw[name][:], src).then_inc(w_in[name], 16)
            sp.dma_start(mem["qk_bias"][:], io["qk1_bias"]).then_inc(next_in, 16)
            sp.dma_start(mem["bv"][:], io["bv1"].rearrange("(o n) -> o n", o=1).to_broadcast([P, E1])).then_inc(next_in, 16)
            sp.dma_start(mem["own"][:], io["own"]).then_inc(next_in, 16)
            sp.dma_start(mem["seen_all"][:].rearrange("p b n -> p (b n)"),
                         io["key_mask"].rearrange("b o n -> (b o n)").rearrange("(o n) -> o n", o=1).to_broadcast([P, B * D])).then_inc(next_in, 16)
            sp.wait_ge(next_in, 64)

        @block.gpsimd
        def _(pool):
            nc.gpsimd.memset(ones[:], 1.0).then_inc(ones_set, 1)
            pool_ln(pool)
            nc.gpsimd.memset(qk_wide[:], 0.0).then_inc(wide_set, 1)
            pool.wait_ge(down_s_in, 16)
            for b in range(B):
                pool.wait_ge(y_add, (NG - 2) * B + (b + 1))
                nc.gpsimd.tensor_tensor(y_acc[:, b, :], y_acc[:, b, :], down_s[:], ALU.mult).then_inc(sums_scaled, 1)
                pool.wait_ge(sums_scaled, b + 1)
                nc.gpsimd.tensor_tensor(mem["x_acc"][:, b, :], mem["x_acc"][:, b, :], y_acc[:, b, :], ALU.add).then_inc(sums_added, 1)
            for b in range(B):
                pool.wait_ge(y_add, (NG - 1) * B + (b + 1))
                pool.wait_ge(sums_added, b + 1)
                nc.gpsimd.tensor_tensor(mem["x_acc"][:, b, :], mem["x_acc"][:, b, :], y_acc[:, b, :], ALU.add).then_inc(x_done, 1)

        @block.scalar
        def _(act):
            def split(name, i):
                act.wait_ge(w_in[name], i * 16 + 16)
                nc.scalar.activation(w[name][0][:], w_raw[name][:], ACT.Copy).then_inc(w_hi[name], 1)

            scalar_ln(act, lambda b: split(list(w)[b - 1], 0) if 1 <= b <= len(w) else None)

            def body(i, first, last):
                act.wait_ge(now_set, i + 1)

                def gate(n):
                    act.wait_ge(gu_mm, i * 4 + (n + 1))
                    if n >= 2 or not first:
                        act.wait_ge(h_full, i * 4 + (n - 1))
                    t = n % 2
                    nc.scalar.activation(silu[:, n % 2, :], gate_ps[n % 2][:], ACT.Silu, scale=now[:, t:t + 1]).then_inc(silu_done, 1)

                def hi(n):
                    r, t = n // 2, n % 2
                    act.wait_ge(h_full, i * 4 + (n + 1))
                    if not first:
                        act.wait_ge(y_mm, i * B + (HB * (r + 1) - B))
                    nc.scalar.activation(hT[0][:, t, r * HR:(r + 1) * HR], hidden[:, n % 2, :], ACT.Copy).then_inc(h_hi, 1)

                gate(0)
                gate(1)
                hi(0)
                gate(2)
                hi(1)
                gate(3)
                hi(2)
                hi(3)
                if not last:
                    act.wait_ge(gu_mm, i * 4 + 4)
                    split("gate", i + 1)
                    split("up", i + 1)
                    act.wait_ge(y_mm, i * B + B)
                    split("down", i + 1)

            def projections():
                act.wait_ge(wide, 2)
                nc.scalar.activation(mem["qk_s"][0][:], qk_wide[:].rearrange("p a t e -> p a (t e)"), ACT.Copy).then_inc(qk_hi, 1)
                nc.scalar.activation(mem["wv_s"][0][:], wv_raw[:], ACT.Copy).then_inc(wv_hi, 1)
            groups(act, body, projections)

        @block.vector
        def _(dve):
            def split(name, i):
                dve.wait_ge(w_hi[name], i + 1)
                nc.vector.tensor_tensor(w[name][1][:], w_raw[name][:], raw(w[name][0][:]), ALU.subtract).then_inc(w_lo[name], 1)

            def measure(i, n):
                name = list(w)[n]
                if n == 0 and not (isinstance(i, int) and i == 0):
                    dve.wait_ge(large_set, i)
                dve.wait_ge(w_in[name], i * 16 + 16)
                nc.vector.tensor_reduce(peak[:, n:n + 1], w_raw[name][:], AX.XY, ALU.max, apply_absolute_value=True).then_inc(peaks, 1)

            def compare(i):
                if not (isinstance(i, int) and i == 0):
                    dve.wait_ge(flag_mm, i)
                dve.wait_ge(peaks, i * len(w) + len(w))
                nc.vector.tensor_scalar(large[:], peak[:], WHOLE, None, ALU.is_gt).then_inc(large_set, 1)

            def set_flag(i):
                dve.wait_ge(flag_mm, i + 1)
                nc.vector.tensor_reduce(flag[:], flag_ps[0:1, :], AX.X, ALU.max).then_inc(flag_set, 1)

            def first_group(b):
                if 1 <= b <= len(w):
                    measure(0, b - 1)
                    split(list(w)[b - 1], 0)

            vector_ln(dve, first_group)
            compare(0)
            set_flag(0)
            dve.wait_ge(scales_in, 16)

            def body(i, first, last):
                nc.vector.tensor_scalar(now[:].unsqueeze(1), scales[:, bass.ds(i, 1), :] if not isinstance(i, int) else scales[:, i:i + 1, :],
                                        1.0, None, ALU.mult).then_inc(now_set, 1)
                dve.wait_ge(now_set, i + 1)

                def product(n):
                    dve.wait_ge(silu_done, i * 4 + (n + 1))
                    if n >= 2 or not first:
                        dve.wait_ge(h_lo, i * 4 + (n - 1))
                    t = n % 2
                    nc.vector.scalar_tensor_tensor(hidden[:, n % 2, :], up_ps[n % 2][:], now[:, FG + t:FG + t + 1], silu[:, n % 2, :],
                                                   ALU.mult, ALU.mult).then_inc(h_full, 1)

                def lo(n):
                    r, t = n // 2, n % 2
                    dve.wait_ge(h_hi, i * 4 + (n + 1))
                    nc.vector.tensor_tensor(hT[1][:, t, r * HR:(r + 1) * HR], hidden[:, n % 2, :],
                                            raw(hT[0][:, t, r * HR:(r + 1) * HR]), ALU.subtract).then_inc(h_lo, 1)

                product(0)
                if not last:
                    measure(i + 1, 0)
                product(1)
                lo(0)
                if not last:
                    measure(i + 1, 1)
                product(2)
                lo(1)
                if not last:
                    measure(i + 1, 2)
                    compare(i + 1)
                product(3)
                lo(2)
                lo(3)

                def finish(b):
                    dve.wait_ge(x_done, b + 1)
                    take_statistics(nc, mem, slice(b, b + 1))

                for b in range(B):
                    dve.wait_ge(y_mm, i * B + (b + 1))
                    if first:
                        nc.vector.tensor_copy(y_acc[:, b, :], y_banks[b % 4][:]).then_inc(y_add, 1)
                    elif last:
                        dve.wait_ge(down_s_in, 16)
                        dve.wait_ge(sums_added, b + 1)
                        nc.vector.tensor_tensor(y_acc[:, b, :], y_banks[b % 4][:], down_s[:], ALU.mult).then_inc(y_add, 1)
                    else:
                        nc.vector.tensor_tensor(y_acc[:, b, :], y_acc[:, b, :], y_banks[b % 4][:], ALU.add).then_inc(y_add, 1)
                    if last and b >= 2:
                        finish(b - 2)
                    if b == 1 and not last:
                        split("gate", i + 1)
                    if b == 3 and not last:
                        split("up", i + 1)
                        set_flag(i + 1)
                if not last:
                    split("down", i + 1)
                if last:
                    finish(B - 2)
                    finish(B - 1)

            def projections():
                dve.wait_ge(qk_in, 32)
                dve.wait_ge(wide_set, 1)
                for n in range(2):
                    nc.vector.tensor_copy(qk_wide[:, 2 * n:2 * n + 2, 0:3, :],
                                          qk_raw[:, n, :].rearrange("p (g e) -> p g e", g=2).unsqueeze(2).to_broadcast([P, 2, 3, 32])).then_inc(wide, 1)
                dve.wait_ge(qk_hi, 1)
                nc.vector.tensor_tensor(mem["qk_s"][1][:], qk_wide[:].rearrange("p a t e -> p a (t e)"), raw(mem["qk_s"][0][:]), ALU.subtract)
                dve.wait_ge(wv_hi, 1)
                nc.vector.tensor_tensor(mem["wv_s"][1][:], wv_raw[:], raw(mem["wv_s"][0][:]), ALU.subtract)
            groups(dve, body, projections)

        @block.tensor
        def _(pe):
            tensor_ln(pe)

            def count_large(i):
                pe.wait_ge(large_set, i + 1)
                nc.tensor.matmul(flag_ps[:], ones[:], large[:], start=True, stop=True).then_inc(flag_mm, 1)

            pe.wait_ge(ones_set, 1)
            count_large(0)
            pe.wait_ge(xn_lo, HB)

            def product(out, operands, low_parts, opened, stop=True):
                passes = []
                for (w_hi_, w_lo_), (x_hi_, x_lo_), stationary_w in operands:
                    passes.append((w_hi_, x_hi_) if stationary_w else (x_hi_, w_hi_))
                    passes.append((w_hi_, x_lo_) if stationary_w else (x_lo_, w_hi_))
                    if low_parts:
                        passes.append((w_lo_, x_hi_) if stationary_w else (x_hi_, w_lo_))
                for n, (a, c) in enumerate(passes):
                    if n or not opened:
                        last_mm = nc.tensor.matmul(out, a, c, start=(n == 0), stop=(n == len(passes) - 1))
                return last_mm

            def body(i, first, last):
                pe.wait_ge(w_lo["gate"], i + 1)
                pe.wait_ge(w_lo["up"], i + 1)

                def into(name, n):
                    r, t = n // 2, n % 2
                    cut = lambda part, k: part[:, k, t * P:(t + 1) * P]
                    rows = lambda part, k: part[:, k, r * HR:(r + 1) * HR]
                    return [((cut(w[name][0], k), cut(w[name][1], k)), (rows(xnT[0], k), rows(xnT[1], k)), True) for k in range(KT)]

                def back(b):
                    cut = lambda part, t: part[:, t, b * S:(b + 1) * S]
                    return [((w["down"][0][:, t, :], w["down"][1][:, t, :]), (cut(hT[0], t), cut(hT[1], t)), False) for t in range(FG)]

                def hidden_products(low_parts):
                    for n in range(4):
                        if n >= 2 or (n == 1 and not first):
                            pe.wait_ge(h_full, i * 4 + (n - 1))
                        if n == 2 and first:
                            pe.wait_ge(xn_lo, B)
                        if n == 1 and not first:
                            pe.wait_ge(y_add, i * B)
                        for name, bank in (("gate", gate_ps), ("up", up_ps)):
                            last_mm = product(bank[n % 2][:], into(name, n), low_parts, opened=(n == 0 and name == "gate"))
                        last_mm.then_inc(gu_mm, 1)

                def down_products(low_parts):
                    for b in range(B):
                        if b == HB:
                            pe.wait_ge(h_lo, i * 4 + 4)
                        if b == 1 and not first:
                            pe.wait_ge(y_add, i * B - 2)
                        elif b == 2:
                            pe.wait_ge(h_full, i * 4 + 4)
                        elif b >= 4:
                            pe.wait_ge(y_add, i * B + (b - 3))
                        product(y_banks[b % 4][:], back(b), low_parts, opened=(b == 0)).then_inc(y_mm, 1)

                if not first:
                    pe.wait_ge(h_full, i * 4 - 1)
                pe.wait_ge(flag_set, i + 1)
                a, c = into("gate", 0)[0][0][0], into("gate", 0)[0][1][0]
                nc.tensor.matmul(gate_ps[0][:], a, c, start=True, stop=False)
                has_low = pe.value_load(flag[0:1, 0:1])
                with pe.If(has_low > 0):
                    hidden_products(True)
                with pe.Else():
                    hidden_products(False)
                if not last:
                    count_large(i + 1)
                pe.wait_ge(w_lo["down"], i + 1)
                pe.wait_ge(h_lo, i * 4 + 2)
                if not first:
                    pe.wait_ge(y_add, i * B - 3)
                c, a = back(0)[0][0][0], back(0)[0][1][0]
                nc.tensor.matmul(y_ps[0][:], a, c, start=True, stop=False)
                with pe.If(has_low > 0):
                    down_products(True)
                with pe.Else():
                    down_products(False)
            groups(pe, body)


H1, DH1 = 8, 8
E1 = H1 * DH1
NP = D // P
HG = 4
PICKED = 3
VW = 32
NO_KEY = 1e9 * 8 ** 0.5


def layer1_attention(nc, io, mem):
    with ExitStack() as ctx:
        sb = lambda name, shape, dt=F32: ctx.enter_context(nc.sbuf_tensor(f"att_{name}", shape, dt))
        ps = lambda name, shape, dt=F32: ctx.enter_context(nc.psum_tensor(f"att_{name}", shape, dt))
        sem = stage_semaphores(nc, ctx, "att_")
        BF16 = mybir.dt.bfloat16
        ctx_raw = sb("ctx_raw", [P, D])
        ctx_s = [sb(f"ctx_{n}", [P, D], F32R) for n in ("hi", "lo")]
        xn = sb("xn", [P, 1, D])
        xn_s = [sb(f"xn_{n}", [P, D], F32R) for n in ("hi", "lo")]
        seen = sb("seen", [P, 1, D])
        qk_s, wv_s, bias, bv, own = (mem[n] for n in ("qk_s", "wv_s", "qk_bias", "bv", "own"))
        q_full = sb("q_full", [P, 2, D])
        k_full = sb("k_full", [P, 2, D])
        k_s = sb("k_s", [P, 2, D], F32R)
        v_full = sb("v_full", [P, NP, H1, DH1])
        v_rest = sb("v_rest", [P, NP, H1, DH1])
        q_s = [sb(f"q_s{u}", [P, 2, D], F32R) for u in range(2)]
        k_own = [sb(f"k_own{u}", [P, 2, NP, HG, P], F32R) for u in range(2)]
        vT = sb("vT", [P, 2, NP, H1, VW], BF16)
        top = sb("top", [P, 2, H1])
        prob = sb("prob", [P, 2, H1, P])
        pT = [sb(f"pT_{n}", [P, 2, H1, P], F16) for n in ("hi", "lo")]
        o_sum = sb("o_sum", [P, 2 * H1, DH1])
        rsum = sb("rsum", [P, 2 * H1])
        sc_ps = [ps(f"sc{i}", [P, 2, 512]) for i in range(2)]
        t_ps = [ps(f"t{i}", [P, HG, P]) for i in range(2)]
        o_ps = ps("o", [P, 2, H1, VW])
        f_ps = ps("f", [P, 512])

        def f_bank(b, n):
            return sc_ps[n // 2][:, n % 2, :] if isinstance(b, int) and b == 0 else f_ps[:]

        ln_sems = [sem(n) for n in ("stat", "aggr", "eps_added", "rstd_done")]
        vector_ln, pool_ln = row_statistics(nc, mem, ln_sems, False)
        (ctx_in, ones_set, is_seen, xn_full, xn_hi, xn_lo,
         ctx_hi, ctx_lo, q_mm, k_mm, v_mm, q_out, q_hi, q_lo, k_out, k_hi, k_lo, own_a, own_b,
         v_out, v1, v2, v3, rest, s_mm, top_done, s_sub, p_exp, t_mm, t_hi, t_lo, o_mm, o_added, o_inv, o_done) = [
            sem(n) for n in (
                "ctx_in ones_set is_seen xn_full xn_hi xn_lo "
                "ctx_hi ctx_lo q_mm k_mm v_mm q_out q_hi q_lo k_out k_hi k_lo own_a own_b "
                "v_out v1 v2 v3 rest s_mm top_done s_sub p_exp t_mm t_hi t_lo o_mm o_added o_inv o_done").split()]
        block = ctx.enter_context(nc.Block())

        def among(b, firsts):
            return isinstance(b, int) and b < firsts

        def exists(b):
            return not (isinstance(b, int) and b >= B)

        def batches(eng, turn):
            def pair(b):
                for u in range(2):
                    for p in range(NP):
                        turn(b + u, u, p)
            pair(0)
            with eng.Fori(1, B // 2 - 1) as i:
                pair(i * 2)
            pair(B - 2)

        def after(b, p):
            return (b, p + 1) if p + 1 < NP else (b + 1, 0)

        @block.sync
        def _(sp):
            sp.dma_start(ctx_raw[:], io["ctx"][0]).then_inc(ctx_in, 16)
            with sp.Fori(0, B - 1) as b:
                sp.wait_ge(ctx_lo, b + 1)
                sp.dma_start(ctx_raw[:].unsqueeze(1), io["ctx"].rearrange("b d s -> d b s")[:, bass.ds(b + 1, 1), :]).then_inc(ctx_in, 16)

        @block.gpsimd
        def _(pool):
            pool_ln(pool)
            nc.gpsimd.memset(vT[:], 1.0).then_inc(ones_set, 1)

            def rows_lo(b):
                pool.wait_ge(xn_hi, b + 1)
                nc.gpsimd.tensor_tensor(xn_s[1][:], xn[:, 0, :], raw(xn_s[0][:]), ALU.subtract).then_inc(xn_lo, 1)

            def context_lo(b):
                pool.wait_ge(ctx_hi, b + 1)
                nc.gpsimd.tensor_tensor(ctx_s[1][:], ctx_raw[:], raw(ctx_s[0][:]), ALU.subtract).then_inc(ctx_lo, 1)

            def queries_lo(b, u):
                pool.wait_ge(q_hi, b * 2 + 2)
                pool.wait_ge(ctx_lo, b + 1)
                nc.gpsimd.tensor_tensor(q_s[u][64:96], q_full[64:96], raw(q_s[u][64:96]), ALU.subtract).then_inc(q_lo, 1)

            def place(b, u):
                pool.wait_ge(q_lo, b + 1)
                pool.wait_ge(k_lo, b + 1)
                if not among(b, 2):
                    pool.wait_ge(s_mm, (b - 1) * NP)
                for g in range(2):
                    for h in (2, 3):
                        last = nc.gpsimd.tensor_tensor(k_own[u][:, g, :, h, :], raw(k_s[:, g, :]).rearrange("p (a j) -> p a j", a=NP),
                                                       own[:, h:h + 1].unsqueeze(2).to_broadcast([P, NP, P]), ALU.mult)
                last.then_inc(own_b, 1)

            def values_rest(b, u, n):
                pool.wait_ge((v1, v2)[n], b + 1)
                nc.gpsimd.tensor_tensor(v_rest[:], (v_full, v_rest)[n][:], vT[:, u, :, :, n * DH1:(n + 1) * DH1], ALU.subtract).then_inc(rest, 1)

            rows_lo(0)
            context_lo(0)
            queries_lo(0, 0)
            place(0, 0)
            values_rest(0, 0, 0)
            values_rest(0, 0, 1)
            rows_lo(1)
            context_lo(1)

            def turn(b, u, p):
                if exists(b + 1):
                    if p == 1:
                        queries_lo(b + 1, 1 - u)
                    elif p == 2:
                        place(b + 1, 1 - u)
                        if exists(b + 2):
                            rows_lo(b + 2)
                    elif p == 3:
                        values_rest(b + 1, 1 - u, 0)
                        values_rest(b + 1, 1 - u, 1)
                if exists(b + 2) and p == 3:
                    context_lo(b + 2)
            batches(pool, turn)

        @block.scalar
        def _(act):
            def rows_hi(b):
                act.wait_ge(xn_full, b + 1)
                if not among(b, 1):
                    act.wait_ge(k_mm, b * 2)
                nc.scalar.activation(xn_s[0][:], xn[:, 0, :], ACT.Copy).then_inc(xn_hi, 1)

            def context_hi(b):
                act.wait_ge(ctx_in, b * 16 + 16)
                if not among(b, 1):
                    act.wait_ge(v_mm, b)
                nc.scalar.activation(ctx_s[0][:], ctx_raw[:], ACT.Copy).then_inc(ctx_hi, 1)

            def queries(b, u, g):
                act.wait_ge(q_mm, b * 2 + (g + 1))
                if not among(b, 1):
                    act.wait_ge(q_lo, b)
                if not among(b, 2):
                    act.wait_ge(s_mm, (b - 1) * NP)
                nc.scalar.activation(q_full[:, g, :], f_bank(b, g), ACT.Identity, bias=bias[:, g:g + 1]).then_inc(q_out, 1)
                nc.scalar.activation(q_s[u][:, g, :], f_bank(b, g), ACT.Identity, bias=bias[:, g:g + 1]).then_inc(q_hi, 1)

            def keys_hi(b):
                act.wait_ge(k_out, b * 2 + 2)
                if not among(b, 1):
                    act.wait_ge(own_a, b)
                    act.wait_ge(own_b, b)
                nc.scalar.activation(k_s[:], k_full[:], ACT.Identity, bias=bias[:, 4:5]).then_inc(k_hi, 1)

            def place(b, u):
                act.wait_ge(k_lo, b + 1)
                if not among(b, 2):
                    act.wait_ge(s_mm, (b - 1) * NP)
                for g in range(2):
                    for h in (0, 1):
                        last = nc.scalar.activation(k_own[u][:, g, :, h, :], raw(k_s[:, g, :]).rearrange("p (a j) -> p a j", a=NP),
                                                    ACT.Copy, scale=own[:, h:h + 1])
                last.then_inc(own_a, 1)

            def values(b, u, n):
                if n == 0:
                    act.wait_ge(v_out, b + 1)
                    if not among(b, 2):
                        act.wait_ge(o_mm, (b - 1) * NP)
                else:
                    act.wait_ge(rest, b * 2 + n)
                nc.scalar.activation(vT[:, u, :, :, n * DH1:(n + 1) * DH1], (v_full if n == 0 else v_rest)[:], ACT.Copy).then_inc((v1, v2, v3)[n], 1)

            def exp(b, p):
                act.wait_ge(s_sub, b * NP + (p + 1))
                nc.scalar.activation(prob[:, p % 2], prob[:, p % 2], ACT.Exp, scale=DH1 ** -0.5).then_inc(p_exp, 1)

            def turned_hi(b, p):
                for n in range(2):
                    act.wait_ge(t_mm, b * (2 * NP) + (2 * p + n + 1))
                    if n == 0 and not (among(b, 1) and p < 2):
                        act.wait_ge(o_mm, b * NP + (p - 1))
                    nc.scalar.activation(pT[0][:, p % 2, n * HG:(n + 1) * HG], t_ps[n][:], ACT.Copy).then_inc(t_hi, 1)

            rows_hi(0)
            context_hi(0)
            queries(0, 0, 0)
            queries(0, 0, 1)
            keys_hi(0)
            place(0, 0)
            for n in range(3):
                values(0, 0, n)
            rows_hi(1)
            context_hi(1)
            exp(0, 0)

            def turn(b, u, p):
                if p == 0 and exists(b + 1):
                    queries(b + 1, 1 - u, 0)
                if p == 3 and exists(b + 1):
                    values(b + 1, 1 - u, 0)
                if p == 2 and exists(b + 1):
                    place(b + 1, 1 - u)
                turned_hi(b, p)
                if exists(after(b, p)[0]):
                    exp(*after(b, p))
                if p == 1 and exists(b + 1):
                    keys_hi(b + 1)
                if p == 0 and exists(b + 1):
                    queries(b + 1, 1 - u, 1)
                if p == 2 and exists(b + 2):
                    rows_hi(b + 2)
                if p == 3 and exists(b + 1):
                    values(b + 1, 1 - u, 1)
                if p == 3 and exists(b + 2):
                    context_hi(b + 2)
                if p == 3 and exists(b + 1):
                    values(b + 1, 1 - u, 2)
            batches(act, turn)

        @block.vector
        def _(dve):
            vector_ln(dve)
            dve.wait_ge(ln_sems[3], 1)

            def rows(b):
                if not among(b, 1):
                    dve.wait_ge(k_out, b * 2)
                    dve.wait_ge(xn_lo, b)
                nc.vector.tensor_scalar(seen[:], mem["seen_all"][:, bass.ds(b, 1), :], 0.0, None, ALU.is_gt).then_inc(is_seen, 1)
                nc.vector.tensor_scalar(xn[:], mem["x_acc"][:, bass.ds(b, 1), :], mem["mv"][:].rearrange("p b s -> p (b s)")[:, bass.ds(b * 2, 1)],
                                        mem["rstd"][:, bass.ds(b, 1)], ALU.subtract, ALU.mult).then_inc(xn_full, 1)

            def keys(b, g):
                dve.wait_ge(k_mm, b * 2 + (g + 1))
                if g == 0:
                    dve.wait_ge(is_seen, b + 1)
                    if not among(b, 1):
                        dve.wait_ge(k_lo, b)
                nc.vector.scalar_tensor_tensor(k_full[:, g, :], f_bank(b, 2 + g), bias[:, 2 + g:3 + g], seen[:, 0, :], ALU.add, ALU.mult).then_inc(k_out, 1)

            def keys_lo(b):
                dve.wait_ge(k_hi, b + 1)
                nc.vector.tensor_tensor(k_s[32:64], k_full[32:64], raw(k_s[32:64]), ALU.subtract).then_inc(k_lo, 1)

            def values(b):
                dve.wait_ge(v_mm, b + 1)
                if not among(b, 1):
                    dve.wait_ge(v3, b)
                nc.vector.tensor_tensor(v_full[:], f_ps[:, 0:NP * E1].rearrange("p (a h c) -> p a h c", a=NP, h=H1),
                                        bv[:].rearrange("p (h c) -> p h c", h=H1).unsqueeze(1).to_broadcast([P, NP, H1, DH1]), ALU.add).then_inc(v_out, 1)

            def centre(b, p):
                dve.wait_ge(s_mm, b * NP + (p + 1))
                scores = sc_ps[p % 2][:].rearrange("p g (h j) -> p (g h) j", h=HG)
                early = among(b, 1) and p < 2
                if not early:
                    dve.wait_ge(s_sub, b * NP + (p - 1))
                nc.vector.tensor_reduce(top[:, p % 2, :], scores, AX.X, ALU.max).then_inc(top_done, 1)
                dve.wait_ge(top_done, b * NP + (p + 1))
                if not early:
                    dve.wait_ge(t_mm, b * (2 * NP) + (2 * p - 2))
                nc.vector.tensor_tensor(prob[:, p % 2], scores, top[:, p % 2, :].unsqueeze(2).to_broadcast([P, H1, P]),
                                        ALU.subtract).then_inc(s_sub, 1)

            def turned_lo(b, p):
                for n in range(2):
                    dve.wait_ge(t_hi, b * (2 * NP) + (2 * p + n + 1))
                    nc.vector.tensor_tensor(pT[1][:, p % 2, n * HG:(n + 1) * HG], t_ps[n][:], pT[0][:, p % 2, n * HG:(n + 1) * HG],
                                            ALU.subtract).then_inc(t_lo, 1)

            def outputs(b, n):
                dve.wait_ge(o_mm, b * NP + (2 * n + 2))
                if not (among(b, 1) and n == 0):
                    dve.wait_ge(o_done, b * 2 + n)
                outs = o_ps[:].rearrange("p a h c -> p (a h) c")
                nc.vector.tensor_reduce(o_sum[:], outs[:, :, 0:PICKED * DH1].rearrange("p n (t c) -> p n c t", t=PICKED),
                                        AX.X, ALU.add).then_inc(o_added, 1)
                nc.vector.reciprocal(rsum[:], outs[:, :, PICKED * DH1]).then_inc(o_inv, 1)
                dve.wait_ge(o_added, b * 2 + (n + 1))
                dve.wait_ge(o_inv, b * 2 + (n + 1))
                nc.vector.tensor_tensor(mem["o_all"][:, bass.ds(b * (NP * H1) + n * (2 * H1), 2 * H1), :], o_sum[:],
                                        rsum[:].unsqueeze(2).to_broadcast([P, 2 * H1, DH1]), ALU.mult).then_inc(o_done, 1)

            rows(0)
            keys(0, 0)
            keys(0, 1)
            rows(1)
            keys_lo(0)
            values(0)
            centre(0, 0)

            def turn(b, u, p):
                if p == 3 and exists(b + 1):
                    values(b + 1)
                if p == 2 and exists(b + 1):
                    keys_lo(b + 1)
                if exists(after(b, p)[0]):
                    centre(*after(b, p))
                if p == 1 and exists(b + 1):
                    keys(b + 1, 0)
                turned_lo(b, p)
                if p == 1 and exists(b + 1):
                    keys(b + 1, 1)
                if p == 1 and exists(b + 2):
                    rows(b + 2)
                if p == 0:
                    if not among(b, 1):
                        outputs(b - 1, 1)
                if p == 2:
                    outputs(b, 0)
            batches(dve, turn)
            outputs(B - 1, 1)

        @block.tensor
        def _(pe):
            pe.wait_ge(ones_set, 1)

            def project(b, n):
                if n == 0:
                    pe.wait_ge(xn_lo, b + 1)
                    if not among(b, 1):
                        pe.wait_ge(v_out, b)
                elif among(b, 1):
                    pass
                elif n < 3:
                    pe.wait_ge(q_hi, b * 2 + n)
                else:
                    pe.wait_ge(k_out, b * 2 + 1)
                for m, (a, c) in enumerate(split_passes(qk_s[0], qk_s[1], xn_s[0], xn_s[1])):
                    last = nc.tensor.matmul(f_bank(b, n), a[:, n, :], c[:], start=(m == 0), stop=(m == 2))
                last.then_inc(q_mm if n < 2 else k_mm, 1)

            def values(b):
                pe.wait_ge(ctx_lo, b + 1)
                if not among(b, 1):
                    pe.wait_ge(k_out, b * 2 + 2)
                for p in range(NP):
                    for m, (a, c) in enumerate(split_passes(ctx_s[0], ctx_s[1], wv_s[0], wv_s[1])):
                        last = nc.tensor.matmul(f_ps[:, p * E1:(p + 1) * E1], a[:, p * P:(p + 1) * P], c[:], start=(m == 0), stop=(m == 2))
                last.then_inc(v_mm, 1)

            def scores(b, u, p):
                if p == 0:
                    pe.wait_ge(q_lo, b + 1)
                    pe.wait_ge(own_a, b + 1)
                    pe.wait_ge(own_b, b + 1)
                if not (among(b, 1) and p < 2):
                    pe.wait_ge(s_sub, b * NP + (p - 1))
                for g in range(2):
                    last = nc.tensor.matmul(sc_ps[p % 2][:, g, :], q_s[u][:, g, p * P:(p + 1) * P], k_own[u][:, g, p],
                                            start=True, stop=True)
                last.then_inc(s_mm, 1)

            def turned(b, p):
                for n in range(2):
                    if n == 0:
                        pe.wait_ge(p_exp, b * NP + (p + 1))
                    if not (among(b, 1) and p == 0):
                        pe.wait_ge(t_lo, b * (2 * NP) + (2 * p + n - 1))
                    for h in range(HG):
                        last = nc.tensor.transpose(t_ps[n][:, h, :], prob[:, p % 2, n * HG + h, :], mem["ident"][:])
                    last.then_inc(t_mm, 1)

            def outputs(b, u, p):
                pe.wait_ge(t_lo, b * (2 * NP) + (2 * p + 2))
                if p == 0:
                    pe.wait_ge(v3, b + 1)
                if p % 2 == 0 and not (among(b, 1) and p == 0):
                    pe.wait_ge(o_done, b * 2 + p // 2)
                for h in range(H1):
                    for n in range(2):
                        last = nc.tensor.matmul(o_ps[:, p % 2, h, 0:PICKED * DH1 + 1], pT[n][:, p % 2, h, :],
                                                vT[:, u, p, h, 0:PICKED * DH1 + 1], start=(n == 0), stop=(n == 1))
                last.then_inc(o_mm, 1)

            for n in range(4):
                project(0, n)
            values(0)
            scores(0, 0, 0)

            def turn(b, u, p):
                follows = after(b, p)
                if exists(follows[0]):
                    scores(follows[0], u if p + 1 < NP else 1 - u, follows[1])
                if exists(b + 1) and p < 2:
                    project(b + 1, 2 * p)
                turned(b, p)
                if exists(b + 1) and p < 2:
                    project(b + 1, 2 * p + 1)
                if p > 0:
                    outputs(b, u, p - 1)
                elif not among(b, 1):
                    outputs(b - 1, 1 - u, NP - 1)
                if exists(b + 1) and p == 2:
                    values(b + 1)
            batches(pe, turn)
            outputs(B - 1, 1, NP - 1)


def layer1_rest(nc, io, mem, out):
    NE = 2
    with ExitStack() as ctx:
        sb = lambda name, shape, dt=F32: ctx.enter_context(nc.sbuf_tensor(f"rest_{name}", shape, dt))
        ps = lambda name: ctx.enter_context(nc.psum_tensor(f"rest_{name}", [P, 512], F32))
        sem = stage_semaphores(nc, ctx, "rest_")
        wo_raw = sb("wo_raw", [E1, P])
        wo_s = [sb(f"wo_{n}", [E1, P], F32R) for n in ("hi", "lo")]
        bo = sb("bo", [P, 1])
        gelu = sb("gelu", [E1, 2, D])
        gelu_s = [sb(f"gelu_{n}", [E1, 2, D], F32R) for n in ("hi", "lo")]
        masked = sb("masked", [P, 2, D])
        a_raw = sb("a_raw", [P, NE, D])
        a_s = [sb(f"a_{n}", [P, NE, D], F32R) for n in ("hi", "lo")]
        b_raw = sb("b_raw", [P, NE, D])
        b_s = [sb(f"b_{n}", [P, NE, D], F32R) for n in ("hi", "lo")]
        cs = sb("cs", [P, 2, NE])
        w_exp = sb("w_exp", [P, NE])
        w1 = sb("w1", [P, KT, D])
        w1_s = [sb(f"w1_{n}", [P, KT, D], F32R) for n in ("hi", "lo")]
        bias = sb("bias", [P, D])
        xn = sb("xn", [P, B, D])
        xnT = [sb(f"xnT_{n}", [P, KT, B * S], F32R) for n in ("hi", "lo")]
        o_t_ps = [ps("o_t0"), ps("o_t1")]
        y_ps = [ps("y0"), ps("y1")]
        tr_ps = [ps("tr0"), ps("tr1")]
        m_ps = [ps("m0"), ps("m1")]
        z_ps = y_ps + m_ps + o_t_ps
        ln_sems = [sem(n) for n in ("stat", "aggr", "eps_added", "rstd_done")]
        vector_ln, pool_ln, scalar_ln, tensor_ln, xn_done, xn_lo = normalised_columns(nc, mem, xn, xnT, tr_ps, sem, ln_sems, True)
        (wo_in, lora_in, w_in, bias_in, wo_hi, wo_lo, a_hi, a_lo, w_set, b_set, b_hi, b_lo, m_mm, w_add, w_hi, w_lo,
         o_t, g_done, g_hi, g_lo, p_mm, p_mask, x_done, z_mm, z_add, z_bias, stored) = [sem(n) for n in (
            "wo_in lora_in w_in bias_in wo_hi wo_lo a_hi a_lo w_set b_set b_hi b_lo m_mm w_add w_hi w_lo "
            "o_t g_done g_hi g_lo p_mm p_mask x_done z_mm z_add z_bias stored").split()]
        block = ctx.enter_context(nc.Block())

        @block.sync
        def _(sp):
            sp.dma_start(wo_raw[:], io["wo1_t"]).then_inc(wo_in, 16)
            sp.dma_start(bo[:], io["bo1"].rearrange("(p o) -> p o", o=1)).then_inc(wo_in, 16)
            sp.dma_start(a_raw[:], io["lora_a"].rearrange("(t p) d -> p t d", p=P)).then_inc(lora_in, 16)
            sp.dma_start(b_raw[:], io["lora_b"].rearrange("(t p) d -> p t d", p=P)).then_inc(lora_in, 16)
            sp.dma_start(cs[:], io["lora_cs"]).then_inc(lora_in, 16)
            sp.dma_start(w1[:], io["w1_t"].rearrange("(k p) n -> p k n", p=P)).then_inc(w_in, 16)
            sp.dma_start(bias[:], io["bias1"].rearrange("(o n) -> o n", o=1).to_broadcast([P, D])).then_inc(bias_in, 16)
            for b in range(B):
                sp.wait_ge(z_add, b + 1)
                sp.dma_start(out[b], mem["x_acc"][:, b, :]).then_inc(stored, 16)
            sp.wait_ge(stored, 16 * B)

        @block.gpsimd
        def _(pool):
            for b in range(B):
                pool.wait_ge(p_mask, b + 1)
                nc.gpsimd.tensor_tensor(mem["x_acc"][:, b, :], mem["x_acc"][:, b, :], masked[:, b % 2, :], ALU.add).then_inc(x_done, 1)
            pool_ln(pool)
            pool.wait_ge(bias_in, 16)
            for b in range(B):
                pool.wait_ge(xn_done, b + 1)
                nc.gpsimd.tensor_tensor(mem["x_acc"][:, b, :], mem["x_acc"][:, b, :], bias[:], ALU.add).then_inc(z_bias, 1)

        @block.scalar
        def _(act):
            act.wait_ge(wo_in, 32)
            nc.scalar.activation(wo_s[0][:], wo_raw[:], ACT.Copy).then_inc(wo_hi, 1)

            def project(b):
                act.wait_ge(o_t, b + 1)
                if b >= 2:
                    act.wait_ge(g_lo, b - 1)
                nc.scalar.activation(gelu[:, b % 2, :], o_t_ps[b % 2][0:E1, :], ACT.Gelu).then_inc(g_done, 1)
                act.wait_ge(g_done, b + 1)
                if b >= 2:
                    act.wait_ge(p_mm, b - 1)
                nc.scalar.activation(gelu_s[0][:, b % 2, :], gelu[:, b % 2, :], ACT.Copy).then_inc(g_hi, 1)
            def merged_hi(k):
                act.wait_ge(w_add, k + 1)
                nc.scalar.activation(w1_s[0][:, k, :], w1[:, k, :], ACT.Copy).then_inc(w_hi, 1)

            for b in range(B):
                project(b)
                if b == 1:
                    act.wait_ge(lora_in, 48)
                    nc.scalar.activation(a_s[0][:], a_raw[:], ACT.Copy).then_inc(a_hi, 1)
                    act.wait_ge(b_set, NE)
                    nc.scalar.activation(b_s[0][:], b_raw[:], ACT.Copy).then_inc(b_hi, 1)
                if b >= 5:
                    merged_hi(b - 5)
            merged_hi(KT - 1)
            scalar_ln(act)

        @block.vector
        def _(dve):
            dve.wait_ge(wo_hi, 1)
            nc.vector.tensor_tensor(wo_s[1][:], wo_raw[:], raw(wo_s[0][:]), ALU.subtract).then_inc(wo_lo, 1)

            def factors():
                dve.wait_ge(lora_in, 48)
                nc.vector.tensor_tensor(w_exp[:], cs[:, 0, :], cs[:, 1, :], ALU.mult).then_inc(w_set, 1)
                dve.wait_ge(w_set, 1)
                for t in range(NE):
                    nc.vector.tensor_scalar(b_raw[:, t, :], b_raw[:, t, :], w_exp[:, t:t + 1], None, ALU.mult).then_inc(b_set, 1)
                dve.wait_ge(a_hi, 1)
                nc.vector.tensor_tensor(a_s[1][:], a_raw[:], raw(a_s[0][:]), ALU.subtract).then_inc(a_lo, 1)
                dve.wait_ge(b_hi, 1)
                nc.vector.tensor_tensor(b_s[1][:], b_raw[:], raw(b_s[0][:]), ALU.subtract).then_inc(b_lo, 1)
                dve.wait_ge(w_in, 16)

            def merge(k):
                dve.wait_ge(m_mm, k + 1)
                nc.vector.tensor_tensor(w1[:, k, :], w1[:, k, :], m_ps[k % 2][:], ALU.add).then_inc(w_add, 1)

            def lo(b):
                dve.wait_ge(g_hi, b + 1)
                nc.vector.tensor_tensor(gelu_s[1][:, b % 2, :], gelu[:, b % 2, :], raw(gelu_s[0][:, b % 2, :]), ALU.subtract).then_inc(g_lo, 1)

            def add(b):
                dve.wait_ge(p_mm, b + 1)
                if b >= 2:
                    dve.wait_ge(x_done, b - 1)
                nc.vector.scalar_tensor_tensor(masked[:, b % 2, :], y_ps[b % 2][:], bo[:, 0:1], mem["seen_all"][:, b, :], ALU.add, ALU.mult).then_inc(p_mask, 1)
                if b >= 2:
                    take_statistics(nc, mem, slice(b - 2, b - 1)).then_inc(ln_sems[0], 1)
            lo(0)
            lo(1)
            factors()
            for b in range(2, B):
                lo(b)
                add(b - 2)
                if b >= B - KT:
                    merge(b - (B - KT))
            add(B - 2)
            add(B - 1)

            def merged_lo():
                for k in range(KT):
                    dve.wait_ge(w_hi, k + 1)
                    nc.vector.tensor_tensor(w1_s[1][:, k, :], w1[:, k, :], raw(w1_s[0][:, k, :]), ALU.subtract).then_inc(w_lo, 1)
            for b in (B - 2, B - 1):
                dve.wait_ge(x_done, b + 1)
                take_statistics(nc, mem, slice(b, b + 1)).then_inc(ln_sems[0], 1)
            vector_ln(dve, meanwhile=merged_lo)
            for b in range(B):
                dve.wait_ge(z_bias, b + 1)
                dve.wait_ge(z_mm, b + 1)
                nc.vector.tensor_tensor(mem["x_acc"][:, b, :], mem["x_acc"][:, b, :], z_ps[b % len(z_ps)][:], ALU.add).then_inc(z_add, 1)

        @block.tensor
        def _(pe):
            def turn(b):
                if b >= 2:
                    pe.wait_ge(g_done, b - 1)
                for p in range(NP):
                    last = nc.tensor.transpose(o_t_ps[b % 2][0:E1, p * P:(p + 1) * P],
                                               mem["o_all"][:, (b * NP + p) * H1:(b * NP + p + 1) * H1, :].rearrange("p h c -> p (h c)"),
                                               mem["ident"][:])
                last.then_inc(o_t, 1)

            def project(b):
                pe.wait_ge(g_lo, b + 1)
                if b >= 2:
                    pe.wait_ge(p_mask, b - 1)
                for m, (a, c) in enumerate(split_passes(wo_s[0], wo_s[1], gelu_s[0], gelu_s[1])):
                    last = nc.tensor.matmul(y_ps[b % 2][:], a[:], c[:, b % 2, :], start=(m == 0), stop=(m == 2))
                last.then_inc(p_mm, 1)

            turn(0)
            turn(1)

            def merge(k):
                if k == 0:
                    pe.wait_ge(a_lo, 1)
                    pe.wait_ge(b_lo, 1)
                if k >= 2:
                    pe.wait_ge(w_add, k - 1)
                n = 0
                for t in range(NE):
                    for a, c in split_passes(a_s[0], a_s[1], b_s[0], b_s[1]):
                        last = nc.tensor.matmul(m_ps[k % 2][:], a[:, t, k * P:(k + 1) * P], c[:, t, :], start=(n == 0), stop=(n == 3 * NE - 1))
                        n += 1
                last.then_inc(m_mm, 1)

            pe.wait_ge(wo_lo, 1)
            for b in range(B):
                project(b)
                if b + 2 < B:
                    turn(b + 2)
                if 2 <= b < 2 + KT:
                    merge(b - 2)

            pe.wait_ge(p_mask, B)
            pe.wait_ge(w_add, KT)
            pe.wait_ge(g_done, B)

            def linear(b):
                if b == 0:
                    pe.wait_ge(w_lo, KT)
                pe.wait_ge(xn_lo, b + 1)
                if b >= len(z_ps):
                    pe.wait_ge(z_add, b + 1 - len(z_ps))
                n = 0
                for k in range(KT):
                    for a, c in split_passes(xnT[0], xnT[1], w1_s[0], w1_s[1]):
                        last = nc.tensor.matmul(z_ps[b % len(z_ps)][:], a[:, k, b * S:(b + 1) * S], c[:, k, :], start=(n == 0), stop=(n == 3 * KT - 1))
                        n += 1
                last.then_inc(z_mm, 1)

            tensor_ln(pe, lambda b: linear(b - 2) if b >= 2 else None)
            linear(B - 2)
            linear(B - 1)


def build(nc, io, out):
    with ExitStack() as ctx:
        sb = lambda name, shape, dt=F32: ctx.enter_context(nc.sbuf_tensor(name, shape, dt))
        mem = {
            "x_acc": sb("x_acc", [P, B, D]),
            "cos_k": sb("cos_k", [P, S]), "sin_k": sb("sin_k", [P, S]),
            "cos_q": sb("cos_q", [P, S]), "sin_q": sb("sin_q", [P, S]),
            "mask_bias": sb("mask_bias", [P, S]), "ident": sb("ident", [P, P]),
            "minus_half": sb("minus_half", [P, B]), "pick": sb("pick", [P, HB, P], F32R),
            "row": sb("row", [P, HB, P], F32R),
            "stats": sb("stats", [P, B, 6]), "mv": sb("mv", [P, B, 2]), "rstd": sb("rstd", [P, B]),
        }
        with ExitStack() as attention:
            mem["v_all"] = attention.enter_context(nc.sbuf_tensor("v_all", [P, HB, NKV * DH], F32))
            prepare(nc, io, mem)
            layer0_attention(nc, io, mem)
        mem["seen_all"] = sb("seen_all", [P, B, D])
        mem["qk_s"] = [sb(f"qk_{n}", [P, 4, P], F32R) for n in ("hi", "lo")]
        mem["wv_s"] = [sb(f"wv_{n}", [P, E1], F32R) for n in ("hi", "lo")]
        mem["qk_bias"], mem["bv"], mem["own"] = sb("qk_bias", [P, 5]), sb("bv", [P, E1]), sb("own", [P, HG])
        layer0_ffn(nc, io, mem)
        mem["o_all"] = sb("o_all", [P, B * NP * H1, DH1])
        layer1_attention(nc, io, mem)
        layer1_rest(nc, io, mem, out)


def score_rows():
    import numpy as np
    own = np.zeros((P, HG), np.float32)
    for part in range(3):
        for h in range(HG):
            own[part * 32 + h * DH1:part * 32 + (h + 1) * DH1, h] = 1.0
    own[96, :] = 1.0
    return own


def rotary_tables():
    import numpy as np
    inv = (1.0 / (np.float32(10000.0) ** (np.arange(0, DH, 2, dtype=np.float32) / np.float32(DH)))).astype(np.float32)
    phase = (np.arange(S, dtype=np.float32)[:, None] * inv[None, :]).astype(np.float32)
    c, s = np.cos(phase).astype(np.float32).T, np.sin(phase).astype(np.float32).T
    return np.ascontiguousarray(np.concatenate([c, c])), np.ascontiguousarray(np.concatenate([-s, s]))


def kernel(**inputs):
    import numpy as np
    import concourse.bacc as bacc
    from concourse.bass_utils import run_bass_kernel_spmd as run

    nc = bacc.Bacc("TRN2", target_bir_lowering=False, num_devices=1)
    get = lambda n: np.ascontiguousarray(inputs[n])
    cos, sin = rotary_tables()
    bias = np.zeros((P, 5), np.float32)
    for n, name in enumerate(("L1_xattn_bq", "L1_xattn_bk")):
        for part in range(3):
            bias[part * 32:part * 32 + 32, 2 * n:2 * n + 2] = get(name).reshape(2, 32).T
    bias[96, 0:2] = 1.0
    bias[96, 2:4] = NO_KEY
    bias[96, 4] = -NO_KEY
    arrays = {
        "x": get("x"),
        "ctx_t": np.ascontiguousarray(get("ctx_4096").reshape(B * S, D).T),
        "mask_t": np.ascontiguousarray(get("mask_1x1xSxS2_bk0").reshape(S, S).T),
        "cos": cos, "sin": sin,
        "gate_t": np.ascontiguousarray(get("L0_ffn_gate_t").T), "up_t": np.ascontiguousarray(get("L0_ffn_up_t").T),
        "down_t": np.ascontiguousarray(get("L0_ffn_down_t").T),
        "gu_s": np.ascontiguousarray(np.stack([get("L0_ffn_gate_s").reshape(NG, FG, P), get("L0_ffn_up_s").reshape(NG, FG, P)], 1)
                                     .reshape(NG * 2 * FG, P).T),
        "down_s": get("L0_ffn_down_s"),
        "ctx": get("ctx_4096"), "key_mask": get("mask_Bx1x4096_ff1"),
        "qk1_t": np.ascontiguousarray(np.stack([get("L1_xattn_Wq").T, get("L1_xattn_Wk").T], 1)),
        "wv1_t": np.ascontiguousarray(get("L1_xattn_Wv").T), "bv1": get("L1_xattn_bv"),
        "qk1_bias": np.ascontiguousarray(bias), "own": score_rows(),
        "wo1_t": np.ascontiguousarray(get("L1_xattn_Wo").T), "bo1": get("L1_xattn_bo"),
        "lora_a": get("L1_ffn_A").reshape(256, D), "lora_b": np.ascontiguousarray(get("L1_ffn_Bf").transpose(0, 2, 1)).reshape(256, D),
        "lora_cs": np.ascontiguousarray(np.stack([np.repeat(get("L1_ffn_coeffs"), 16).reshape(2, P).T,
                                                  np.repeat(get("L1_ffn_scales"), 16).reshape(2, P).T], 1)),
        "w1_t": np.ascontiguousarray(get("L1_ffn_W").T), "bias1": get("L1_ffn_bias"),
        "Wq0": get("L0_xattn_Wq"), "Wk0": get("L0_xattn_Wk"), "Wv0": get("L0_xattn_Wv"), "Wo0": get("L0_xattn_Wo"),
    }
    io = {n: nc.dram_tensor(f"in_{n}", a.shape, mybir.dt.from_np(a.dtype), kind="ExternalInput").ap()
          for n, a in arrays.items()}
    out = nc.dram_tensor("out", (B, S, D), F32, kind="ExternalOutput").ap()
    build(nc, io, out)
    r = run(nc, [{f"in_{n}": a for n, a in arrays.items()}], core_ids=[0])
    return r.results[0]["out"]
```
